# Optimizing a Trainium2 kernel written in Bass

```python
import numpy as np
import jax
import jax.numpy as jnp

def _softmax(x, axis=-1):
    return jax.nn.softmax(x, axis=axis)

def _gelu(x):
    return jax.nn.gelu(x, approximate=True)

def _silu(x):
    return jax.nn.silu(x)

def _sigmoid(x):
    return jax.nn.sigmoid(x)

def _layernorm(x, axis=-1, eps=1e-05):
    m = jnp.mean(x, axis=axis, keepdims=True)
    v = jnp.var(x, axis=axis, keepdims=True)
    return (x - m) / jnp.sqrt(v + eps)

def _scatter_add(tgt, idx, src, axis=0):
    return tgt.at[idx].add(src)

def _segment_sum(src, seg, n):
    return jax.ops.segment_sum(src, seg, n)
kernel_name = 'mk_vit_tower_d2_tok_img1024_r4_12b890'

def setup_inputs(seed: int=0):
    np.random.seed(seed)
    _w = jnp.asarray

    def _rec_inputs():
        import jax
        import jax.numpy as jnp
        _rk = jax.random.key(seed)
        x = -0.00016672 + 0.999947 * jax.random.normal(jax.random.fold_in(_rk, 1), (64, 3, 96, 96), jnp.float32)
        return x
    x = _rec_inputs()

    def _L0_tok_setup():
        import jax, jax.numpy as jnp
        import numpy as np
        PATCH = 16

        def _patchify(x, p):
            B, C, H, W = x.shape
            nh, nw = (H // p, W // p)
            x = x.reshape(B, C, nh, p, nw, p)
            x = x.transpose(0, 2, 4, 1, 3, 5)
            return x.reshape(B, nh * nw, C * p * p)
        key = jax.random.key(seed)
        k1, k2, k3, k4, k5 = jax.random.split(key, 5)
        B, C, H = (64, 3, 96)
        d_model = 256
        p = PATCH
        num_patches = (H // p) ** 2
        in_dim = p * p * C
        x = jax.random.normal(k1, (B, C, H, H), dtype=jnp.float32)
        bound = 1.0 / np.sqrt(in_dim)
        W = jax.random.uniform(k2, (d_model, in_dim), dtype=jnp.float32, minval=-bound, maxval=bound)
        b = jax.random.uniform(k3, (d_model,), dtype=jnp.float32, minval=-bound, maxval=bound)
        cls_token = jax.random.normal(k4, (1, 1, d_model), dtype=jnp.float32)
        pos_enc = jax.random.normal(k5, (1, num_patches + 1, d_model), dtype=jnp.float32)
        return {'x': x, 'W': W, 'b': b, 'cls_token': cls_token, 'pos_enc': pos_enc}
    _L0_tok_all = _L0_tok_setup()
    _L0_tok_in = {k: v for k, v in _L0_tok_all.items() if k in ('W', 'b', 'cls_token', 'pos_enc')}
    del _L0_tok_all

    def _L0_attn_setup():
        import jax, jax.numpy as jnp
        import numpy as np
        D_MODEL = 256
        NHEAD = 16
        HEAD_DIM = D_MODEL // NHEAD
        MAX_DIST = 128

        def _rel_bias(rel_emb, seq_len):
            pos = jnp.arange(seq_len)
            rel = pos[None, :] - pos[:, None]
            rel = jnp.clip(rel, -MAX_DIST, MAX_DIST) + MAX_DIST
            bias = rel_emb[rel]
            bias = jnp.transpose(bias, (2, 0, 1))
            causal_mask = jnp.triu(jnp.ones((seq_len, seq_len), dtype=bool), k=1)
            return jnp.where(causal_mask[None, :, :], -jnp.inf, bias)
        key = jax.random.key(seed)
        ks = jax.random.split(key, 6)
        B, T = (2, 512)
        x = jax.random.normal(ks[0], (B, T, D_MODEL), dtype=jnp.float32)
        Wqkv = jax.random.normal(ks[1], (D_MODEL, 3 * D_MODEL), dtype=jnp.float32) * 0.02
        bqkv = jnp.zeros((3 * D_MODEL,), dtype=jnp.float32)
        Wout = jax.random.normal(ks[2], (D_MODEL, D_MODEL), dtype=jnp.float32) * 0.02
        bout = jnp.zeros((D_MODEL,), dtype=jnp.float32)
        rel_emb = jax.random.normal(ks[3], (2 * MAX_DIST + 1, NHEAD), dtype=jnp.float32) * 0.02
        return {'x': x, 'Wqkv': Wqkv, 'bqkv': bqkv, 'Wout': Wout, 'bout': bout, 'rel_emb': rel_emb}
    _L0_attn_all = _L0_attn_setup()
    _L0_attn_in = {k: v for k, v in _L0_attn_all.items() if k in ('Wqkv', 'bqkv', 'Wout', 'bout', 'rel_emb')}
    del _L0_attn_all

    def _L0_ffn_setup():
        import jax, jax.numpy as jnp
        import numpy as np
        H, I, E_ROUTED, TOP_K = (256, 704, 7, 2)
        B, S = (4, 512)

        def _expert(h, g, u, d):
            return jnp.einsum('...i,hi->...h', jax.nn.silu(h @ g.T) * (h @ u.T), d)
        key = jax.random.key(seed)
        ks = jax.random.split(key, 10)
        sc = 0.02
        return {'x': jax.random.normal(ks[0], (B, S, H), dtype=jnp.float32), 'sg': jax.random.normal(ks[1], (I, H), dtype=jnp.float32) * sc, 'su': jax.random.normal(ks[2], (I, H), dtype=jnp.float32) * sc, 'sd': jax.random.normal(ks[3], (H, I), dtype=jnp.float32) * sc, 'rg': jax.random.normal(ks[4], (E_ROUTED, I, H), dtype=jnp.float32) * sc, 'ru': jax.random.normal(ks[5], (E_ROUTED, I, H), dtype=jnp.float32) * sc, 'rd': jax.random.normal(ks[6], (E_ROUTED, H, I), dtype=jnp.float32) * sc, 'wr': jax.random.normal(ks[7], (E_ROUTED, H), dtype=jnp.float32) * sc, 'rb': jnp.zeros((E_ROUTED,), dtype=jnp.float32)}
    _L0_ffn_all = _L0_ffn_setup()
    _L0_ffn_in = {k: v for k, v in _L0_ffn_all.items() if k in ('sg', 'su', 'sd', 'rg', 'ru', 'rd', 'wr', 'rb')}
    del _L0_ffn_all

    def _L1_attn_setup():
        import jax, jax.numpy as jnp
        import numpy as np
        EMBED_DIM = 256
        NUM_HEADS = 16
        HEAD_DIM = EMBED_DIM // NUM_HEADS
        key = jax.random.key(seed)
        ks = jax.random.split(key, 6)
        s = 1.0 / np.sqrt(EMBED_DIM)
        x = jax.random.normal(ks[0], (2, 512, EMBED_DIM), dtype=jnp.float32)
        Wq = jax.random.uniform(ks[1], (EMBED_DIM, EMBED_DIM), jnp.float32, -s, s)
        Wk = jax.random.uniform(ks[2], (EMBED_DIM, EMBED_DIM), jnp.float32, -s, s)
        Wv = jax.random.uniform(ks[3], (EMBED_DIM, EMBED_DIM), jnp.float32, -s, s)
        Wo = jax.random.uniform(ks[4], (EMBED_DIM, EMBED_DIM), jnp.float32, -s, s)
        bo = jax.random.uniform(ks[5], (EMBED_DIM,), jnp.float32, -s, s)
        return {'x': x, 'Wq': Wq, 'Wk': Wk, 'Wv': Wv, 'Wo': Wo, 'bo': bo}
    _L1_attn_all = _L1_attn_setup()
    _L1_attn_in = {k: v for k, v in _L1_attn_all.items() if k in ('Wq', 'Wk', 'Wv', 'Wo', 'bo')}
    del _L1_attn_all

    def _L1_ffn_setup():
        import jax, jax.numpy as jnp
        import numpy as np
        DIM = 256
        HIDDEN = 768
        SCALE = 1.0 / 127.0

        def _dequant(w_int, dtype):
            return w_int.astype(dtype) * jnp.asarray(SCALE, dtype)
        key = jax.random.key(seed)
        k_x, k_g, k_u, k_d = jax.random.split(key, 4)
        x = jax.random.normal(k_x, (4, 512, DIM), dtype=jnp.float32)
        w_gate = jax.random.randint(k_g, (HIDDEN, DIM), -127, 128, dtype=jnp.int32)
        w_up = jax.random.randint(k_u, (HIDDEN, DIM), -127, 128, dtype=jnp.int32)
        w_down = jax.random.randint(k_d, (DIM, HIDDEN), -127, 128, dtype=jnp.int32)
        return {'x': x, 'w_gate': w_gate, 'w_up': w_up, 'w_down': w_down}
    _L1_ffn_all = _L1_ffn_setup()
    _L1_ffn_in = {k: v for k, v in _L1_ffn_all.items() if k in ('w_gate', 'w_up', 'w_down')}
    del _L1_ffn_all
    return {'x': x, 'L0_tok_W': _L0_tok_in['W'], 'L0_tok_b': _L0_tok_in['b'], 'L0_tok_cls_token': _L0_tok_in['cls_token'], 'L0_tok_pos_enc': _L0_tok_in['pos_enc'], 'L0_attn_Wqkv': _L0_attn_in['Wqkv'], 'L0_attn_bqkv': _L0_attn_in['bqkv'], 'L0_attn_Wout': _L0_attn_in['Wout'], 'L0_attn_bout': _L0_attn_in['bout'], 'L0_attn_rel_emb': _L0_attn_in['rel_emb'], 'L0_ffn_sg': _L0_ffn_in['sg'], 'L0_ffn_su': _L0_ffn_in['su'], 'L0_ffn_sd': _L0_ffn_in['sd'], 'L0_ffn_rg': _L0_ffn_in['rg'], 'L0_ffn_ru': _L0_ffn_in['ru'], 'L0_ffn_rd': _L0_ffn_in['rd'], 'L0_ffn_wr': _L0_ffn_in['wr'], 'L0_ffn_rb': _L0_ffn_in['rb'], 'L1_attn_Wq': _L1_attn_in['Wq'], 'L1_attn_Wk': _L1_attn_in['Wk'], 'L1_attn_Wv': _L1_attn_in['Wv'], 'L1_attn_Wo': _L1_attn_in['Wo'], 'L1_attn_bo': _L1_attn_in['bo'], 'L1_ffn_w_gate': _L1_ffn_in['w_gate'], 'L1_ffn_w_up': _L1_ffn_in['w_up'], 'L1_ffn_w_down': _L1_ffn_in['w_down']}

def reference(x, L0_tok_W, L0_tok_b, L0_tok_cls_token, L0_tok_pos_enc, L0_attn_Wqkv, L0_attn_bqkv, L0_attn_Wout, L0_attn_bout, L0_attn_rel_emb, L0_ffn_sg, L0_ffn_su, L0_ffn_sd, L0_ffn_rg, L0_ffn_ru, L0_ffn_rd, L0_ffn_wr, L0_ffn_rb, L1_attn_Wq, L1_attn_Wk, L1_attn_Wv, L1_attn_Wo, L1_attn_bo, L1_ffn_w_gate, L1_ffn_w_up, L1_ffn_w_down):
    import jax
    import jax.numpy as jnp

    def _L0_tok_ref(x, W, b, cls_token, pos_enc):
        import jax, jax.numpy as jnp
        import numpy as np
        PATCH = 16

        def _patchify(x, p):
            B, C, H, W = x.shape
            nh, nw = (H // p, W // p)
            x = x.reshape(B, C, nh, p, nw, p)
            x = x.transpose(0, 2, 4, 1, 3, 5)
            return x.reshape(B, nh * nw, C * p * p)
        B = x.shape[0]
        patches = _patchify(x, PATCH)
        proj = jnp.einsum('bnf,df->bnd', patches, W) + b
        cls = jnp.broadcast_to(cls_token, (B, 1, cls_token.shape[-1]))
        out = jnp.concatenate([cls, proj], axis=1) + pos_enc
        return out

    def _L0_attn_ref(x, Wqkv, bqkv, Wout, bout, rel_emb):
        import jax, jax.numpy as jnp
        import numpy as np
        D_MODEL = 256
        NHEAD = 16
        HEAD_DIM = D_MODEL // NHEAD
        MAX_DIST = 128

        def _rel_bias(rel_emb, seq_len):
            pos = jnp.arange(seq_len)
            rel = pos[None, :] - pos[:, None]
            rel = jnp.clip(rel, -MAX_DIST, MAX_DIST) + MAX_DIST
            bias = rel_emb[rel]
            bias = jnp.transpose(bias, (2, 0, 1))
            causal_mask = jnp.triu(jnp.ones((seq_len, seq_len), dtype=bool), k=1)
            return jnp.where(causal_mask[None, :, :], -jnp.inf, bias)
        B, T, C = x.shape
        qkv = x @ Wqkv + bqkv
        q, k, v = jnp.split(qkv, 3, axis=-1)

        def split_heads(t):
            return jnp.transpose(t.reshape(B, T, NHEAD, HEAD_DIM), (0, 2, 1, 3))
        q, k, v = (split_heads(q), split_heads(k), split_heads(v))
        scale = jnp.sqrt(jnp.float32(HEAD_DIM))
        attn = jnp.einsum('bhtd,bhsd->bhts', q, k) / scale
        bias = _rel_bias(rel_emb, T)
        attn = attn + bias[None, :, :, :]
        attn = jax.nn.softmax(attn, axis=-1)
        out = jnp.einsum('bhts,bhsd->bhtd', attn, v)
        out = jnp.transpose(out, (0, 2, 1, 3)).reshape(B, T, C)
        return out @ Wout + bout

    def _L0_ffn_ref(x, sg, su, sd, rg, ru, rd, wr, rb):
        import jax, jax.numpy as jnp
        import numpy as np
        H, I, E_ROUTED, TOP_K = (256, 704, 7, 2)
        B, S = (4, 512)

        def _expert(h, g, u, d):
            return jnp.einsum('...i,hi->...h', jax.nn.silu(h @ g.T) * (h @ u.T), d)
        shared_out = _expert(x, sg, su, sd)
        logits = x @ wr.T + rb
        probs = jax.nn.softmax(logits, axis=-1)
        scores, idx = jax.lax.top_k(probs, TOP_K)
        scores = scores / scores.sum(axis=-1, keepdims=True)
        w = jnp.sum(scores[..., None] * jax.nn.one_hot(idx, E_ROUTED, dtype=x.dtype), axis=-2)
        out = shared_out
        for e in range(E_ROUTED):
            out = out + w[..., e:e + 1] * _expert(x, rg[e], ru[e], rd[e])
        return out

    def _L1_attn_ref(x, Wq, Wk, Wv, Wo, bo):
        import jax, jax.numpy as jnp
        import numpy as np
        EMBED_DIM = 256
        NUM_HEADS = 16
        HEAD_DIM = EMBED_DIM // NUM_HEADS
        B, T, C = x.shape
        H, D = (NUM_HEADS, HEAD_DIM)
        Q = (x @ Wq.T).reshape(B, T, H, D).transpose(0, 2, 1, 3)
        K = (x @ Wk.T).reshape(B, T, H, D).transpose(0, 2, 1, 3)
        V = (x @ Wv.T).reshape(B, T, H, D).transpose(0, 2, 1, 3)
        scores = jnp.einsum('bhqd,bhkd->bhqk', Q, K) / jnp.sqrt(jnp.float32(D))
        causal = jnp.tril(jnp.ones((T, T), dtype=bool))
        scores = jnp.where(causal, scores, -jnp.inf)
        weights = jax.nn.softmax(scores, axis=-1)
        out = jnp.einsum('bhqk,bhkd->bhqd', weights, V)
        out = out.transpose(0, 2, 1, 3).reshape(B, T, C)
        return out @ Wo.T + bo

    def _L1_ffn_ref(x, w_gate, w_up, w_down):
        import jax, jax.numpy as jnp
        import numpy as np
        DIM = 256
        HIDDEN = 768
        SCALE = 1.0 / 127.0

        def _dequant(w_int, dtype):
            return w_int.astype(dtype) * jnp.asarray(SCALE, dtype)
        wg = _dequant(w_gate, x.dtype)
        wu = _dequant(w_up, x.dtype)
        wd = _dequant(w_down, x.dtype)
        gate = jnp.einsum('bsd,hd->bsh', x, wg)
        up = jnp.einsum('bsd,hd->bsh', x, wu)
        h = jax.nn.silu(gate) * up
        return jnp.einsum('bsh,dh->bsd', h, wd)
    h = _L0_tok_ref(x, L0_tok_W, L0_tok_b, L0_tok_cls_token, L0_tok_pos_enc)
    h = h + _L0_attn_ref(_layernorm(h, axis=-1), L0_attn_Wqkv, L0_attn_bqkv, L0_attn_Wout, L0_attn_bout, L0_attn_rel_emb)
    h = h + _L0_ffn_ref(_layernorm(h, axis=-1), L0_ffn_sg, L0_ffn_su, L0_ffn_sd, L0_ffn_rg, L0_ffn_ru, L0_ffn_rd, L0_ffn_wr, L0_ffn_rb)
    h = h + _L1_attn_ref(_layernorm(h, axis=-1), L1_attn_Wq, L1_attn_Wk, L1_attn_Wv, L1_attn_Wo, L1_attn_bo)
    h = h + _L1_ffn_ref(_layernorm(h, axis=-1), L1_ffn_w_gate, L1_ffn_w_up, L1_ffn_w_down)
    return h

_drawn_inputs = setup_inputs


def setup_inputs(seed=0):
    import zlib

    import numpy as np

    out = dict(_drawn_inputs(seed))
    spreads = {'L0_attn_bqkv': (0.0, 0.1), 'L0_attn_bout': (0.0, 0.1), 'L0_ffn_rb': (0.0, 2.0)}
    factors = {'L0_attn_rel_emb': 64.0, 'L0_ffn_wr': 8.552}
    for name, (base, spread) in spreads.items():
        noise = np.random.default_rng([zlib.crc32(name.encode()), seed]).standard_normal(out[name].shape)
        drawn = base * np.exp(spread * noise) if base else spread * noise
        out[name] = jnp.asarray(drawn.astype(out[name].dtype))
    for name, factor in factors.items():
        out[name] = (out[name] * factor).astype(out[name].dtype)
    return out
```

```python
from collections import namedtuple
from contextlib import ExitStack

import concourse.bass as bass
from concourse import mybir

ALU = mybir.AluOpType
ACT = mybir.ActivationFunctionType
F32 = mybir.dt.float32
I32 = mybir.dt.int32
AX_X = mybir.AxisListType.X

P = 128
IMAGES, CHANNELS, SIDE, PATCH = 64, 3, 96, 16
T = (SIDE // PATCH) ** 2 + 1
D = 256
DK = D // P
PK = CHANNELS * PATCH * PATCH // P
EK = PK + 1
ADDED = T + 2
TOKENS = IMAGES * T
GI = 8
GROUPS = IMAGES // GI
N = GI * T
PAIRS = GI // 2
W2 = 2 * T
PITCH = 64
NPAD = (GI - 1) * T + PITCH
HEADS = 16
HD = D // HEADS
HG = P // HD
HP = HEADS // 2
EXPERTS = 7
I0, I1 = 704, 768
SCALE1 = 1.0 / 127.0
EPS = 1e-5
BIG = 3.0e38
FREE = 2


def hidden_chunks(width):
    return [min(P, width - a) for a in range(0, width, P)]


def vit_kernel(nc, xT, onehot, embW, embAdd, consts, qkv0, qkvb0, wo0, wob0, bias0, qkv1, wo1, wob1,
               gu0, dn0, rT, rb, gu1, dn1, out):
    with ExitStack() as ctx:
        def sb(name, shape, dt=F32):
            return ctx.enter_context(nc.sbuf_tensor(name, shape, dt))

        def sem(name):
            return ctx.enter_context(nc.semaphore(name))

        ps = ctx.enter_context(nc.psum_tensor("ps", [P, 8, 512], F32))

        h = sb("h", [P, DK, TOKENS])
        xn_all = sb("xn_all", [P, DK, TOKENS])
        cst = sb("cst", [P, 3 * P + HG + PAIRS * EXPERTS + EXPERTS * P])
        ident = cst[:, 0:P]
        mean_w = cst[:, P:2 * P]
        headmask = cst[:, 3 * P:3 * P + HG]
        prio = cst[:, 3 * P + HG:3 * P + HG + PAIRS * EXPERTS]
        pick = cst[0:EXPERTS, 3 * P + HG + PAIRS * EXPERTS:].rearrange("p (e m) -> p e m", e=EXPERTS)
        eps_t = sb("eps_t", [P, 1])
        zero_t = sb("zero_t", [P, 1])

        emb_w = sb("emb_w", [P, PK, D])
        emb_a = sb("emb_a", [ADDED, D])
        one_s = sb("one_s", [ADDED, N])
        x_in = xn_all[:].rearrange("p c n -> p (c n)")[:, 0:2 * PK * N].rearrange("p (b k n) -> p b k n", b=2, k=PK)

        qkv_w = [sb(f"qkv_w{l}", [P, DK, 3 * D]) for l in range(2)]
        out_w = [sb(f"out_w{l}", [P, DK, D]) for l in range(2)]
        qkv_b = sb("qkv_b", [P, 3 * DK])
        out_b = [sb(f"out_b{l}", [P, DK]) for l in range(2)]
        bias = [sb(f"bias{l}", [P, HEADS, T]) for l in range(2)]
        cen = sb("cen", [P, DK, N])
        squ = sb("squ", [P, DK, N])
        lnv = sb("lnv", [P, N])
        rsd = sb("rsd", [P, N])
        xn = [sb(f"xn{b}", [P, DK, N]) for b in range(2)]
        QT = sb("QT", [P, DK, NPAD])
        KT = sb("KT", [P, DK, N])
        VT = sb("VT", [P, DK, GI, 2, PITCH])
        Km = [sb(f"Km{b}", [P, DK, HG, W2]) for b in range(2)]
        Sb = [sb(f"Sb{b}", [P, HEADS, T]) for b in range(2)]
        Sc = Sb
        Pr = [sb(f"Pr{b}", [P, HEADS, PITCH]) for b in range(2)]
        PTs = [sb(f"PTs{b}", [P, HP, 2, T]) for b in range(2)]
        Vb = [sb(f"Vb{b}", [P, 2, HP, 2 * HD]) for b in range(2)]
        On = [sb(f"On{b}", [P, D]) for b in range(2)]
        OTs = sb("OTs", [P, DK, N])
        mx = [sb(f"mx{b}", [P, HEADS]) for b in range(2)]
        sm = [sb(f"sm{b}", [P, HEADS]) for b in range(2)]
        rs = [sb(f"rs{b}", [P, HEADS]) for b in range(2)]

        gu_w = [sb(f"gu_w{b}", [P, DK, 2 * I0]) for b in range(2)]
        dn_w = [sb(f"dn_w{b}", [P, 6, D]) for b in range(2)]
        gu1_i = sb("gu1_i", [P, DK, 2 * I1], I32)
        dn1_i = sb("dn1_i", [P, 6, D], I32)
        gu1_w = gu1_i[:, :, :].bitcast(F32)
        dn1_w = dn1_i[:, :, :].bitcast(F32)
        Sg = [sb(f"Sg{b}", [P, N]) for b in range(2)]
        Hd = [sb(f"Hd{b}", [P, N]) for b in range(2)]
        r_w = sb("r_w", [P, DK, EXPERTS])
        r_b = sb("r_b", [P, PAIRS * EXPERTS])
        rt = sb("rt", [P, 12, PAIRS * EXPERTS])
        wt_all = sb("wt_all", [EXPERTS, TOKENS])
        wbc = [sb(f"wbc{b}", [P, N]) for b in range(2)]
        yw = [sb(f"yw{b}", [P, N]) for b in range(2)]

        s_cst, s_embw, s_out = sem("s_cst"), sem("s_embw"), sem("s_out")
        s_x = [sem("s_x0"), sem("s_x1")]
        s_attw, s_bias, s_rw, s_w1 = sem("s_attw"), sem("s_bias"), sem("s_rw"), sem("s_w1")
        s_ew = [sem("s_ew0"), sem("s_ew1")]
        s_zero, s_tab, s_deq = sem("s_zero"), sem("s_tab"), sem("s_deq")
        emb_mm, emb_cp = sem("emb_mm"), sem("emb_cp")

        def group(g, w=N):
            return bass.ds(g * N, w)

        def counted(names, prefix):
            return namedtuple("Semaphores", names)(*[sem(prefix + n) for n in names.split()])

        A = [counted("mean_mm var_mm proj_mm S_mm PT_mm V_mm O_mm OT_mm out_mm "
                     "cen squ lnv rsd xn proj km sb mx sc ex sum rs PTs Vb On OTs res", f"a{l}_") for l in range(2)]
        F = [counted("mean_mm var_mm lg_mm wT_mm gu_mm dn_mm cen squ lnv rsd xn xa lg wT sg hd y r r_ex",
                     f"f{l}_") for l in range(2)]
        E = [counted("gu_mm dn_mm w_mm w sg hd yw y", f"e{b}_") for b in range(2)]

        block = ctx.enter_context(nc.Block())
        LOOPED = (GROUPS - 2) // 2

        def over_groups(eng, step):
            with eng.Fori(0, LOOPED) as i:
                for b in range(2):
                    step(2 * i + b, b, False)
            for g in range(2 * LOOPED, GROUPS):
                step(g, g % 2, g == GROUPS - 1)

        @block.sync
        def _(sp):
            sp.dma_start(emb_w[:], embW).then_inc(s_embw, 16)
            sp.dma_start(emb_a[:], embAdd).then_inc(s_embw, 16)
            sp.dma_start(one_s[:], onehot).then_inc(s_embw, 16)
            with sp.Fori(0, GROUPS // 2) as i:
                for b in range(2):
                    g = 2 * i + b
                    sp.wait_ge(emb_mm, g + 1)
                    sp.dma_start(x_in[:, b], xT[bass.ds(g, 1)].rearrange("a p k n -> (a p) k n")).then_inc(s_x[b], 16)
            for e in range(1 + EXPERTS):
                b = e % 2
                if e == 2:
                    sp.wait_ge(F[0].dn_mm, FREE + 6 * GROUPS)
                elif e > 2:
                    sp.wait_ge(E[b].dn_mm, FREE + 6 * GROUPS * ((e - 1) // 2))
                sp.dma_start(gu_w[b][:], gu0[e]).then_inc(s_ew[b], 16)
                sp.dma_start(dn_w[b][:], dn0[e]).then_inc(s_ew[b], 16)
            sp.wait_ge(F[1].y, FREE + 2 * GROUPS)
            sp.dma_start(out, h[:]).then_inc(s_out, 16)
            sp.wait_ge(s_out, 16)

        @block.gpsimd
        def _(pool):
            def km(a, l, n, p, b):
                pool.wait_ge(a.S_mm, n + 1)
                for c in range(DK):
                    src = KT[:, c, p * W2:(p + 1) * W2].unsqueeze(1).to_broadcast([P, HG, W2])
                    ins = pool.tensor_tensor(Km[p % 2][:, c], src, headmask.unsqueeze(2).to_broadcast([P, HG, W2]),
                                             ALU.mult)
                ins.then_inc(a.km, 1)

            def norm(s, g, b):
                pool.wait_ge(s.rsd, FREE + g + 1)
                pool.tensor_tensor(xn[b][:], cen[:], rsd[:].unsqueeze(1).to_broadcast([P, DK, N]),
                                   ALU.mult).then_inc(s.xn, 1)

            def attention(l):
                a = A[l]
                pool.sem_inc(a.xn, FREE)
                pool.sem_inc(a.km, FREE)
                norm(a, 0, 0)
                pool.wait_ge(a.proj, FREE + 4)
                km(a, l, 0, 0, 0)
                km(a, l, 1, 1, 0)

                def step(g, b, last):
                    km(a, l, 4 * g + 2, 2, b)
                    if not last:
                        norm(a, g + 1, 1 - b)
                    km(a, l, 4 * g + 3, 3, b)
                    if not last:
                        pool.wait_ge(a.proj, FREE + 6 * g + 10)
                        km(a, l, 4 * g + 4, 0, 1 - b)
                        km(a, l, 4 * g + 5, 1, 1 - b)
                over_groups(pool, step)

            def ffn(l):
                s = F[l]
                pool.sem_inc(s.xn, FREE)
                pool.sem_inc(s.xa, FREE)

                def front(g, b):
                    norm(s, g, b)
                    if l == 0:
                        pool.wait_ge(s.xn, FREE + g + 1)
                        pool.tensor_copy(xn_all[:, :, group(g)], xn[b][:]).then_inc(s.xa, 1)

                front(0, 0)

                def step(g, b, last):
                    if not last:
                        front(g + 1, 1 - b)
                over_groups(pool, step)

            pool.memset(eps_t[:], EPS).then_inc(s_zero, 1)
            pool.memset(zero_t[:], 0.0).then_inc(s_zero, 1)
            pool.memset(QT[:, :, N:], 0.0).then_inc(s_zero, 1)
            pool.memset(VT[:], 0.0).then_inc(s_zero, 1)
            for b in range(2):
                pool.memset(Pr[b][:], 0.0).then_inc(s_zero, 1)
                pool.memset(Vb[b][:], 0.0).then_inc(s_zero, 1)
                pool.memset(On[b][:], 0.0).then_inc(s_zero, 1)
            pool.memset(bias[0][:], 0.0).then_inc(s_zero, 1)
            pool.memset(bias[1][:], 0.0).then_inc(s_zero, 1)
            pool.wait_ge(s_bias, 32)
            for l in range(2):
                for q in (0, PITCH):
                    tab = bias[l][q:q + T]
                    pool.affine_select(out=tab, in_=tab, compare_op=ALU.is_ge, fill=-BIG, base=0,
                                       pattern=[[0, HEADS], [-1, T]], channel_multiplier=1).then_inc(s_tab, 1)
            pool.wait_ge(s_cst, 16)
            attention(0)
            pool.wait_ge(s_w1, 32)
            pool.tensor_scalar(gu1_w, gu1_i[:], SCALE1, None, ALU.mult).then_inc(s_deq, 1)
            pool.tensor_scalar(dn1_w, dn1_i[:], SCALE1, None, ALU.mult).then_inc(s_deq, 1)
            ffn(0)
            attention(1)
            ffn(1)

        @block.scalar
        def _(act):
            act.dma_start(cst[:], consts).then_inc(s_cst, 16)
            for l, (w, o, ob) in enumerate(((qkv0, wo0, wob0), (qkv1, wo1, wob1))):
                act.dma_start(qkv_w[l][:], w).then_inc(s_attw, 16)
                act.dma_start(out_w[l][:], o).then_inc(s_attw, 16)
                act.dma_start(out_b[l][:], ob).then_inc(s_attw, 16)
            act.dma_start(qkv_b[:], qkvb0).then_inc(s_attw, 16)
            act.dma_start(r_w[:], rT).then_inc(s_rw, 16)
            act.dma_start(r_b[:], rb).then_inc(s_rw, 16)
            act.dma_start(gu1_i[:], gu1).then_inc(s_w1, 16)
            act.dma_start(dn1_i[:], dn1).then_inc(s_w1, 16)
            act.wait_ge(s_zero, 12)
            for q in (0, PITCH):
                act.dma_start(bias[0][q:q + T], bias0).then_inc(s_bias, 16)

            act.sem_inc(emb_cp, FREE)
            with act.Fori(0, GROUPS // 2) as i:
                for b in range(2):
                    g = 2 * i + b
                    act.wait_ge(emb_mm, FREE + g + 1)
                    act.activation(h[:, :, group(g)], ps[:, 2 * b:2 * b + 2, 0:N], ACT.Copy).then_inc(emb_cp, 1)

            def squares(s, g):
                act.wait_ge(s.cen, FREE + g + 1)
                act.activation(squ[:], cen[:], ACT.Square).then_inc(s.squ, 1)

            def deviation(s, g, bk):
                act.wait_ge(s.var_mm, g + 1)
                act.activation(lnv[:], ps[:, bk, 0:N], ACT.Ln, bias=eps_t[:]).then_inc(s.lnv, 1)
                act.wait_ge(s.lnv, FREE + g + 1)
                act.activation(rsd[:], lnv[:], ACT.Exp, bias=zero_t[:], scale=-0.5).then_inc(s.rsd, 1)

            def attention(l):
                a = A[l]
                for buf_free in (a.squ, a.lnv, a.rsd, a.proj, a.ex, a.PTs, a.OTs):
                    act.sem_inc(buf_free, FREE)

                def project(g, b, k, bk):
                    act.wait_ge(a.proj_mm, 6 * g + k + 1)
                    if k < 2 * DK:
                        dst, src = (QT, KT)[k // DK][:, k % DK, 0:N], ps[:, bk, 0:N]
                    else:
                        dst = VT[:, k % DK, :, :, 0:T]
                        src = ps[:, bk, 0:N].rearrange("p (i t) -> p i t", t=T).unsqueeze(2).to_broadcast([P, GI, 2, T])
                    act.activation(dst, src, ACT.Identity,
                                   bias=qkv_b[:, k:k + 1] if l == 0 else zero_t[:]).then_inc(a.proj, 1)

                def exps(n, p):
                    act.wait_ge(a.sc, FREE + n + 1)
                    act.wait_ge(a.PT_mm, n + 1)
                    act.wait_ge(a.sum, n + 1)
                    act.activation(Pr[p % 2][:, :, 0:T], Sc[p % 2][:], ACT.Exp).then_inc(a.ex, 1)

                def probs_t(n, p):
                    act.wait_ge(a.PT_mm, FREE + n + 1)
                    act.wait_ge(a.O_mm, n + 1)
                    src = ps[:, 4:6, :].rearrange("p b (h i q) -> p (b h) i q", h=HP // 2, i=2)[:, :, :, 0:T]
                    act.activation(PTs[p % 2][:], src, ACT.Copy).then_inc(a.PTs, 1)

                def out_t(n, p, bk):
                    act.wait_ge(a.OT_mm, FREE + n + 1)
                    src = ps[:, bk, 0:DK * P].rearrange("p (c i q) -> p c i q", c=DK, i=2)[:, :, :, 0:T]
                    dst = OTs[:, :, p * W2:(p + 1) * W2].rearrange("p c (i q) -> p c i q", i=2)
                    act.activation(dst, src, ACT.Copy).then_inc(a.OTs, 1)

                squares(a, 0)
                deviation(a, 0, 7)
                for k in range(6):
                    project(0, 0, k, 6 + k % 2)

                def step(g, b, last):
                    X = LAST if last else BODY
                    n = 4 * g
                    exps(n, 0)
                    exps(n + 1, 1)
                    if not last:
                        squares(a, g + 1)
                    probs_t(n, 0)
                    exps(n + 2, 2)
                    if not last:
                        deviation(a, g + 1, X.bank("var"))
                    probs_t(n + 1, 1)
                    out_t(n, 0, X.bank("OT0"))
                    exps(n + 3, 3)
                    probs_t(n + 2, 2)
                    out_t(n + 1, 1, X.bank("OT1"))
                    if not last:
                        for k in range(3):
                            project(g + 1, 1 - b, k, X.bank(f"proj{k}"))
                    probs_t(n + 3, 3)
                    out_t(n + 2, 2, X.bank("OT2"))
                    if not last:
                        for k in range(3, 6):
                            project(g + 1, 1 - b, k, X.bank(f"proj{k}"))
                    out_t(n + 3, 3, X.bank("OT3"))
                over_groups(act, step)

            def silus(s, g, rows):
                for j, r in enumerate(rows):
                    act.wait_ge(s.gu_mm, len(rows) * g + j + 1)
                    act.wait_ge(s.hd, len(rows) * g + j + 1)
                    act.activation(Sg[j % 2][0:r], ps[0:r, 2 * (j % 2), 0:N], ACT.Silu).then_inc(s.sg, 1)
                    yield j

            def ffn(l):
                s = F[l]
                for buf_free in (s.squ, s.lnv, s.rsd, s.wT):
                    act.sem_inc(buf_free, FREE)

                def r_exp(g):
                    if l == 0:
                        act.wait_ge(s.r, RCHAIN * g + 10)
                        act.activation(rt[0:W2, 9, 0:PAIRS], rt[0:W2, 8, 0:PAIRS], ACT.Exp).then_inc(s.r_ex, 1)

                squares(s, 0)
                deviation(s, 0, 7)
                r_exp(0)

                def step(g, b, last):
                    for j in silus(s, g, hidden_chunks((I0, I1)[l])):
                        if j == 0 and l == 0:
                            act.wait_ge(s.wT_mm, 1 + g + 1)
                            act.activation(wt_all[:, group(g)], ps[0:EXPERTS, 7, 0:N], ACT.Copy).then_inc(s.wT, 1)
                        if j == 2 and not last:
                            squares(s, g + 1)
                        if j == 4 and not last:
                            deviation(s, g + 1, 7)
                    if not last:
                        r_exp(g + 1)
                over_groups(act, step)

            def expert(e):
                s = E[e % 2]
                first = GROUPS * ((e - 1) // 2)
                if e < 3:
                    act.sem_inc(s.w, FREE)

                def step(g, b, last):
                    g = g + first
                    act.wait_ge(s.w_mm, g + 1)
                    act.wait_ge(s.y, 2 * g + 1)
                    act.activation(wbc[b][:], ps[:, 6 + b, 0:N], ACT.Copy).then_inc(s.w, 1)
                    for j in silus(s, g, hidden_chunks(I0)):
                        pass
                over_groups(act, step)

            attention(0)
            ffn(0)
            for e in range(1, 1 + EXPERTS):
                expert(e)
            attention(1)
            ffn(1)

        @block.vector
        def _(dve):
            def centre(s, g, bk):
                dve.wait_ge(s.mean_mm, g + 1)
                dve.tensor_tensor(cen[:], h[:, :, group(g)], ps[:, bk, 0:N].unsqueeze(1).to_broadcast([P, DK, N]),
                                  ALU.subtract).then_inc(s.cen, 1)

            def attention(l):
                a = A[l]
                for buf_free in (a.cen, a.sb, a.mx, a.sc, a.sum, a.rs, a.Vb, a.On, a.res):
                    dve.sem_inc(buf_free, FREE)

                def softmax_in(n, p):
                    b = p % 2
                    dve.wait_ge(a.S_mm, FREE + n + 1)
                    dve.wait_ge(a.ex, n + 1)
                    src = ps[:, 2 * b:2 * b + 2, :].rearrange("p b (h k) -> p (b h) k", k=PITCH)[:, :, 0:T]
                    dve.scalar_tensor_tensor(out=Sb[b][:], in0=src, scalar=HD ** -0.5, in1=bias[l][:],
                                             op0=ALU.mult, op1=ALU.add).then_inc(a.sb, 1)
                    dve.wait_ge(a.sb, FREE + n + 1)
                    dve.tensor_reduce(mx[b][:], Sb[b][:], AX_X, ALU.max).then_inc(a.mx, 1)
                    dve.wait_ge(a.mx, FREE + n + 1)
                    dve.tensor_tensor(Sc[b][:], Sb[b][:], mx[b][:].unsqueeze(2).to_broadcast([P, HEADS, T]),
                                      ALU.subtract).then_inc(a.sc, 1)

                def sums(n, p):
                    b = p % 2
                    dve.wait_ge(a.ex, FREE + n + 1)
                    dve.tensor_reduce(sm[b][:], Pr[b][:, :, 0:T], AX_X, ALU.add).then_inc(a.sum, 1)
                    dve.wait_ge(a.sum, FREE + n + 1)
                    dve.reciprocal(rs[b][:], sm[b][:]).then_inc(a.rs, 1)

                def values(n, p, bk):
                    dve.wait_ge(a.V_mm, n + 1)
                    dve.wait_ge(a.O_mm, n + 1)
                    for half in range(2):
                        rows = slice(half * PITCH, half * PITCH + PITCH)
                        cols = slice(half * HD, half * HD + HD)
                        src = ps[rows, bk, :].rearrange("p (r w) -> p r w", w=2 * HD)[:, :, cols]
                        dst = Vb[p % 2][rows].rearrange("p i h w -> p (i h) w")[:, :, cols]
                        ins = dve.tensor_copy(dst, src)
                    ins.then_inc(a.Vb, 1)

                def normalise(n, p, bk):
                    b = p % 2
                    dve.wait_ge(a.O_mm, FREE + n + 1)
                    dve.wait_ge(a.rs, FREE + n + 1)
                    dve.wait_ge(a.OT_mm, n + 1)
                    for i in range(2):
                        r = slice(i * PITCH, i * PITCH + T)
                        ins = dve.tensor_tensor(On[b][r].rearrange("p (h d) -> p h d", d=HD),
                                                ps[r, bk, 0:D].rearrange("p (h d) -> p h d", d=HD),
                                                rs[b][r].unsqueeze(2).to_broadcast([T, HEADS, HD]), ALU.mult)
                    ins.then_inc(a.On, 1)

                def residual(g, m, bk):
                    dve.wait_ge(a.out_mm, 2 * g + m + 1)
                    hm = h[:, m, group(g)]
                    dve.scalar_tensor_tensor(out=hm, in0=ps[:, bk, 0:N], scalar=out_b[l][:, m:m + 1], in1=hm,
                                             op0=ALU.add, op1=ALU.add).then_inc(a.res, 1)

                centre(a, 0, 6)

                def step(g, b, last):
                    X = LAST if last else BODY
                    n = 4 * g
                    softmax_in(n, 0)
                    values(n, 0, X.bank("V0"))
                    softmax_in(n + 1, 1)
                    values(n + 1, 1, X.bank("V1"))
                    sums(n, 0)
                    if not last:
                        centre(a, g + 1, X.bank("mean"))
                    normalise(n, 0, X.bank("O0"))
                    softmax_in(n + 2, 2)
                    values(n + 2, 2, X.bank("V2"))
                    sums(n + 1, 1)
                    normalise(n + 1, 1, X.bank("O1"))
                    softmax_in(n + 3, 3)
                    values(n + 3, 3, X.bank("V3"))
                    sums(n + 2, 2)
                    normalise(n + 2, 2, X.bank("O2"))
                    sums(n + 3, 3)
                    normalise(n + 3, 3, X.bank("O3"))
                    residual(g, 0, X.bank("out0"))
                    residual(g, 1, X.bank("out1"))
                over_groups(dve, step)

            def gates(s, g, rows):
                for j, r in enumerate(rows):
                    n = len(rows) * g + j
                    dve.wait_ge(s.sg, n + 1)
                    dve.wait_ge(s.dn_mm, n + 1)
                    up = ps[0:P, 2 * (j % 2) + 1, 0:N] if r == P else ps[r:2 * r, 2 * (j % 2), 0:N]
                    dve.tensor_tensor(Hd[j % 2][0:r], Sg[j % 2][0:r], up, ALU.mult).then_inc(s.hd, 1)
                    yield j

            def ffn(l):
                s = F[l]
                for buf_free in (s.cen, s.hd, s.y, s.lg):
                    dve.sem_inc(buf_free, FREE)

                def route(g):
                    R = slice(0, W2)
                    base = RCHAIN * g
                    step = [0]

                    def t(i):
                        return rt[R, i].rearrange("p (a e) -> p a e", e=EXPERTS)

                    def c(i):
                        return rt[R, i, 0:PAIRS]

                    def wide(i):
                        return c(i).unsqueeze(2).to_broadcast([W2, PAIRS, EXPERTS])

                    def link(ins):
                        ins.then_inc(s.r, 1)
                        step[0] += 1
                        dve.wait_ge(s.r, base + step[0])

                    pr = prio[R].rearrange("p (a e) -> p a e", e=EXPERTS)
                    dve.wait_ge(s.lg_mm, g + 1)
                    dve.wait_ge(s.wT_mm, g + 1)
                    dve.tensor_tensor(rt[R, 0], ps[R, 6, 0:PAIRS * EXPERTS], r_b[R], ALU.add).then_inc(s.lg, 1)
                    dve.wait_ge(s.lg, FREE + g + 1)
                    link(dve.tensor_reduce(c(1), t(0), AX_X, ALU.max))
                    link(dve.tensor_tensor(t(2), t(0), wide(1), ALU.is_equal))
                    link(dve.tensor_tensor(t(2), t(2), pr, ALU.mult))
                    link(dve.tensor_reduce(c(3), t(2), AX_X, ALU.max))
                    link(dve.tensor_tensor(t(4), t(2), wide(3), ALU.is_equal))
                    link(dve.scalar_tensor_tensor(out=t(5), in0=t(4), scalar=-BIG, in1=t(0), op0=ALU.mult, op1=ALU.add))
                    link(dve.tensor_reduce(c(6), t(5), AX_X, ALU.max))
                    link(dve.tensor_tensor(t(7), t(5), wide(6), ALU.is_equal))
                    link(dve.tensor_tensor(t(7), t(7), pr, ALU.mult))
                    link(dve.tensor_tensor(c(8), c(6), c(1), ALU.subtract))
                    link(dve.tensor_reduce(c(3), t(7), AX_X, ALU.max))
                    link(dve.tensor_tensor(t(5), t(7), wide(3), ALU.is_equal))
                    dve.wait_ge(s.r_ex, g + 1)
                    link(dve.tensor_scalar(c(1), c(9), 1.0, None, ALU.add))
                    link(dve.reciprocal(c(6), c(1)))
                    link(dve.tensor_tensor(c(1), c(6), c(9), ALU.mult))
                    link(dve.tensor_tensor(t(10), t(4), wide(6), ALU.mult))
                    link(dve.tensor_tensor(t(11), t(5), wide(1), ALU.mult))
                    link(dve.tensor_tensor(t(10), t(10), t(11), ALU.add))
                    assert step[0] == RCHAIN

                def add_y(g):
                    dve.wait_ge(s.dn_mm, FREE + 6 * g + 6)
                    for m in range(DK):
                        hm = h[:, m, group(g)]
                        dve.tensor_tensor(hm, hm, ps[:, 4 + m, 0:N], ALU.add).then_inc(s.y, 1)

                centre(s, 0, 6)
                if l == 0:
                    route(0)

                def step(g, b, last):
                    for j in gates(s, g, hidden_chunks((I0, I1)[l])):
                        if j == 1 and not last:
                            centre(s, g + 1, 6)
                    add_y(g)
                    if l == 0 and not last:
                        route(g + 1)
                over_groups(dve, step)

            def expert(e):
                s = E[e % 2]
                first = GROUPS * ((e - 1) // 2)
                if e < 3:
                    for buf_free in (s.hd, s.y, s.yw):
                        dve.sem_inc(buf_free, FREE)

                def step(g, b, last):
                    k = g + first
                    for j in gates(s, k, hidden_chunks(I0)):
                        pass
                    dve.wait_ge(s.dn_mm, FREE + 6 * k + 6)
                    dve.wait_ge(s.w, FREE + k + 1)
                    for m in range(DK):
                        dve.tensor_tensor(yw[m][:], wbc[b][:], ps[:, 4 + m, 0:N], ALU.mult).then_inc(s.yw, 1)
                    for m in range(DK):
                        dve.wait_ge(s.yw, FREE + 2 * k + m + 1)
                        hm = h[:, m, group(g)]
                        dve.tensor_tensor(hm, hm, yw[m][:], ALU.add).then_inc(s.y, 1)
                over_groups(dve, step)

            dve.wait_ge(emb_cp, FREE + GROUPS)
            dve.wait_ge(s_tab, 4)
            attention(0)
            dve.wait_ge(s_rw, 32)
            dve.wait_ge(A[0].res, FREE + 2 * GROUPS)
            ffn(0)
            dve.wait_ge(F[0].y, FREE + 2 * GROUPS)
            for e in range(1, 1 + EXPERTS):
                expert(e)
                dve.wait_ge(E[e % 2].y, FREE + 2 * GROUPS * ((e + 1) // 2))
            attention(1)
            dve.wait_ge(A[1].res, FREE + 2 * GROUPS)
            ffn(1)

        @block.tensor
        def _(pe):
            def mm(out_, lhsT, rhs, start=True, stop=True):
                return pe.matmul(out_, lhsT, rhs, start=start, stop=stop)

            pe.sem_inc(emb_mm, FREE)
            pe.wait_ge(s_embw, 48)
            with pe.Fori(0, GROUPS // 2) as i:
                for b in range(2):
                    g = 2 * i + b
                    pe.wait_ge(s_x[b], 16 * i + 16)
                    pe.wait_ge(emb_cp, g + 1)
                    for m in range(DK):
                        o = ps[:, 2 * b + m, 0:N]
                        cols = slice(m * P, m * P + P)
                        mm(o, emb_a[:, cols], one_s[:], True, False)
                        for k in range(PK):
                            ins = mm(o, emb_w[:, k, cols], x_in[:, b, k], False, k == PK - 1)
                    ins.then_inc(emb_mm, 1)

            def mean(s, g, bk):
                o = ps[:, bk, 0:N]
                for c in range(DK):
                    ins = mm(o, mean_w, h[:, c, group(g)], c == 0, c == DK - 1)
                ins.then_inc(s.mean_mm, 1)

            def variance(s, g, bk):
                pe.wait_ge(s.squ, FREE + g + 1)
                o = ps[:, bk, 0:N]
                for c in range(DK):
                    ins = mm(o, mean_w, squ[:, c], c == 0, c == DK - 1)
                ins.then_inc(s.var_mm, 1)

            def attention(l):
                a = A[l]
                for buf_free in (a.S_mm, a.PT_mm, a.O_mm, a.OT_mm):
                    pe.sem_inc(buf_free, FREE)

                def free(X, name, g):
                    prev = X.before(name)
                    if prev is None:
                        pe.wait_ge(a.res, FREE + 2 * g)
                        return
                    kind, k = prev.rstrip("0123456789"), int(prev[-1]) if prev[-1].isdigit() else 0
                    if kind == "V":
                        pe.wait_ge(a.Vb, FREE + 4 * g + k + 1)
                    elif kind == "O":
                        pe.wait_ge(a.On, FREE + 4 * g + k + 1)
                    elif kind == "OT":
                        pe.wait_ge(a.OTs, FREE + 4 * g + k + 1)
                    elif kind == "mean":
                        pe.wait_ge(a.cen, FREE + g + 2)
                    elif kind == "var":
                        pe.wait_ge(a.lnv, FREE + g + 2)
                    elif kind == "proj":
                        pe.wait_ge(a.proj, FREE + 6 * (g + 1) + k + 1)
                    elif kind == "out":
                        pe.wait_ge(a.res, FREE + 2 * g + k + 1)

                def project(g, b, k, bk):
                    pe.wait_ge(a.xn, FREE + g + 1)
                    for c in range(DK):
                        ins = mm(ps[:, bk, 0:N], qkv_w[l][:, c, k * P:(k + 1) * P], xn[b][:, c], c == 0, c == DK - 1)
                    ins.then_inc(a.proj_mm, 1)

                def scores(n, p, b):
                    pe.wait_ge(a.km, FREE + n + 1)
                    pe.wait_ge(a.sb, n + 1)
                    for c in range(DK):
                        for i in range(2):
                            o = ps[i * PITCH:(i + 1) * PITCH, 2 * (p % 2) + c, :].rearrange("p (h k) -> p h k", k=PITCH)
                            q0 = (2 * p + i) * T
                            ins = mm(o[:, :, 0:T], QT[:, c, q0:q0 + PITCH], Km[p % 2][:, c, :, i * T:(i + 1) * T])
                    ins.then_inc(a.S_mm, 1)

                def values(n, p, b, bk):
                    for i in range(2):
                        for c in range(DK):
                            src = VT[:, c, 2 * p + i].rearrange("p a k -> p (a k)")
                            ins = pe.transpose(ps[:, bk, i * D + c * P:i * D + (c + 1) * P], src, ident)
                    ins.then_inc(a.V_mm, 1)

                def probs_t(n, p):
                    pe.wait_ge(a.ex, FREE + n + 1)
                    pe.wait_ge(a.PTs, FREE + n)
                    for hp in range(HP):
                        ins = pe.transpose(ps[:, 4 + hp // 4, (hp % 4) * P:(hp % 4 + 1) * P],
                                           Pr[p % 2][:, 2 * hp:2 * hp + 2, :].rearrange("p a k -> p (a k)"), ident)
                    ins.then_inc(a.PT_mm, 1)

                def outputs(n, p, bk):
                    pe.wait_ge(a.PTs, FREE + n + 1)
                    pe.wait_ge(a.Vb, FREE + n + 1)
                    for i in range(2):
                        for hp in range(HP):
                            ins = mm(ps[i * PITCH:i * PITCH + T, bk, hp * 2 * HD:(hp + 1) * 2 * HD],
                                     PTs[p % 2][:, hp, i], Vb[p % 2][:, i, hp])
                    ins.then_inc(a.O_mm, 1)

                def outputs_t(n, p, bk):
                    pe.wait_ge(a.On, FREE + n + 1)
                    for c in range(DK):
                        ins = pe.transpose(ps[:, bk, c * P:(c + 1) * P], On[p % 2][:, c * P:(c + 1) * P], ident)
                    ins.then_inc(a.OT_mm, 1)

                def out_proj(g, m, bk):
                    pe.wait_ge(a.OTs, FREE + 4 * g + 4)
                    for c in range(DK):
                        ins = mm(ps[:, bk, 0:N], out_w[l][:, c, m * P:(m + 1) * P], OTs[:, c], c == 0, c == DK - 1)
                    ins.then_inc(a.out_mm, 1)

                mean(a, 0, 6)
                variance(a, 0, 7)
                for k in range(6):
                    if k == 0:
                        pe.wait_ge(a.cen, FREE + 1)
                    elif k == 1:
                        pe.wait_ge(a.lnv, FREE + 1)
                    else:
                        pe.wait_ge(a.proj, FREE + k - 1)
                    project(0, 0, k, 6 + k % 2)

                def step(g, b, last):
                    X = LAST if last else BODY
                    n = 4 * g

                    def at(name, do, *args):
                        free(X, name, g)
                        do(*args, X.bank(name))

                    scores(n, 0, b)
                    pe.wait_ge(a.proj, FREE + 6 * g + 6)
                    at("V0", values, n, 0, b)
                    scores(n + 1, 1, b)
                    at("V1", values, n + 1, 1, b)
                    if not last:
                        at("mean", mean, a, g + 1)
                    probs_t(n, 0)
                    at("O0", outputs, n, 0)
                    scores(n + 2, 2, b)
                    at("V2", values, n + 2, 2, b)
                    if not last:
                        at("var", variance, a, g + 1)
                    probs_t(n + 1, 1)
                    at("O1", outputs, n + 1, 1)
                    at("OT0", outputs_t, n, 0)
                    scores(n + 3, 3, b)
                    at("V3", values, n + 3, 3, b)
                    probs_t(n + 2, 2)
                    at("O2", outputs, n + 2, 2)
                    at("OT1", outputs_t, n + 1, 1)
                    if not last:
                        for k in range(3):
                            at(f"proj{k}", project, g + 1, 1 - b, k)
                    probs_t(n + 3, 3)
                    at("O3", outputs, n + 3, 3)
                    at("OT2", outputs_t, n + 2, 2)
                    if not last:
                        for k in range(3, 6):
                            at(f"proj{k}", project, g + 1, 1 - b, k)
                    at("OT3", outputs_t, n + 3, 3)
                    at("out0", out_proj, g, 0)
                    at("out1", out_proj, g, 1)
                over_groups(pe, step)

            def gate_up(s, g, j, rows, w, x):
                nj = len(rows)
                pe.wait_ge(s.hd, nj * g + j + 1)
                for half in range(2 if rows[j] == P else 1):
                    c0 = (2 * j + half) * P
                    for c in range(DK):
                        ins = mm(ps[:, 2 * (j % 2) + half, 0:N], w[:, c, c0:c0 + P], x(c), c == 0, c == DK - 1)
                ins.then_inc(s.gu_mm, 1)

            def down(s, g, j, rows, w):
                nj, r = len(rows), rows[j]
                pe.wait_ge(s.hd, FREE + nj * g + j + 1)
                if j == 0:
                    pe.wait_ge(s.y, FREE + 2 * g)
                for m in range(DK):
                    ins = pe.matmul(ps[:, 4 + m, 0:N], w[0:r, j, m * P:(m + 1) * P], Hd[j % 2][0:r],
                                    start=(j == 0), stop=(j == nj - 1))
                ins.then_inc(s.dn_mm, 1)

            def ffn(l, w_gu, w_dn):
                s = F[l]
                rows = hidden_chunks((I0, I1)[l])
                pe.sem_inc(s.dn_mm, FREE)
                if l == 0:
                    pe.sem_inc(s.wT_mm, 1)

                def logits(g, b):
                    if l == 0:
                        pe.wait_ge(s.xn, FREE + g + 1)
                        pe.wait_ge(s.cen, FREE + g + 1)
                        for p in range(PAIRS):
                            for c in range(DK):
                                ins = mm(ps[0:W2, 6, p * EXPERTS:(p + 1) * EXPERTS], xn[b][:, c, p * W2:(p + 1) * W2],
                                         r_w[:, c], c == 0, c == DK - 1)
                        ins.then_inc(s.lg_mm, 1)

                def weights_t(g):
                    if l == 0:
                        pe.wait_ge(s.r, RCHAIN * (g + 1))
                        pe.wait_ge(s.lnv, FREE + g + 1)
                        for p in range(PAIRS):
                            ins = pe.transpose(ps[0:EXPERTS, 7, p * W2:(p + 1) * W2],
                                               rt[0:W2, 10, p * EXPERTS:(p + 1) * EXPERTS], ident[0:W2, 0:W2])
                        ins.then_inc(s.wT_mm, 1)

                mean(s, 0, 6)
                variance(s, 0, 7)
                logits(0, 0)

                def step(g, b, last):
                    x = lambda c: xn[b][:, c]
                    pe.wait_ge(s.xn, FREE + g + 1)
                    nj = len(rows)
                    for j in range(nj):
                        gate_up(s, g, j, rows, w_gu, x)
                        if j == 0:
                            weights_t(g)
                        if j == 1 and not last:
                            if l == 0:
                                pe.wait_ge(s.lg, FREE + g + 1)
                            mean(s, g + 1, 6)
                        if j == 3 and not last:
                            if l == 0:
                                pe.wait_ge(s.wT, FREE + g + 1)
                            variance(s, g + 1, 7)
                        if j == nj - 1 and not last:
                            logits(g + 1, 1 - b)
                        if j:
                            down(s, g, j - 1, rows, w_dn)
                    down(s, g, nj - 1, rows, w_dn)
                over_groups(pe, step)

            def expert(e):
                s = E[e % 2]
                first = GROUPS * ((e - 1) // 2)
                rows = hidden_chunks(I0)
                if e < 3:
                    pe.sem_inc(s.dn_mm, FREE)

                def step(g, b, last):
                    k = g + first
                    pe.wait_ge(s.w, k + 1)
                    mm(ps[:, 6 + b, 0:N], pick[:, e - 1], wt_all[:, group(g)]).then_inc(s.w_mm, 1)
                    x = lambda c: xn_all[:, c, group(g)]
                    for j in range(len(rows)):
                        gate_up(s, k, j, rows, gu_w[e % 2], x)
                        if j:
                            down(s, k, j - 1, rows, dn_w[e % 2])
                    down(s, k, len(rows) - 1, rows, dn_w[e % 2])
                over_groups(pe, step)

            pe.wait_ge(s_cst, 16)
            pe.wait_ge(s_attw, 16 * 7)
            pe.wait_ge(s_zero, 12)
            pe.wait_ge(emb_cp, FREE + GROUPS)
            attention(0)
            pe.wait_ge(A[0].res, FREE + 2 * GROUPS)
            pe.wait_ge(s_ew[0], 32)
            pe.wait_ge(s_rw, 32)
            ffn(0, gu_w[0], dn_w[0])
            pe.wait_ge(F[0].y, FREE + 2 * GROUPS)
            pe.wait_ge(F[0].wT, FREE + GROUPS)
            pe.wait_ge(F[0].xa, FREE + GROUPS)
            for e in range(1, 1 + EXPERTS):
                pe.wait_ge(s_ew[e % 2], 32 * (e // 2 + 1))
                expert(e)
                pe.wait_ge(E[e % 2].y, FREE + 2 * GROUPS * ((e + 1) // 2))
            attention(1)
            pe.wait_ge(A[1].res, FREE + 2 * GROUPS)
            pe.wait_ge(s_deq, 2)
            ffn(1, gu1_w, dn1_w)


RCHAIN = 18


class Turn:

    def __init__(self, order):
        self.order = order.split()

    def bank(self, name):
        return 6 + self.order.index(name) % 2

    def before(self, name):
        i = self.order.index(name)
        return self.order[i - 2] if i >= 2 else None


BODY = Turn("V0 V1 mean O0 V2 var O1 OT0 V3 O2 OT1 proj0 proj1 proj2 O3 OT2 proj3 proj4 proj5 OT3 out0 out1")
LAST = Turn("V0 V1 O0 V2 O1 OT0 V3 O2 OT1 O3 OT2 OT3 out0 out1")

_INS = "xT onehot embW embAdd consts qkv0 qkvb0 wo0 wob0 bias0 qkv1 wo1 wob1 gu0 dn0 rT rb gu1 dn1".split()


def kernel(**inputs):
    import numpy as np
    import concourse.bacc as bacc
    from concourse.bass_utils import run_bass_kernel_spmd

    v = {k: np.asarray(a) for k, a in inputs.items()}

    def rows(w):
        return w.reshape(-1, P, w.shape[1]).transpose(1, 0, 2)

    def cols(b):
        return b.reshape(-1, P).T

    side = SIDE // PATCH
    px = v["x"].reshape(IMAGES, CHANNELS, side, PATCH, side, PATCH).transpose(0, 2, 4, 1, 3, 5)
    px = px.reshape(IMAGES, T - 1, PK * P)
    px = np.concatenate([np.zeros((IMAGES, 1, PK * P), px.dtype), px], axis=1)
    onehot = np.zeros((ADDED, N), np.float32)
    at = np.arange(N)
    onehot[at % T, at] = 1.0
    onehot[T, at[at % T == 0]] = 1.0
    onehot[T + 1, at[at % T != 0]] = 1.0

    consts = np.zeros((P, 3 * P + HG + PAIRS * EXPERTS + EXPERTS * P), np.float32)
    consts[:, 0:P] = np.eye(P)
    consts[:, P:2 * P] = 1.0 / D
    consts[np.arange(P), 3 * P + np.arange(P) // HD] = 1.0
    o = 3 * P + HG
    consts[:, o:o + PAIRS * EXPERTS] = np.tile(EXPERTS - np.arange(EXPERTS), PAIRS)
    o += PAIRS * EXPERTS
    for e in range(EXPERTS):
        consts[e, o + e * P:o + (e + 1) * P] = 1.0

    def gate_up(g, u):
        parts = [w[a:a + P] for a in range(0, g.shape[0], P) for w in (g, u)]
        return rows(np.concatenate(parts, axis=0).T)

    def down(d):
        w = d.T
        pad = -w.shape[0] % P
        return rows(np.concatenate([w, np.zeros((pad, D), w.dtype)], axis=0))

    relT = v["L0_attn_rel_emb"].T
    mid = (v["L0_attn_rel_emb"].shape[0] - 1) // 2
    gs = [v["L0_ffn_sg"], *v["L0_ffn_rg"]]
    us = [v["L0_ffn_su"], *v["L0_ffn_ru"]]
    ds = [v["L0_ffn_sd"], *v["L0_ffn_rd"]]
    arrays = {
        "xT": px.reshape(GROUPS, N, PK, P).transpose(0, 3, 2, 1),
        "onehot": onehot,
        "embW": rows(v["L0_tok_W"].T),
        "embAdd": np.concatenate([v["L0_tok_pos_enc"][0], v["L0_tok_cls_token"][0], v["L0_tok_b"][None]], axis=0),
        "consts": consts,
        "qkv0": rows(v["L0_attn_Wqkv"]),
        "qkvb0": cols(v["L0_attn_bqkv"]),
        "wo0": rows(v["L0_attn_Wout"]),
        "wob0": cols(v["L0_attn_bout"]),
        "bias0": np.stack([relT[:, mid - q:mid - q + T] for q in range(T)]),
        "qkv1": rows(np.concatenate([v["L1_attn_Wq"].T, v["L1_attn_Wk"].T, v["L1_attn_Wv"].T], axis=1)),
        "wo1": rows(v["L1_attn_Wo"].T),
        "wob1": cols(v["L1_attn_bo"]),
        "gu0": np.stack([gate_up(g, u) for g, u in zip(gs, us)]),
        "dn0": np.stack([down(d) for d in ds]),
        "rT": rows(v["L0_ffn_wr"].T),
        "rb": np.broadcast_to(v["L0_ffn_rb"], (P, PAIRS, EXPERTS)).reshape(P, PAIRS * EXPERTS),
        "gu1": gate_up(v["L1_ffn_w_gate"], v["L1_ffn_w_up"]),
        "dn1": down(v["L1_ffn_w_down"]),
    }
    nc = bacc.Bacc("TRN2", target_bir_lowering=False, num_devices=1)
    arrays = {f"in_{k}_dram": np.ascontiguousarray(arrays[k]) for k in _INS}
    args = [nc.dram_tensor(k, a.shape, mybir.dt.from_np(a.dtype), kind="ExternalInput").ap() for k, a in arrays.items()]
    out = nc.dram_tensor("out_0_dram", (P, DK, TOKENS), F32, kind="ExternalOutput").ap()
    vit_kernel(nc, *args, out)
    r = run_bass_kernel_spmd(nc, [arrays], core_ids=[0])
    got = r.results[0]["out_0_dram"]
    return got.transpose(2, 1, 0).reshape(IMAGES, T, D)
```

```python
from collections import namedtuple
from contextlib import ExitStack

import concourse.bass as bass
import numpy as np
from concourse import mybir

ALU = mybir.AluOpType
ACT = mybir.ActivationFunctionType
F32 = mybir.dt.float32
I32 = mybir.dt.int32
U32 = mybir.dt.uint32
AX_X = mybir.AxisListType.X

P = 128
IMAGES, CHANNELS, SIDE, PATCH = 64, 3, 96, 16
T = (SIDE // PATCH) ** 2 + 1
D = 256
DK = D // P
PK = CHANNELS * PATCH * PATCH // P
EK = PK + 1
ADDED = T + 2
TOKENS = IMAGES * T
GI = 8
GROUPS = IMAGES // GI
N = GI * T
PAIRS = GI // 2
W2 = 2 * T
PITCH = 64
NPAD = (GI - 1) * T + PITCH
HEADS = 16
HD = D // HEADS
HG = P // HD
HP = HEADS // 2
EXPERTS = 7
I0, I1 = 704, 768
SCALE1 = 1.0 / 127.0
EPS = 1e-5
BIG = 3.0e38
XW = D + 1
REGION = TOKENS + P
TILES = (2 * TOKENS + EXPERTS * (P - 1)) // P
SPARE = TILES - 2 * TOKENS // P
KT_MAX = -(-TOKENS // P)
ROWS = EXPERTS * REGION + SPARE * P
EW = DK * 2 * I0 + 6 * D
IH = I0 // 2
FREE = 2


def hidden_chunks(width):
    return [min(P, width - a) for a in range(0, width, P)]


def vit_kernel(nc, xT, onehot, embW, embAdd, consts, qkv0, qkvb0, wo0, wob0, bias0, qkv1, wo1, wob1,
               gu0, dn0, ew, rT, rb, gu1, dn1, xs, ys, out):
    with ExitStack() as ctx:
        def sb(name, shape, dt=F32):
            return ctx.enter_context(nc.sbuf_tensor(name, shape, dt))

        def sem(name):
            return ctx.enter_context(nc.semaphore(name))

        ps = ctx.enter_context(nc.psum_tensor("ps", [P, 8, 512], F32))

        h = sb("h", [P, DK, TOKENS])
        cst = sb("cst", [P, CONST.width])
        ident, mean_w, ones = CONST.of(cst, "ident"), CONST.of(cst, "mean"), CONST.of(cst, "ones")
        before = CONST.of(cst, "before")[0:W2]
        headmask, prio = CONST.of(cst, "headmask"), CONST.of(cst, "prio")
        region0, row_no = CONST.of(cst, "region0"), CONST.of(cst, "row_no")
        eps_t = sb("eps_t", [P, 1])
        zero_t = sb("zero_t", [P, 1])

        arena = sb("arena", [P, EXPERTS * EW])
        used = [0]

        def carve(*shape, rows=P, dt=F32):
            n = int(np.prod(shape))
            flat = arena[0:rows, used[0]:used[0] + n]
            used[0] += n
            assert used[0] <= EXPERTS * EW
            flat = flat if dt == F32 else flat.bitcast(dt)
            names = "abcd"[:len(shape)]
            return flat.rearrange(f"p ({' '.join(names)}) -> p {' '.join(names)}",
                                  **{k: w for k, w in zip(names[1:], shape[1:])})

        KT = carve(DK, N)
        Km = [carve(DK, HG, W2) for b in range(2)]
        Sb = [carve(HEADS, T) for b in range(2)]
        Sc = Sb
        PTs = [carve(HP, 2, T) for b in range(2)]
        OTs = carve(DK, N)
        QT = carve(DK, NPAD)
        On = [carve(D) for b in range(2)]
        both = used[0]
        emb_w = carve(PK, D)
        emb_a = carve(D, rows=ADDED)
        one_s = carve(N, rows=ADDED)
        x_in = carve(2, PK, N)
        qkv_w, out_w = [carve(DK, 3 * D)], [carve(DK, D)]
        used[0] = both
        qkv_w.append(carve(DK, 3 * D))
        out_w.append(carve(DK, D))
        gu1_at = used[0]
        gu1_i = carve(DK, 2 * I1, dt=I32)
        dn1_i = carve(6, D, dt=I32)
        used[0] = gu1_at
        gu1_w = carve(DK, 2 * I1)
        dn1_w = carve(6, D)

        qkv_b = sb("qkv_b", [P, 3 * DK])
        out_b = [sb(f"out_b{l}", [P, DK]) for l in range(2)]
        bias = [sb(f"bias{l}", [P, HEADS, T]) for l in range(2)]
        cen = sb("cen", [P, DK, N])
        squ = sb("squ", [P, DK, N])
        lnv = sb("lnv", [P, N])
        rsd = sb("rsd", [P, N])
        xn = [sb(f"xn{b}", [P, DK, N]) for b in range(2)]
        VT = sb("VT", [P, DK, GI, 2, PITCH])
        prs = sb("prs", [P, PAIRS * 2 * XW])
        Pr = [prs[:, b * HEADS * PITCH:(b + 1) * HEADS * PITCH].rearrange("p (h k) -> p h k", k=PITCH)
              for b in range(2)]
        Vb = [sb(f"Vb{b}", [P, 2, HP, 2 * HD]) for b in range(2)]
        mx = [sb(f"mx{b}", [P, HEADS]) for b in range(2)]
        sm = [sb(f"sm{b}", [P, HEADS]) for b in range(2)]
        rs = [sb(f"rs{b}", [P, HEADS]) for b in range(2)]

        shared = sb("shared", [P, EW])
        gu0_w = shared[:, 0:DK * 2 * I0].rearrange("p (c n) -> p c n", c=DK)
        dn0_w = shared[:, DK * 2 * I0:EW].rearrange("p (j n) -> p j n", j=6)
        xTs = [shared[:, b * D:(b + 1) * D] for b in range(2)]
        Sgt = shared[:, 2 * D:2 * D + I0]
        Hdt = [shared[:, 2 * D + (1 + b) * I0:2 * D + (2 + b) * I0] for b in range(2)]
        HTs = shared[:, 2 * D + 3 * I0:2 * D + 3 * I0 + 6 * P].rearrange("p (j m) -> p j m", j=6)
        assert 2 * D + 3 * I0 + 6 * P <= EW
        xt = [sb(f"xt{b}", [P, XW]) for b in range(2)]
        yt = [sb(f"yt{b}", [P, D]) for b in range(2)]
        yg = [HTs.rearrange("p j m -> p (j m)")[0:W2, 0:2 * D].rearrange("p (k d) -> p k d", k=2),
              Hdt[0][0:W2, 0:2 * D].rearrange("p (k d) -> p k d", k=2)]

        Sg = [sb(f"Sg{b}", [P, N]) for b in range(2)]
        Hd = [sb(f"Hd{b}", [P, N]) for b in range(2)]
        r_w = sb("r_w", [P, DK, EXPERTS])
        r_b = sb("r_b", [P, PAIRS * EXPERTS])
        rt = sb("rt", [P, 11, PAIRS * EXPERTS])
        place = sb("place", [P, EXPERTS])
        rows_x = prs[0:W2].rearrange("p (a k d) -> p a k d", a=PAIRS, k=2)
        slot = [sb(f"slot{b}", [W2, 2, PAIRS], U32) for b in range(2)]
        slot_f = sb("slot_f", [W2, 2, PAIRS])
        slots_f = sb("slots_f", [W2, 2, GROUPS, PAIRS])
        slots = sb("slots", [W2, 2, GROUPS, PAIRS], U32)
        slot_g = [sb(f"slot_g{b}", [W2, 2, PAIRS], U32) for b in range(2)]
        pad_f = sb("pad_f", [P, EXPERTS])
        pad_i = sb("pad_i", [P, EXPERTS], U32)
        zero_x = sb("zero_x", [P, XW])
        table = sb("table", [1, 2, TILES], I32)

        s_cst, s_embw, s_out = sem("s_cst"), sem("s_embw"), sem("s_out")
        s_x = [sem("s_x0"), sem("s_x1")]
        s_attw, s_bias, s_rw, s_w1 = sem("s_attw"), sem("s_bias"), sem("s_rw"), sem("s_w1")
        s_shw, s_exw, s_attw1 = sem("s_shw"), sem("s_exw"), sem("s_attw1")
        s_scat, s_junk, s_pad, s_table, s_t = sem("s_scat"), sem("s_junk"), sem("s_pad"), sem("s_table"), sem("s_t")
        s_xt, s_yt = [sem("s_xt0"), sem("s_xt1")], sem("s_yt")
        s_turn = sem("s_turn")
        s_gat = [sem("s_gat0"), sem("s_gat1")]
        s_zero, s_tab, s_deq = sem("s_zero"), sem("s_tab"), sem("s_deq")
        emb_mm, emb_cp = sem("emb_mm"), sem("emb_cp")

        def group(g, w=N):
            return bass.ds(g * N, w)

        def counted(names, prefix):
            return namedtuple("Semaphores", names)(*[sem(prefix + n) for n in names.split()])

        A = [counted("mean_mm var_mm proj_mm S_mm PT_mm V_mm O_mm OT_mm out_mm "
                     "cen squ lnv rsd xn proj km sb mx sc ex sum rs PTs Vb On OTs res", f"a{l}_") for l in range(2)]
        F = [counted("mean_mm var_mm lg_mm cnt_mm rowA_mm rowB_mm gu_mm dn_mm cen squ lnv rsd xn lg rowA rowB "
                     "sg hd y r r_ex", f"f{l}_") for l in range(2)]
        E = counted("xt_mm gu_mm ht_mm y_mm xt sg hd ht y stored", "e_")
        C = counted("mm slots slot h", "c_")

        block = ctx.enter_context(nc.Block())
        LOOPED = (GROUPS - 2) // 2

        def over_tiles(eng, step):
            with eng.Fori(0, (TILES - 3) // 2) as i:
                for k in (1, 2):
                    step(2 * i + k, k % 2, False)
            for t in range(TILES - 2, TILES):
                step(t, t % 2, t == TILES - 1)

        def over_groups(eng, step):
            with eng.Fori(0, LOOPED) as i:
                for b in range(2):
                    step(2 * i + b, b, False)
            for g in range(2 * LOOPED, GROUPS):
                step(g, g % 2, g == GROUPS - 1)

        def over_body(eng, step):
            step(0, 0, FIRST)
            with eng.Fori(0, (GROUPS - 2) // 2) as i:
                for k in (1, 2):
                    step(2 * i + k, k % 2, BODY)
            step(GROUPS - 1, 1, LAST)

        @block.sync
        def _(sp):
            sp.dma_start(emb_w, embW).then_inc(s_embw, 16)
            sp.dma_start(emb_a, embAdd).then_inc(s_embw, 16)
            sp.dma_start(one_s, onehot).then_inc(s_embw, 16)
            with sp.Fori(0, GROUPS // 2) as i:
                for b in range(2):
                    g = 2 * i + b
                    sp.wait_ge(emb_mm, g + 1)
                    sp.dma_start(x_in[:, b], xT[bass.ds(g, 1)].rearrange("a p k n -> (a p) k n")).then_inc(s_x[b], 16)
            sp.wait_ge(s_zero, 1)
            for k in range(SPARE):
                r = EXPERTS * REGION + k * P
                sp.dma_start(xs[r:r + P, :], zero_x[:]).then_inc(s_junk, 16)
            sp.wait_ge(A[0].res, FREE + 2 * GROUPS)
            for e in range(EXPERTS):
                sp.dma_start(arena[:, e * EW:(e + 1) * EW], ew[e]).then_inc(s_exw, 16)

            sp.wait_ge(s_scat, 128 * GROUPS)
            sp.wait_ge(s_pad, 16 * EXPERTS)
            sp.wait_ge(s_junk, 16 * SPARE)
            sp.wait_ge(s_table, 1)

            def load(t, b):
                row = sp.value_load(table[0:1, 1, bass.ds(t, 1)], min_val=0, max_val=ROWS - P)
                sp.dma_start(xt[b][:], xs[bass.ds(row, P), :]).then_inc(s_xt[b], 16)

            load(0, 0)
            load(1, 1)
            with sp.Fori(0, (TILES - 3) // 2) as i:
                for b in range(2):
                    sp.wait_ge(E.hd, FREE + 4 * i + 2 * b + 2)
                    load(2 * i + b + 2, b)
            sp.wait_ge(E.hd, FREE + 2 * TILES - 4)
            load(TILES - 1, 0)

            sp.wait_ge(E.y_mm, TILES)
            sp.dma_start(qkv_w[1], qkv1).then_inc(s_attw1, 16)
            sp.dma_start(out_w[1], wo1).then_inc(s_attw1, 16)
            sp.dma_start(gu1_i, gu1).then_inc(s_w1, 16)
            sp.dma_start(dn1_i, dn1).then_inc(s_w1, 16)
            sp.wait_ge(F[1].y, FREE + 2 * GROUPS)
            sp.dma_start(out, h[:]).then_inc(s_out, 16)
            sp.wait_ge(s_out, 16)

        @block.gpsimd
        def _(pool):
            def km(a, l, n, p, b):
                pool.wait_ge(a.S_mm, n + 1)
                for c in range(DK):
                    src = KT[:, c, p * W2:(p + 1) * W2].unsqueeze(1).to_broadcast([P, HG, W2])
                    ins = pool.tensor_tensor(Km[p % 2][:, c], src, headmask.unsqueeze(2).to_broadcast([P, HG, W2]),
                                             ALU.mult)
                ins.then_inc(a.km, 1)

            def norm(s, g, b):
                pool.wait_ge(s.rsd, FREE + g + 1)
                pool.tensor_tensor(xn[b][:], cen[:], rsd[:].unsqueeze(1).to_broadcast([P, DK, N]),
                                   ALU.mult).then_inc(s.xn, 1)

            def attention(l):
                a = A[l]
                pool.sem_inc(a.xn, FREE)
                pool.sem_inc(a.km, FREE)
                norm(a, 0, 0)
                pool.wait_ge(a.proj, FREE + 4)
                km(a, l, 0, 0, 0)
                km(a, l, 1, 1, 0)

                def step(g, b, X):
                    km(a, l, 4 * g + 2, 2, b)
                    km(a, l, 4 * g + 3, 3, b)
                    if X is not LAST:
                        norm(a, g + 1, 1 - b)
                        pool.wait_ge(a.proj, FREE + 6 * g + 10)
                        km(a, l, 4 * g + 4, 0, 1 - b)
                        km(a, l, 4 * g + 5, 1, 1 - b)
                over_body(pool, step)

            def scatter(s, g, b):
                pool.wait_ge(s.r, RCHAIN * (g + 1))
                pool.wait_ge(s.rowA, FREE + g + 1)
                pool.wait_ge(s.rowB, FREE + g + 1)
                pool.sem_inc(s_turn, 1)
                for p in range(PAIRS):
                    for k in range(2):
                        pool.indirect_dma_start(xs, bass.IndirectOffsetOnAxis(slot[b][:, k, p:p + 1], 0),
                                                rows_x[:, p, k, :], None).then_inc(s_scat, 16)

            def ffn(l):
                s = F[l]
                pool.sem_inc(s.xn, FREE)
                norm(s, 0, 0)

                def step(g, b, last):
                    if l == 0:
                        scatter(s, g, b)
                    if not last:
                        norm(s, g + 1, 1 - b)
                over_groups(pool, step)
                if l == 0:
                    pool.wait_ge(s_t, 2)
                    for e in range(EXPERTS):
                        pool.indirect_dma_start(xs, bass.IndirectOffsetOnAxis(pad_i[:, e:e + 1], 0),
                                                zero_x[:], None).then_inc(s_pad, 16)

            def stores():
                pool.sem_inc(E.stored, FREE)

                def store(t, b):
                    pool.wait_ge(E.y, FREE + t + 1)
                    pool.dma_start(ys[bass.ds(t * P, P), :], yt[b][:]).then_inc(s_yt, 16)
                    pool.wait_ge(s_yt, 16 * t + 16)
                    pool.sem_inc(E.stored, 1)
                with pool.Fori(0, TILES // 2) as i:
                    for b in range(2):
                        store(2 * i + b, b)
                store(TILES - 1, 0)

            def gathers():
                pool.sem_inc(C.slot, FREE)
                pool.wait_ge(C.slots, 1)
                with pool.Fori(0, GROUPS // 2) as i:
                    for b in range(2):
                        g = 2 * i + b
                        pool.tensor_copy(slot_g[b][:], slots[:, :, bass.ds(g, 1), :].rearrange("p k g a -> p k (g a)"))\
                            .then_inc(C.slot, 1)
                        pool.wait_ge(C.slot, FREE + g + 1)
                        for p in range(PAIRS):
                            pool.wait_ge(C.mm, 4 * g + p + 1)
                            pool.sem_inc(s_turn, 1)
                            for k in range(2):
                                pool.indirect_dma_start(yg[p % 2][:, k], None, ys,
                                                        bass.IndirectOffsetOnAxis(slot_g[b][:, k, p:p + 1], 0))\
                                    .then_inc(s_gat[p % 2], 16)

            pool.memset(zero_x[:], 0.0).then_inc(s_zero, 1)
            pool.memset(eps_t[:], EPS).then_inc(s_zero, 1)
            pool.memset(zero_t[:], 0.0).then_inc(s_zero, 1)
            pool.memset(QT[:, :, N:], 0.0).then_inc(s_zero, 1)
            pool.memset(VT[:], 0.0).then_inc(s_zero, 1)
            for b in range(2):
                pool.memset(Pr[b], 0.0).then_inc(s_zero, 1)
                pool.memset(Vb[b][:], 0.0).then_inc(s_zero, 1)
                pool.memset(On[b], 0.0).then_inc(s_zero, 1)
            pool.memset(bias[0][:], 0.0).then_inc(s_zero, 1)
            pool.memset(bias[1][:], 0.0).then_inc(s_zero, 1)
            pool.wait_ge(s_bias, 32)
            for l in range(2):
                for q in (0, PITCH):
                    tab = bias[l][q:q + T]
                    pool.affine_select(out=tab, in_=tab, compare_op=ALU.is_ge, fill=-BIG, base=0,
                                       pattern=[[0, HEADS], [-1, T]], channel_multiplier=1).then_inc(s_tab, 1)
            pool.wait_ge(s_cst, 16)
            attention(0)
            ffn(0)
            stores()
            gathers()
            pool.memset(prs[:], 0.0)
            pool.wait_ge(s_w1, 32)
            pool.tensor_scalar(gu1_w, gu1_i, SCALE1, None, ALU.mult).then_inc(s_deq, 1)
            pool.tensor_scalar(dn1_w, dn1_i, SCALE1, None, ALU.mult).then_inc(s_deq, 1)
            attention(1)
            ffn(1)

        @block.scalar
        def _(act):
            act.dma_start(cst[:], consts).then_inc(s_cst, 16)
            act.dma_start(qkv_w[0], qkv0).then_inc(s_attw, 16)
            act.dma_start(out_w[0], wo0).then_inc(s_attw, 16)
            for l, ob in enumerate((wob0, wob1)):
                act.dma_start(out_b[l][:], ob).then_inc(s_attw, 16)
            act.dma_start(qkv_b[:], qkvb0).then_inc(s_attw, 16)
            act.dma_start(r_w[:], rT).then_inc(s_rw, 16)
            act.dma_start(r_b[:], rb).then_inc(s_rw, 16)
            act.dma_start(gu0_w, gu0).then_inc(s_shw, 16)
            act.dma_start(dn0_w, dn0).then_inc(s_shw, 16)
            act.wait_ge(s_zero, 13)
            for q in (0, PITCH):
                act.dma_start(bias[0][q:q + T], bias0).then_inc(s_bias, 16)

            act.sem_inc(emb_cp, FREE)
            with act.Fori(0, GROUPS // 2) as i:
                for b in range(2):
                    g = 2 * i + b
                    act.wait_ge(emb_mm, FREE + g + 1)
                    act.activation(h[:, :, group(g)], ps[:, 2 * b:2 * b + 2, 0:N], ACT.Copy).then_inc(emb_cp, 1)

            def squares(s, g):
                act.wait_ge(s.cen, FREE + g + 1)
                act.activation(squ[:], cen[:], ACT.Square).then_inc(s.squ, 1)

            def deviation(s, g, bk):
                act.wait_ge(s.var_mm, g + 1)
                act.activation(lnv[:], ps[:, bk, 0:N], ACT.Ln, bias=eps_t[:]).then_inc(s.lnv, 1)
                act.wait_ge(s.lnv, FREE + g + 1)
                act.activation(rsd[:], lnv[:], ACT.Exp, bias=zero_t[:], scale=-0.5).then_inc(s.rsd, 1)

            def attention(l):
                a = A[l]
                act.preload_act_table_set("natural_log_exp_and_others")
                for buf_free in (a.squ, a.lnv, a.rsd, a.proj, a.ex, a.PTs, a.Vb, a.OTs):
                    act.sem_inc(buf_free, FREE)

                def project(g, b, k, bk):
                    act.wait_ge(a.proj_mm, 6 * g + k + 1)
                    if k < 2 * DK:
                        dst, src = (QT, KT)[k // DK][:, k % DK, 0:N], ps[:, bk, 0:N]
                    else:
                        dst = VT[:, k % DK, :, :, 0:T]
                        src = ps[:, bk, 0:N].rearrange("p (i t) -> p i t", t=T).unsqueeze(2).to_broadcast([P, GI, 2, T])
                    act.activation(dst, src, ACT.Identity,
                                   bias=qkv_b[:, k:k + 1] if l == 0 else zero_t[:]).then_inc(a.proj, 1)

                def exps(n, p):
                    act.wait_ge(a.sc, FREE + n + 1)
                    act.wait_ge(a.PT_mm, n + 1)
                    act.wait_ge(a.sum, n + 1)
                    act.activation(Pr[p % 2][:, :, 0:T], Sc[p % 2], ACT.Exp).then_inc(a.ex, 1)

                def probs_t(n, p):
                    act.wait_ge(a.PT_mm, FREE + n + 1)
                    act.wait_ge(a.O_mm, n + 1)
                    src = ps[:, 4:6, :].rearrange("p b (h i q) -> p (b h) i q", h=HP // 2, i=2)[:, :, :, 0:T]
                    act.activation(PTs[p % 2], src, ACT.Copy).then_inc(a.PTs, 1)

                def out_t(n, p, bk):
                    act.wait_ge(a.OT_mm, FREE + n + 1)
                    src = ps[:, bk, 0:DK * P].rearrange("p (c i q) -> p c i q", c=DK, i=2)[:, :, :, 0:T]
                    dst = OTs[:, :, p * W2:(p + 1) * W2].rearrange("p c (i q) -> p c i q", i=2)
                    act.activation(dst, src, ACT.Copy).then_inc(a.OTs, 1)

                def values(n, p, bk):
                    act.wait_ge(a.V_mm, n + 1)
                    act.wait_ge(a.O_mm, n + 1)
                    for half in range(2):
                        rows = slice(half * PITCH, half * PITCH + PITCH)
                        cols = slice(half * HD, half * HD + HD)
                        src = ps[rows, bk, :].rearrange("p (r w) -> p r w", w=2 * HD)[:, :, cols]
                        dst = Vb[p % 2][rows].rearrange("p i h w -> p (i h) w")[:, :, cols]
                        ins = act.activation(dst, src, ACT.Copy)
                    ins.then_inc(a.Vb, 1)

                squares(a, 0)
                deviation(a, 0, 7)
                for k in range(6):
                    project(0, 0, k, 6 + k % 2)
                values(0, 0, 7)
                exps(0, 0)

                def step(g, b, X):
                    n = 4 * g
                    values(n + 1, 1, X.bank("V1"))
                    probs_t(n, 0)
                    exps(n + 1, 1)
                    if X is not FIRST:
                        out_t(n - 1, 3, X.bank("OT3p"))
                    if X is not LAST:
                        squares(a, g + 1)
                    values(n + 2, 2, X.bank("V2"))
                    exps(n + 2, 2)
                    probs_t(n + 1, 1)
                    if X is not LAST:
                        deviation(a, g + 1, X.bank("var"))
                    out_t(n, 0, X.bank("OT0"))
                    values(n + 3, 3, X.bank("V3"))
                    probs_t(n + 2, 2)
                    exps(n + 3, 3)
                    out_t(n + 1, 1, X.bank("OT1"))
                    if X is not LAST:
                        for k in range(4):
                            project(g + 1, 1 - b, k, X.bank(f"proj{k}"))
                    probs_t(n + 3, 3)
                    if X is not LAST:
                        for k in (4, 5):
                            project(g + 1, 1 - b, k, X.bank(f"proj{k}"))
                    out_t(n + 2, 2, X.bank("OT2"))
                    if X is not LAST:
                        values(n + 4, 0, X.bank("V0n"))
                        exps(n + 4, 0)
                over_body(act, step)
                out_t(4 * GROUPS - 1, 3, LAST.bank("OT3"))

            def silus(s, g, rows):
                for j, r in enumerate(rows):
                    act.wait_ge(s.gu_mm, len(rows) * g + j + 1)
                    act.wait_ge(s.hd, len(rows) * g + j + 1)
                    act.activation(Sg[j % 2][0:r], ps[0:r, 2 * (j % 2), 0:N], ACT.Silu).then_inc(s.sg, 1)
                    yield j

            def ffn(l):
                s = F[l]
                for buf_free in (s.squ, s.lnv, s.rsd, s.rowA, s.rowB):
                    act.sem_inc(buf_free, FREE)

                def r_exp(g):
                    if l == 0:
                        act.wait_ge(s.r, RCHAIN * g + 10)
                        act.activation(rt[0:W2, 9, 0:PAIRS], rt[0:W2, 8, 0:PAIRS], ACT.Exp).then_inc(s.r_ex, 1)

                def rows(g, half, mm_done, done):
                    if l == 0:
                        act.wait_ge(mm_done, g + 1)
                        src = ps[0:W2, 7, :].rearrange("p (a d) -> p a d", a=2).unsqueeze(2).to_broadcast([W2, 2, 2, D])
                        act.activation(rows_x[:, 2 * half:2 * half + 2, :, 0:D], src, ACT.Copy).then_inc(done, 1)

                squares(s, 0)
                deviation(s, 0, 7)
                rows(0, 0, s.rowA_mm, s.rowA)
                r_exp(0)

                def step(g, b, last):
                    for j in silus(s, g, hidden_chunks((I0, I1)[l])):
                        if j == 0:
                            rows(g, 1, s.rowB_mm, s.rowB)
                        if j == 2 and not last:
                            squares(s, g + 1)
                        if j == 4 and not last:
                            act.preload_act_table_set("natural_log_exp_and_others")
                            deviation(s, g + 1, 7)
                    if not last:
                        if l == 0:
                            act.wait_ge(s_scat, 128 * (g + 1))
                        rows(g + 1, 0, s.rowA_mm, s.rowA)
                        r_exp(g + 1)
                over_groups(act, step)

            def routed():
                s = E
                for buf_free in (s.ht,):
                    act.sem_inc(buf_free, FREE)

                def gate(t, half):
                    act.wait_ge(s.gu_mm, 2 * t + half + 1)
                    act.activation(Sgt[:, half * IH:(half + 1) * IH], ps[:, half, 0:IH], ACT.Silu).then_inc(s.sg, 1)

                def hidden_t(t):
                    act.wait_ge(s.ht_mm, t + 1)
                    act.activation(HTs[:, 0:5], ps[:, 4:6, :].rearrange("p b (j m) -> p (b j) m", m=P)[:, 0:5],
                                   ACT.Copy)
                    act.activation(HTs[0:I0 - 5 * P, 5], ps[0:I0 - 5 * P, 5, P:2 * P], ACT.Copy).then_inc(s.ht, 1)

                def step(t, b, last):
                    gate(t, 0)
                    hidden_t(t - 1)
                    gate(t, 1)

                gate(0, 0)
                gate(0, 1)
                over_tiles(act, step)
                hidden_t(TILES - 1)

            attention(0)
            ffn(0)
            routed()
            attention(1)
            ffn(1)

        @block.vector
        def _(dve):
            def centre(s, g, bk):
                dve.wait_ge(s.mean_mm, g + 1)
                dve.tensor_tensor(cen[:], h[:, :, group(g)], ps[:, bk, 0:N].unsqueeze(1).to_broadcast([P, DK, N]),
                                  ALU.subtract).then_inc(s.cen, 1)

            def attention(l):
                a = A[l]
                for buf_free in (a.cen, a.sb, a.mx, a.sc, a.sum, a.rs, a.On, a.res):
                    dve.sem_inc(buf_free, FREE)

                def softmax_in(n, p):
                    b = p % 2
                    dve.wait_ge(a.S_mm, FREE + n + 1)
                    dve.wait_ge(a.ex, n + 1)
                    src = ps[:, 2 * b:2 * b + 2, :].rearrange("p b (h k) -> p (b h) k", k=PITCH)[:, :, 0:T]
                    dve.scalar_tensor_tensor(out=Sb[b], in0=src, scalar=HD ** -0.5, in1=bias[l][:],
                                             op0=ALU.mult, op1=ALU.add).then_inc(a.sb, 1)
                    dve.wait_ge(a.sb, FREE + n + 1)
                    dve.tensor_reduce(mx[b][:], Sb[b], AX_X, ALU.max).then_inc(a.mx, 1)
                    dve.wait_ge(a.mx, FREE + n + 1)
                    dve.tensor_tensor(Sc[b], Sb[b], mx[b][:].unsqueeze(2).to_broadcast([P, HEADS, T]),
                                      ALU.subtract).then_inc(a.sc, 1)

                def sums(n, p):
                    b = p % 2
                    dve.wait_ge(a.ex, FREE + n + 1)
                    dve.tensor_reduce(sm[b][:], Pr[b][:, :, 0:T], AX_X, ALU.add).then_inc(a.sum, 1)
                    dve.wait_ge(a.sum, FREE + n + 1)
                    dve.reciprocal(rs[b][:], sm[b][:]).then_inc(a.rs, 1)

                def normalise(n, p, bk):
                    b = p % 2
                    dve.wait_ge(a.O_mm, FREE + n + 1)
                    dve.wait_ge(a.rs, FREE + n + 1)
                    dve.wait_ge(a.OT_mm, n + 1)
                    for i in range(2):
                        r = slice(i * PITCH, i * PITCH + T)
                        ins = dve.tensor_tensor(On[b][r].rearrange("p (h d) -> p h d", d=HD),
                                                ps[r, bk, 0:D].rearrange("p (h d) -> p h d", d=HD),
                                                rs[b][r].unsqueeze(2).to_broadcast([T, HEADS, HD]), ALU.mult)
                    ins.then_inc(a.On, 1)

                def residual(g, m, bk):
                    dve.wait_ge(a.out_mm, 2 * g + m + 1)
                    hm = h[:, m, group(g)]
                    dve.scalar_tensor_tensor(out=hm, in0=ps[:, bk, 0:N], scalar=out_b[l][:, m:m + 1], in1=hm,
                                             op0=ALU.add, op1=ALU.add).then_inc(a.res, 1)

                centre(a, 0, 6)
                softmax_in(0, 0)

                def step(g, b, X):
                    n = 4 * g
                    if X is not FIRST:
                        normalise(n - 1, 3, X.bank("O3p"))
                    softmax_in(n + 1, 1)
                    if X is not LAST:
                        centre(a, g + 1, X.bank("mean"))
                    sums(n, 0)
                    normalise(n, 0, X.bank("O0"))
                    softmax_in(n + 2, 2)
                    if X is not FIRST:
                        residual(g - 1, 0, X.bank("out0p"))
                        residual(g - 1, 1, X.bank("out1p"))
                    sums(n + 1, 1)
                    normalise(n + 1, 1, X.bank("O1"))
                    softmax_in(n + 3, 3)
                    sums(n + 2, 2)
                    normalise(n + 2, 2, X.bank("O2"))
                    sums(n + 3, 3)
                    if X is not LAST:
                        softmax_in(n + 4, 0)
                over_body(dve, step)
                normalise(4 * GROUPS - 1, 3, LAST.bank("O3"))
                residual(GROUPS - 1, 0, LAST.bank("out0"))
                residual(GROUPS - 1, 1, LAST.bank("out1"))

            def gates(s, g, rows):
                for j, r in enumerate(rows):
                    n = len(rows) * g + j
                    dve.wait_ge(s.sg, n + 1)
                    dve.wait_ge(s.dn_mm, n + 1)
                    up = ps[0:P, 2 * (j % 2) + 1, 0:N] if r == P else ps[r:2 * r, 2 * (j % 2), 0:N]
                    dve.tensor_tensor(Hd[j % 2][0:r], Sg[j % 2][0:r], up, ALU.mult).then_inc(s.hd, 1)
                    yield j

            def ffn(l):
                s = F[l]
                for buf_free in (s.cen, s.hd, s.y, s.lg):
                    dve.sem_inc(buf_free, FREE)

                R = slice(0, W2)
                done = [0]

                def t(i):
                    return rt[R, i].rearrange("p (a e) -> p a e", e=EXPERTS)

                def c(i):
                    return rt[R, i, 0:PAIRS]

                def wide(i):
                    return c(i).unsqueeze(2).to_broadcast([W2, PAIRS, EXPERTS])

                def linker(base):
                    done[0] = 0

                    def link(ins):
                        ins.then_inc(s.r, 1)
                        done[0] += 1
                        dve.wait_ge(s.r, base + done[0])
                    return link

                def route(g, first=False):
                    link = linker(RCHAIN * g)
                    pr = prio[R].rearrange("p (a e) -> p a e", e=EXPERTS)
                    dve.wait_ge(s.lg_mm, g + 1)
                    dve.tensor_tensor(rt[R, 0], ps[R, 6, 0:PAIRS * EXPERTS], r_b[R], ALU.add).then_inc(s.lg, 1)
                    dve.wait_ge(s.lg, FREE + g + 1)
                    link(dve.tensor_reduce(c(1), t(0), AX_X, ALU.max))
                    link(dve.tensor_tensor(t(2), t(0), wide(1), ALU.is_equal))
                    link(dve.tensor_tensor(t(2), t(2), pr, ALU.mult))
                    link(dve.tensor_reduce(c(3), t(2), AX_X, ALU.max))
                    link(dve.tensor_tensor(t(4), t(2), wide(3), ALU.is_equal))
                    link(dve.scalar_tensor_tensor(out=t(5), in0=t(4), scalar=-BIG, in1=t(0), op0=ALU.mult, op1=ALU.add))
                    link(dve.tensor_reduce(c(6), t(5), AX_X, ALU.max))
                    link(dve.tensor_tensor(t(7), t(5), wide(6), ALU.is_equal))
                    link(dve.tensor_tensor(t(7), t(7), pr, ALU.mult))
                    link(dve.tensor_tensor(c(8), c(6), c(1), ALU.subtract))
                    link(dve.tensor_reduce(c(3), t(7), AX_X, ALU.max))
                    link(dve.tensor_tensor(t(5), t(7), wide(3), ALU.is_equal))
                    link(dve.tensor_tensor(t(10), t(4), t(5), ALU.add))
                    dve.wait_ge(s.r_ex, g + 1)
                    link(dve.tensor_scalar(c(1), c(9), 1.0, None, ALU.add))
                    link(dve.reciprocal(c(6), c(1)))
                    link(dve.tensor_tensor(c(1), c(6), c(9), ALU.mult))
                    if not first:
                        dve.wait_ge(s_scat, 128 * g)
                    link(dve.tensor_copy(rows_x[:, :, 0, D], c(6)))
                    link(dve.tensor_copy(rows_x[:, :, 1, D], c(1)))
                    assert done[0] == ROUTE

                def slots_of(g, b):
                    link = linker(RCHAIN * g + ROUTE)
                    dve.wait_ge(s.cnt_mm, g + 1)
                    link(dve.tensor_tensor(t(7), ps[R, 6, 0:PAIRS * EXPERTS].rearrange("p (a e) -> p a e", e=EXPERTS),
                                           place[R].unsqueeze(1).to_broadcast([W2, PAIRS, EXPERTS]), ALU.add))
                    for k in range(2):
                        link(dve.tensor_tensor(t(2), t(7), t(4 + k), ALU.mult))
                        link(dve.tensor_reduce(slot_f[:, k], t(2), AX_X, ALU.add))
                    link(dve.tensor_copy(slot[b][:], slot_f[:]))
                    link(dve.tensor_copy(slots_f[:, :, bass.ds(g, 1), :].rearrange("p k g a -> p k (g a)"), slot_f[:]))
                    link(dve.tensor_tensor(place[:], place[:], ps[:, 6, 32:32 + EXPERTS], ALU.add))
                    assert done[0] == RCHAIN - ROUTE

                def table_of_tiles():
                    count = [0]

                    def link(ins):
                        ins.then_inc(s_t, 1)
                        count[0] += 1
                        dve.wait_ge(s_t, count[0])

                    link(dve.tensor_scalar(pad_f[:], place[:], row_no, None, ALU.add))
                    link(dve.tensor_copy(pad_i[:], pad_f[:]))
                    at_a, at_b = cen[:].rearrange("p c n -> p (c n)"), squ[:].rearrange("p c n -> p (c n)")

                    def cut(src, at, *shape):
                        v = src[:, at:at + int(np.prod(shape))]
                        return v if len(shape) == 1 else v.rearrange("p (a b) -> p a b", b=shape[1])

                    def over(v, *shape):
                        return v.unsqueeze(1).to_broadcast([v.shape[0], *shape])

                    def under(v, *shape):
                        return v.unsqueeze(2).to_broadcast([v.shape[0], *shape])

                    count_e, tiles_e, last_e, move_e = [rt[:, i, 0:EXPERTS] for i in range(4)]
                    used, tri = cut(at_a, 0, EXPERTS, KT_MAX), cut(at_a, 136, EXPERTS, EXPERTS)
                    past, gone = cut(at_a, 192, TILES, EXPERTS), cut(at_b, 0, TILES, EXPERTS)
                    expert_t, first_t, row_t, w_t = [cut(at_b, 304 + 48 * i, TILES) for i in range(4)]
                    k128, tri_c = CONST.of(cst, "k128"), CONST.of(cst, "tri").rearrange("p (a b) -> p a b", b=EXPERTS)
                    tile_no, tile_row = CONST.of(cst, "tile_no"), CONST.of(cst, "tile_row")
                    link(dve.tensor_tensor(count_e, place[:], region0, ALU.subtract))
                    link(dve.tensor_tensor(used, over(k128, EXPERTS, KT_MAX), under(count_e, EXPERTS, KT_MAX), ALU.is_lt))
                    link(dve.tensor_reduce(tiles_e, used, AX_X, ALU.add))
                    link(dve.tensor_tensor(tri, tri_c, over(tiles_e, EXPERTS, EXPERTS), ALU.mult))
                    link(dve.tensor_reduce(last_e, tri, AX_X, ALU.add))
                    link(dve.tensor_tensor(past, under(tile_no, TILES, EXPERTS), over(last_e, TILES, EXPERTS), ALU.is_ge))
                    link(dve.tensor_reduce(expert_t, past, AX_X, ALU.add))
                    link(dve.tensor_tensor(gone, past, over(tiles_e, TILES, EXPERTS), ALU.mult))
                    link(dve.tensor_reduce(first_t, gone, AX_X, ALU.add))
                    link(dve.scalar_tensor_tensor(out=row_t, in0=expert_t, scalar=float(REGION), in1=tile_row,
                                                  op0=ALU.mult, op1=ALU.add))
                    link(dve.scalar_tensor_tensor(out=row_t, in0=first_t, scalar=-float(P), in1=row_t,
                                                  op0=ALU.mult, op1=ALU.add))
                    link(dve.tensor_scalar(w_t, expert_t, float(EXPERTS - 1), float(EW), ALU.min, ALU.mult))
                    link(dve.tensor_copy(table[:, 0], w_t[0:1]))
                    dve.tensor_copy(table[:, 1], row_t[0:1]).then_inc(s_table, 1)
                    at = slots_f[:].rearrange("p k g a -> p (k g a)")
                    n = 2 * GROUPS * PAIRS
                    past, move = cut(at_a, 0, n, EXPERTS - 1), move_e[:, 0:EXPERTS - 1]
                    link(dve.tensor_scalar(move, tiles_e[:, 0:EXPERTS - 1], float(P), -float(REGION), ALU.mult, ALU.add))
                    link(dve.tensor_tensor(past[R], under(at, n, EXPERTS - 1), over(region0[R, 1:EXPERTS], n, EXPERTS - 1),
                                           ALU.is_ge))
                    link(dve.tensor_tensor(past[R], past[R], over(move[R], n, EXPERTS - 1), ALU.mult))
                    link(dve.tensor_reduce(at_b[R, 0:n], past[R], AX_X, ALU.add))
                    dve.tensor_tensor(slots[:].rearrange("p k g a -> p (k g a)"), at_b[R, 0:n], at, ALU.add)\
                        .then_inc(C.slots, 1)

                def add_y(g):
                    dve.wait_ge(s.dn_mm, FREE + 6 * g + 6)
                    for m in range(DK):
                        hm = h[:, m, group(g)]
                        dve.tensor_tensor(hm, hm, ps[:, 4 + m, 0:N], ALU.add).then_inc(s.y, 1)

                centre(s, 0, 6)
                if l == 0:
                    route(0, True)

                def step(g, b, last):
                    for j in gates(s, g, hidden_chunks((I0, I1)[l])):
                        if j == 0 and l == 0:
                            slots_of(g, b)
                        if j == 2 and not last:
                            centre(s, g + 1, 6)
                    add_y(g)
                    if l == 0 and not last:
                        route(g + 1)
                over_groups(dve, step)
                if l == 0:
                    table_of_tiles()

            def routed():
                s = E
                for buf_free in (s.xt, s.hd, s.y):
                    dve.sem_inc(buf_free, FREE)

                def tile_in(t, b):
                    dve.wait_ge(s.xt_mm, t + 1)
                    dve.tensor_copy(xTs[b], ps[:, 6, 0:D]).then_inc(s.xt, 1)

                def gate(t, b, half):
                    dve.wait_ge(s.sg, 2 * t + half + 1)
                    cols = slice(half * IH, (half + 1) * IH)
                    dve.scalar_tensor_tensor(out=Hdt[b][:, cols], in0=Sgt[:, cols], scalar=xt[b][:, D:XW],
                                             in1=ps[:, 2 + half, 0:IH], op0=ALU.mult, op1=ALU.mult).then_inc(s.hd, 1)

                def tile_out(t, b):
                    dve.wait_ge(s.y_mm, t + 1)
                    dve.wait_ge(s.stored, t + 1)
                    dve.tensor_copy(yt[b][:], ps[:, 7, 0:D]).then_inc(s.y, 1)

                tile_in(0, 0)
                gate(0, 0, 0)
                gate(0, 0, 1)
                tile_in(1, 1)
                with dve.Fori(0, (TILES - 3) // 2) as i:
                    for k in (1, 2):
                        t, b = 2 * i + k, k % 2
                        gate(t, b, 0)
                        gate(t, b, 1)
                        tile_in(t + 1, 1 - b)
                        tile_out(t - 1, 1 - b)
                t = TILES - 2
                gate(t, 1, 0)
                gate(t, 1, 1)
                tile_in(t + 1, 0)
                tile_out(t - 1, 0)
                gate(t + 1, 0, 0)
                gate(t + 1, 0, 1)
                tile_out(t, 1)
                tile_out(t + 1, 0)

            def combine():
                dve.sem_inc(C.h, FREE)
                with dve.Fori(0, GROUPS // 2) as i:
                    for b in range(2):
                        g = 2 * i + b
                        dve.wait_ge(C.mm, FREE + 4 * g + 4)
                        hg = h[:, :, group(g)]
                        dve.tensor_tensor(hg, hg, ps[:, 2 * b:2 * b + 2, 0:N], ALU.add).then_inc(C.h, 1)

            dve.wait_ge(emb_cp, FREE + GROUPS)
            dve.wait_ge(s_tab, 4)
            attention(0)
            dve.wait_ge(s_rw, 32)
            dve.tensor_copy(place[:], region0)
            dve.wait_ge(A[0].res, FREE + 2 * GROUPS)
            ffn(0)
            routed()
            dve.wait_ge(F[0].y, FREE + 2 * GROUPS)
            combine()
            dve.wait_ge(C.h, FREE + GROUPS)
            attention(1)
            dve.wait_ge(A[1].res, FREE + 2 * GROUPS)
            ffn(1)

        @block.tensor
        def _(pe):
            def mm(out_, lhsT, rhs, start=True, stop=True):
                return pe.matmul(out_, lhsT, rhs, start=start, stop=stop)

            pe.sem_inc(emb_mm, FREE)
            pe.wait_ge(s_embw, 48)
            with pe.Fori(0, GROUPS // 2) as i:
                for b in range(2):
                    g = 2 * i + b
                    pe.wait_ge(s_x[b], 16 * i + 16)
                    pe.wait_ge(emb_cp, g + 1)
                    for m in range(DK):
                        o = ps[:, 2 * b + m, 0:N]
                        cols = slice(m * P, m * P + P)
                        mm(o, emb_a[:, cols], one_s[:], True, False)
                        for k in range(PK):
                            ins = mm(o, emb_w[:, k, cols], x_in[:, b, k], False, k == PK - 1)
                    ins.then_inc(emb_mm, 1)

            def mean(s, g, bk):
                o = ps[:, bk, 0:N]
                for c in range(DK):
                    ins = mm(o, mean_w, h[:, c, group(g)], c == 0, c == DK - 1)
                ins.then_inc(s.mean_mm, 1)

            def variance(s, g, bk):
                pe.wait_ge(s.squ, FREE + g + 1)
                o = ps[:, bk, 0:N]
                for c in range(DK):
                    ins = mm(o, mean_w, squ[:, c], c == 0, c == DK - 1)
                ins.then_inc(s.var_mm, 1)

            def attention(l):
                a = A[l]
                for buf_free in (a.S_mm, a.PT_mm, a.O_mm, a.OT_mm):
                    pe.sem_inc(buf_free, FREE)

                def read_out(name, g):
                    kind, k, later = Turn.parts(name)
                    n = 4 * g + k + 4 * later
                    if kind == "V":
                        pe.wait_ge(a.Vb, FREE + n + 1)
                    elif kind == "O":
                        pe.wait_ge(a.On, FREE + n + 1)
                    elif kind == "OT":
                        pe.wait_ge(a.OTs, FREE + n + 1)
                    elif kind == "mean":
                        pe.wait_ge(a.cen, FREE + g + 2)
                    elif kind == "var":
                        pe.wait_ge(a.lnv, FREE + g + 2)
                    elif kind == "proj":
                        pe.wait_ge(a.proj, FREE + 6 * (g + 1) + k + 1)
                    elif kind == "out":
                        pe.wait_ge(a.res, FREE + 2 * (g + later) + k + 1)

                def project(g, b, k, bk):
                    pe.wait_ge(a.xn, FREE + g + 1)
                    for c in range(DK):
                        ins = mm(ps[:, bk, 0:N], qkv_w[l][:, c, k * P:(k + 1) * P], xn[b][:, c], c == 0, c == DK - 1)
                    ins.then_inc(a.proj_mm, 1)

                def scores(n, p, b):
                    pe.wait_ge(a.km, FREE + n + 1)
                    pe.wait_ge(a.sb, n + 1)
                    for c in range(DK):
                        for i in range(2):
                            o = ps[i * PITCH:(i + 1) * PITCH, 2 * (p % 2) + c, :].rearrange("p (h k) -> p h k", k=PITCH)
                            q0 = (2 * p + i) * T
                            ins = mm(o[:, :, 0:T], QT[:, c, q0:q0 + PITCH], Km[p % 2][:, c, :, i * T:(i + 1) * T])
                    ins.then_inc(a.S_mm, 1)

                def values(n, p, b, bk):
                    for i in range(2):
                        for c in range(DK):
                            src = VT[:, c, 2 * p + i].rearrange("p a k -> p (a k)")
                            ins = pe.transpose(ps[:, bk, i * D + c * P:i * D + (c + 1) * P], src, ident)
                    ins.then_inc(a.V_mm, 1)

                def probs_t(n, p):
                    pe.wait_ge(a.ex, FREE + n + 1)
                    pe.wait_ge(a.PTs, FREE + n)
                    for hp in range(HP):
                        ins = pe.transpose(ps[:, 4 + hp // 4, (hp % 4) * P:(hp % 4 + 1) * P],
                                           Pr[p % 2][:, 2 * hp:2 * hp + 2, :].rearrange("p a k -> p (a k)"), ident)
                    ins.then_inc(a.PT_mm, 1)

                def outputs(n, p, bk):
                    pe.wait_ge(a.PTs, FREE + n + 1)
                    pe.wait_ge(a.Vb, FREE + n + 1)
                    for i in range(2):
                        for hp in range(HP):
                            ins = mm(ps[i * PITCH:i * PITCH + T, bk, hp * 2 * HD:(hp + 1) * 2 * HD],
                                     PTs[p % 2][:, hp, i], Vb[p % 2][:, i, hp])
                    ins.then_inc(a.O_mm, 1)

                def outputs_t(n, p, bk):
                    pe.wait_ge(a.On, FREE + n + 1)
                    for c in range(DK):
                        ins = pe.transpose(ps[:, bk, c * P:(c + 1) * P], On[p % 2][:, c * P:(c + 1) * P], ident)
                    ins.then_inc(a.OT_mm, 1)

                def out_proj(g, m, bk):
                    pe.wait_ge(a.OTs, FREE + 4 * g + 4)
                    for c in range(DK):
                        ins = mm(ps[:, bk, 0:N], out_w[l][:, c, m * P:(m + 1) * P], OTs[:, c], c == 0, c == DK - 1)
                    ins.then_inc(a.out_mm, 1)

                mean(a, 0, 6)
                variance(a, 0, 7)
                for k in range(6):
                    if k == 0:
                        pe.wait_ge(a.cen, FREE + 1)
                    elif k == 1:
                        pe.wait_ge(a.lnv, FREE + 1)
                    else:
                        pe.wait_ge(a.proj, FREE + k - 1)
                    project(0, 0, k, 6 + k % 2)
                scores(0, 0, 0)
                pe.wait_ge(a.proj, FREE + 6)
                values(0, 0, 0, 7)

                def step(g, b, X):
                    n = 4 * g

                    def at(name, do, *args):
                        prev, back = X.before(name)
                        if prev is not None:
                            read_out(prev, g - back)
                        do(*args, X.bank(name))

                    scores(n + 1, 1, b)
                    if X is not FIRST:
                        at("O3p", outputs, n - 1, 3)
                    at("V1", values, n + 1, 1, b)
                    probs_t(n, 0)
                    if X is not LAST:
                        at("mean", mean, a, g + 1)
                    if X is not FIRST:
                        at("OT3p", outputs_t, n - 1, 3)
                    scores(n + 2, 2, b)
                    at("O0", outputs, n, 0)
                    at("V2", values, n + 2, 2, b)
                    if X is not FIRST:
                        at("out0p", out_proj, g - 1, 0)
                        at("out1p", out_proj, g - 1, 1)
                    probs_t(n + 1, 1)
                    if X is not LAST:
                        at("var", variance, a, g + 1)
                    at("OT0", outputs_t, n, 0)
                    scores(n + 3, 3, b)
                    at("O1", outputs, n + 1, 1)
                    at("V3", values, n + 3, 3, b)
                    probs_t(n + 2, 2)
                    at("OT1", outputs_t, n + 1, 1)
                    if X is not LAST:
                        for k in range(4):
                            at(f"proj{k}", project, g + 1, 1 - b, k)
                    at("O2", outputs, n + 2, 2)
                    probs_t(n + 3, 3)
                    if X is not LAST:
                        for k in (4, 5):
                            at(f"proj{k}", project, g + 1, 1 - b, k)
                    at("OT2", outputs_t, n + 2, 2)
                    if X is not LAST:
                        scores(n + 4, 0, 1 - b)
                        pe.wait_ge(a.proj, FREE + 6 * g + 12)
                        at("V0n", values, n + 4, 0, 1 - b)
                    else:
                        at("O3", outputs, n + 3, 3)
                        at("OT3", outputs_t, n + 3, 3)
                        at("out0", out_proj, g, 0)
                        at("out1", out_proj, g, 1)
                over_body(pe, step)

            def gate_up(s, g, j, rows, w, x):
                nj = len(rows)
                pe.wait_ge(s.hd, nj * g + j + 1)
                for half in range(2 if rows[j] == P else 1):
                    c0 = (2 * j + half) * P
                    for c in range(DK):
                        ins = mm(ps[:, 2 * (j % 2) + half, 0:N], w[:, c, c0:c0 + P], x(c), c == 0, c == DK - 1)
                ins.then_inc(s.gu_mm, 1)

            def down(s, g, j, rows, w):
                nj, r = len(rows), rows[j]
                pe.wait_ge(s.hd, FREE + nj * g + j + 1)
                if j == 0:
                    pe.wait_ge(s.y, FREE + 2 * g)
                for m in range(DK):
                    ins = pe.matmul(ps[:, 4 + m, 0:N], w[0:r, j, m * P:(m + 1) * P], Hd[j % 2][0:r],
                                    start=(j == 0), stop=(j == nj - 1))
                ins.then_inc(s.dn_mm, 1)

            def ffn(l, w_gu, w_dn):
                s = F[l]
                rows = hidden_chunks((I0, I1)[l])
                pe.sem_inc(s.dn_mm, FREE)

                def logits(g, b):
                    if l == 0:
                        pe.wait_ge(s.xn, FREE + g + 1)
                        pe.wait_ge(s.cen, FREE + g + 1)
                        for p in range(PAIRS):
                            for c in range(DK):
                                ins = mm(ps[0:W2, 6, p * EXPERTS:(p + 1) * EXPERTS], xn[b][:, c, p * W2:(p + 1) * W2],
                                         r_w[:, c], c == 0, c == DK - 1)
                        ins.then_inc(s.lg_mm, 1)

                def token_rows(g, b, half):
                    if l == 0:
                        for a in range(2):
                            for c in range(DK):
                                p = 2 * half + a
                                ins = pe.transpose(ps[0:W2, 7, a * D + c * P:a * D + (c + 1) * P],
                                                   xn[b][:, c, p * W2:(p + 1) * W2], ident)
                        ins.then_inc((s.rowA_mm, s.rowB_mm)[half], 1)

                def counts(g):
                    if l == 0:
                        pe.wait_ge(s.r, RCHAIN * g + 13)
                        n = PAIRS * EXPERTS
                        chosen = rt[0:W2, 10, 0:n]
                        mm(ps[0:W2, 6, 0:n], before, chosen, True, False)
                        for k in range(1, PAIRS):
                            mm(ps[0:W2, 6, k * EXPERTS:n], ones[0:W2, 0:W2], chosen[:, 0:n - k * EXPERTS],
                               False, k == PAIRS - 1)
                        for p in range(PAIRS):
                            ins = pe.matmul(ps[:, 6, 32:32 + EXPERTS], ones[0:W2], chosen[:, p * EXPERTS:(p + 1) * EXPERTS],
                                            start=False, stop=p == PAIRS - 1, skip_group_check=True)
                        ins.then_inc(s.cnt_mm, 1)

                mean(s, 0, 6)
                variance(s, 0, 7)
                logits(0, 0)
                if l == 0:
                    pe.wait_ge(s.lnv, FREE + 1)
                token_rows(0, 0, 0)

                def step(g, b, last):
                    x = lambda c: xn[b][:, c]
                    pe.wait_ge(s.xn, FREE + g + 1)
                    nj = len(rows)
                    for j in range(nj):
                        gate_up(s, g, j, rows, w_gu, x)
                        if j == 1 and l == 0:
                            pe.wait_ge(s.lg, FREE + g + 1)
                            counts(g)
                            pe.wait_ge(s.rowA, FREE + g + 1)
                            token_rows(g, b, 1)
                        if j == 2 and not last:
                            if l == 0:
                                pe.wait_ge(s.r, RCHAIN * (g + 1))
                            mean(s, g + 1, 6)
                        if j == 4 and not last:
                            if l == 0:
                                pe.wait_ge(s.rowB, FREE + g + 1)
                            variance(s, g + 1, 7)
                        if j:
                            down(s, g, j - 1, rows, w_dn)
                        if j == nj - 1 and not last:
                            logits(g + 1, 1 - b)
                            if l == 0:
                                pe.wait_ge(s.lnv, FREE + g + 2)
                            token_rows(g + 1, 1 - b, 0)
                    down(s, g, nj - 1, rows, w_dn)
                over_groups(pe, step)

            def routed():
                s = E

                def tile_in(t, b, turn):
                    pe.wait_ge(s_xt[b], 16 * turn + 16)
                    pe.wait_ge(s.xt, FREE + t)
                    for c in range(DK):
                        ins = pe.transpose(ps[:, 6, c * P:(c + 1) * P], xt[b][:, c * P:(c + 1) * P], ident)
                    ins.then_inc(s.xt_mm, 1)

                def gate_up_half(t, b, half, w):
                    pe.wait_ge(s.xt, FREE + t + 1)
                    pe.wait_ge(s.hd, FREE + 2 * t + half - 1)
                    for u in range(2):
                        for c in range(DK):
                            at = c * 2 * I0 + u * I0 + half * IH
                            ins = mm(ps[:, 2 * u + half, 0:IH], xTs[b][:, c * P:(c + 1) * P],
                                     arena[:, bass.ds(w + at, IH)], c == 0, c == DK - 1)
                    ins.then_inc(s.gu_mm, 1)

                def hidden_t(t, b):
                    pe.wait_ge(s.hd, FREE + 2 * t + 2)
                    pe.wait_ge(s.ht, FREE + t)
                    for j, r in enumerate(hidden_chunks(I0)):
                        ins = pe.transpose(ps[0:r, 4 + j // 4, (j % 4) * P:(j % 4 + 1) * P],
                                           Hdt[b][:, j * P:j * P + r], ident)
                    ins.then_inc(s.ht_mm, 1)

                def tile_out(t, w):
                    pe.wait_ge(s.ht, FREE + t + 1)
                    pe.wait_ge(s.y, FREE + t)
                    for j, r in enumerate(hidden_chunks(I0)):
                        ins = mm(ps[:, 7, 0:D], HTs[0:r, j], arena[0:r, bass.ds(w + DK * 2 * I0 + j * D, D)],
                                 j == 0, j == 5)
                    ins.then_inc(s.y_mm, 1)

                def weights(t):
                    return pe.value_load(table[0:1, 0, bass.ds(t, 1)], min_val=0, max_val=(EXPERTS - 1) * EW)

                def step(t, b, turn_next, last):
                    w = weights(t)
                    w_before = weights(t - 1)
                    gate_up_half(t, b, 0, w)
                    hidden_t(t - 1, 1 - b)
                    gate_up_half(t, b, 1, w)
                    if not last:
                        tile_in(t + 1, 1 - b, turn_next)
                    tile_out(t - 1, w_before)

                tile_in(0, 0, 0)
                w = weights(0)
                gate_up_half(0, 0, 0, w)
                gate_up_half(0, 0, 1, w)
                tile_in(1, 1, 0)
                with pe.Fori(0, (TILES - 3) // 2) as i:
                    step(2 * i + 1, 1, i + 1, False)
                    step(2 * i + 2, 0, i + 1, False)
                step(TILES - 2, 1, (TILES - 1) // 2, False)
                step(TILES - 1, 0, None, True)
                hidden_t(TILES - 1, 0)
                tile_out(TILES - 1, weights(TILES - 1))

            def combine():
                pe.sem_inc(C.mm, FREE)
                with pe.Fori(0, GROUPS // 2) as i:
                    for b in range(2):
                        g = 2 * i + b
                        pe.wait_ge(C.h, g + 1)
                        for p in range(PAIRS):
                            pe.wait_ge(s_gat[p % 2], 32 * (2 * g + p // 2 + 1))
                            for c in range(DK):
                                for k in range(2):
                                    ins = mm(ps[:, 2 * b + c, p * W2:(p + 1) * W2], yg[p % 2][:, k, c * P:(c + 1) * P],
                                             ident[0:W2, 0:W2], k == 0, k == 1)
                            ins.then_inc(C.mm, 1)

            pe.wait_ge(s_cst, 16)
            pe.wait_ge(s_attw, 16 * 5)
            pe.wait_ge(s_zero, 13)
            pe.wait_ge(emb_cp, FREE + GROUPS)
            attention(0)
            pe.wait_ge(A[0].res, FREE + 2 * GROUPS)
            pe.wait_ge(s_shw, 32)
            pe.wait_ge(s_rw, 32)
            ffn(0, gu0_w, dn0_w)
            pe.wait_ge(F[0].y, FREE + 2 * GROUPS)
            pe.wait_ge(F[0].rowB, FREE + GROUPS)
            pe.wait_ge(s_table, 1)
            pe.wait_ge(s_exw, 16 * EXPERTS)
            routed()
            pe.wait_ge(E.y, FREE + TILES)
            combine()
            pe.wait_ge(C.h, FREE + GROUPS)
            pe.wait_ge(s_attw1, 32)
            attention(1)
            pe.wait_ge(A[1].res, FREE + 2 * GROUPS)
            pe.wait_ge(s_deq, 2)
            ffn(1, gu1_w, dn1_w)


ROUTE = 18
RCHAIN = ROUTE + 8


class Packed:

    def __init__(self, **widths):
        self.at, self.width = {}, 0
        for name, w in widths.items():
            self.at[name] = (self.width, w)
            self.width += w

    def of(self, tensor, name):
        a, w = self.at[name]
        return tensor[:, a:a + w]


CONST = Packed(ident=P, mean=P, ones=P, before=W2, headmask=HG, prio=PAIRS * EXPERTS, region0=EXPERTS, row_no=1,
               k128=KT_MAX, tri=EXPERTS * EXPERTS, tile_no=TILES, tile_row=TILES)


class Turn:

    def __init__(self, order, last_two):
        self.order = order.split()
        self.last_two = last_two

    @staticmethod
    def parts(name):
        later = {"p": -1, "n": 1}.get(name[-1], 0) if name[-2].isdigit() else 0
        stem = name[:-1] if later else name
        kind = stem.rstrip("0123456789")
        return kind, int(stem[len(kind):] or 0), later

    def bank(self, name):
        return 6 + self.order.index(name) % 2

    def before(self, name):
        i = self.order.index(name)
        return (self.order[i - 2], 0) if i >= 2 else (self.last_two[i], 1)


FIRST = Turn("V1 mean O0 V2 var OT0 O1 V3 OT1 proj0 proj1 proj2 proj3 O2 proj4 proj5 OT2 V0n",
             (None, "V0n"))
BODY = Turn("O3p V1 mean OT3p O0 V2 out0p out1p var OT0 O1 V3 OT1 proj0 proj1 proj2 proj3 O2 proj4 proj5 OT2 V0n",
            ("OT2", "V0n"))
LAST = Turn("O3p V1 OT3p O0 V2 out0p out1p OT0 O1 V3 OT1 O2 OT2 O3 OT3 out0 out1", ("OT2", "V0n"))

_INS = "xT onehot embW embAdd consts qkv0 qkvb0 wo0 wob0 bias0 qkv1 wo1 wob1 gu0 dn0 ew rT rb gu1 dn1".split()


def kernel(**inputs):
    import numpy as np
    import concourse.bacc as bacc
    from concourse.bass_utils import run_bass_kernel_spmd

    v = {k: np.asarray(a) for k, a in inputs.items()}

    def rows(w):
        return w.reshape(-1, P, w.shape[1]).transpose(1, 0, 2)

    def cols(b):
        return b.reshape(-1, P).T

    side = SIDE // PATCH
    px = v["x"].reshape(IMAGES, CHANNELS, side, PATCH, side, PATCH).transpose(0, 2, 4, 1, 3, 5)
    px = px.reshape(IMAGES, T - 1, PK * P)
    px = np.concatenate([np.zeros((IMAGES, 1, PK * P), px.dtype), px], axis=1)
    onehot = np.zeros((ADDED, N), np.float32)
    at = np.arange(N)
    onehot[at % T, at] = 1.0
    onehot[T, at[at % T == 0]] = 1.0
    onehot[T + 1, at[at % T != 0]] = 1.0

    consts = np.zeros((P, CONST.width), np.float32)
    CONST.of(consts, "ident")[:] = np.eye(P)
    CONST.of(consts, "mean")[:] = 1.0 / D
    CONST.of(consts, "ones")[:] = 1.0
    CONST.of(consts, "before")[0:W2] = np.triu(np.ones((W2, W2)), 1)
    CONST.of(consts, "headmask")[np.arange(P), np.arange(P) // HD] = 1.0
    CONST.of(consts, "prio")[:] = np.tile(EXPERTS - np.arange(EXPERTS), PAIRS)
    CONST.of(consts, "region0")[:] = REGION * np.arange(EXPERTS)
    CONST.of(consts, "row_no")[:, 0] = np.arange(P)
    CONST.of(consts, "k128")[:] = P * np.arange(KT_MAX)
    CONST.of(consts, "tri")[:] = np.tril(np.ones((EXPERTS, EXPERTS))).reshape(-1)
    CONST.of(consts, "tile_no")[:] = np.arange(TILES)
    CONST.of(consts, "tile_row")[:] = P * np.arange(TILES)

    def gate_up(g, u):
        parts = [w[a:a + P] for a in range(0, g.shape[0], P) for w in (g, u)]
        return rows(np.concatenate(parts, axis=0).T)

    def down(d):
        w = d.T
        pad = -w.shape[0] % P
        return rows(np.concatenate([w, np.zeros((pad, D), w.dtype)], axis=0))

    relT = v["L0_attn_rel_emb"].T
    mid = (v["L0_attn_rel_emb"].shape[0] - 1) // 2

    def expert(g, u, d):
        gu = rows(np.concatenate([g.T, u.T], axis=1)).reshape(P, -1)
        return np.concatenate([gu, down(d).reshape(P, -1)], axis=1)

    arrays = {
        "xT": px.reshape(GROUPS, N, PK, P).transpose(0, 3, 2, 1),
        "onehot": onehot,
        "embW": rows(v["L0_tok_W"].T),
        "embAdd": np.concatenate([v["L0_tok_pos_enc"][0], v["L0_tok_cls_token"][0], v["L0_tok_b"][None]], axis=0),
        "consts": consts,
        "qkv0": rows(v["L0_attn_Wqkv"]),
        "qkvb0": cols(v["L0_attn_bqkv"]),
        "wo0": rows(v["L0_attn_Wout"]),
        "wob0": cols(v["L0_attn_bout"]),
        "bias0": np.stack([relT[:, mid - q:mid - q + T] for q in range(T)]),
        "qkv1": rows(np.concatenate([v["L1_attn_Wq"].T, v["L1_attn_Wk"].T, v["L1_attn_Wv"].T], axis=1)),
        "wo1": rows(v["L1_attn_Wo"].T),
        "wob1": cols(v["L1_attn_bo"]),
        "gu0": gate_up(v["L0_ffn_sg"], v["L0_ffn_su"]),
        "dn0": down(v["L0_ffn_sd"]),
        "ew": np.stack([expert(v["L0_ffn_rg"][e], v["L0_ffn_ru"][e], v["L0_ffn_rd"][e]) for e in range(EXPERTS)]),
        "rT": rows(v["L0_ffn_wr"].T),
        "rb": np.broadcast_to(v["L0_ffn_rb"], (P, PAIRS, EXPERTS)).reshape(P, PAIRS * EXPERTS),
        "gu1": gate_up(v["L1_ffn_w_gate"], v["L1_ffn_w_up"]),
        "dn1": down(v["L1_ffn_w_down"]),
    }
    nc = bacc.Bacc("TRN2", target_bir_lowering=False, num_devices=1)
    arrays = {f"in_{k}_dram": np.ascontiguousarray(arrays[k]) for k in _INS}
    args = [nc.dram_tensor(k, a.shape, mybir.dt.from_np(a.dtype), kind="ExternalInput").ap() for k, a in arrays.items()]
    out = nc.dram_tensor("out_0_dram", (P, DK, TOKENS), F32, kind="ExternalOutput").ap()
    xs = nc.dram_tensor("routed_in", (ROWS, XW), F32, kind="Internal").ap()
    ys = nc.dram_tensor("routed_out", (TILES * P, D), F32, kind="Internal").ap()
    vit_kernel(nc, *args, xs, ys, out)
    r = run_bass_kernel_spmd(nc, [arrays], core_ids=[0])
    got = r.results[0]["out_0_dram"]
    return got.transpose(2, 1, 0).reshape(IMAGES, T, D)
```

```python
from collections import namedtuple
from contextlib import ExitStack

import concourse.bass as bass
import numpy as np
from concourse import mybir

ALU = mybir.AluOpType
ACT = mybir.ActivationFunctionType
F32 = mybir.dt.float32
I32 = mybir.dt.int32
U32 = mybir.dt.uint32
F32R = mybir.dt.float32r
AX_X = mybir.AxisListType.X

P = 128
IMAGES, CHANNELS, SIDE, PATCH = 64, 3, 96, 16
T = (SIDE // PATCH) ** 2 + 1
D = 256
DK = D // P
PK = CHANNELS * PATCH * PATCH // P
PK_HALVES = slice(0, PK // 2), slice(PK // 2, PK)
EK = PK + 1
ADDED = T + 2
TOKENS = IMAGES * T
GI = 8
GROUPS = IMAGES // GI
N = GI * T
PAIRS = GI // 2
W2 = 2 * T
PITCH = 64
NPAD = (GI - 1) * T + PITCH
HEADS = 16
HD = D // HEADS
HG = P // HD
HP = HEADS // 2
EXPERTS = 7
I0, I1 = 704, 768
SCALE1 = 1.0 / 127.0
EPS = 1e-5
BIG = 3.0e38
XW = D + 1
REGION = TOKENS + P
TILES = (2 * TOKENS + EXPERTS * (P - 1)) // P
SPARE = TILES - 2 * TOKENS // P
KT_MAX = -(-TOKENS // P)
ROWS = EXPERTS * REGION + SPARE * P
EW = DK * 2 * I0 + 6 * D
IH = I0 // 2
ALL = slice(None)
MEAN_AT, VARIANCE_AT = (2, 0), (4, 2)
LAG = 2
FREE = 2


def hidden_chunks(width):
    return [min(P, width - a) for a in range(0, width, P)]


def vit_kernel(nc, xT, onehot, embW, embAdd, consts, qkv0, qkvb0, wo0, wob0, bias0, qkv1, wo1, wob1,
               gu0, dn0, ew, rT, rb, gu1, dn1, xs, ys, out):
    with ExitStack() as ctx:
        def sb(name, shape, dt=F32):
            return ctx.enter_context(nc.sbuf_tensor(name, shape, dt))

        def sem(name):
            return ctx.enter_context(nc.semaphore(name))

        ps = ctx.enter_context(nc.psum_tensor("ps", [P, 8, 512], F32))

        h = sb("h", [P, DK, TOKENS])
        cst = sb("cst", [P, CONST.width])
        ident, mean_w, ones = CONST.of(cst, "ident"), CONST.of(cst, "mean"), CONST.of(cst, "ones")
        before = CONST.of(cst, "before")[0:W2]
        headmask, prio = CONST.of(cst, "headmask"), CONST.of(cst, "prio")
        region0 = CONST.of(cst, "region0")
        eps_t = sb("eps_t", [P, 1])
        zero_t = sb("zero_t", [P, 1])

        arena_at = -(-nc.sbuf_base // 32) * 32
        arena = sb("arena", [P, EXPERTS * EW])
        used = [0]

        def carve(name, *shape, rows=P, dt=F32):
            t = nc.alloc_sbuf_tensor_at(name, [rows, *shape], dt, offset=arena_at + 4 * used[0])
            used[0] += -(-int(np.prod(shape)) // 8) * 8
            assert used[0] <= EXPERTS * EW
            return t[:]

        def halves(name, *shape, rows=P):
            return [carve(f"{name}_{part}", *shape, rows=rows, dt=F32R) for part in ("hi", "lo")]

        KT = carve("KT", DK, N)
        Km = [carve(f"Km{b}", DK, HG, W2) for b in range(2)]
        Sb = [carve(f"Sb{b}", HEADS, T) for b in range(2)]
        Sc = Sb
        PTs = [carve(f"PTs{b}", HP, 2, T) for b in range(2)]
        OTs = halves("OTs", DK, N)
        xa = halves("xa", DK, N)
        QT = carve("QT", DK, NPAD)
        On = [carve(f"On{b}", D) for b in range(2)]
        qkv_w, out_w = carve("qkv_w", DK, 3 * D), carve("out_w", DK, D)
        qkv_p, out_p = halves("qkv_p", DK, 3 * D), halves("out_p", DK, D)
        both = embedding_at = used[0]
        emb_a = carve("emb_a", D, rows=ADDED)
        one_s = carve("one_s", N, rows=ADDED)
        x_in = carve("x_in", 2, PK, N)
        emb_p, add_p = halves("emb_p", PK, D), halves("add_p", D, rows=ADDED)
        one_r = carve("one_r", N, rows=ADDED, dt=F32R)
        x_p = [halves(f"x_p{b}", PK, N) for b in range(2)]
        used[0] = both
        as_int = used[0]
        gu1_i, dn1_i = carve("gu1_i", DK, 2 * I1, dt=I32), carve("dn1_i", 6, D, dt=I32)
        used[0] = as_int
        gu1_w, dn1_w = carve("gu1_w", DK, 2 * I1), carve("dn1_w", 6, D)
        gu1_hi, dn1_hi = carve("gu1_hi", DK, 2 * I1, dt=F32R), carve("dn1_hi", 6, D, dt=F32R)
        merge = used[0]
        yg = [carve(f"yg{b}", PAIRS, 2, D, rows=W2) for b in range(2)]
        used[0] = merge
        gu1_lo, dn1_lo = carve("gu1_lo", DK, 2 * I1, dt=F32R), carve("dn1_lo", 6, D, dt=F32R)
        gu1_p, dn1_p = (gu1_hi, gu1_lo), (dn1_hi, dn1_lo)
        xf1 = [halves("xf1_0", DK, N)]
        used[0] = 0
        xf1.append(halves("xf1_1", DK, N))
        Hf1 = [halves(f"Hf1_{b}", N) for b in range(LAG + 1)]

        qkv_b = sb("qkv_b", [P, 3 * DK])
        out_b = [sb(f"out_b{l}", [P, DK]) for l in range(2)]
        bias = [sb(f"bias{l}", [P, HEADS, T]) for l in range(2)]
        norm_at = -(-nc.sbuf_base // 32) * 32
        cen = sb("cen", [P, DK, N])
        squ = sb("squ", [P, DK, N])
        lnv = sb("lnv", [P, N])
        rsd = sb("rsd", [P, N])
        xn = [sb(f"xn{b}", [P, DK, N]) for b in range(2)]
        vts = sb("vts", [P, PAIRS * 2 * XW])
        VT = vts[:, 0:DK * GI * 2 * PITCH].rearrange("p (c i a k) -> p c i a k", c=DK, i=GI, a=2)
        Vb = [sb(f"Vb{b}", [P, 2, HP, 2 * HD]) for b in range(2)]
        tile_w = [[nc.alloc_sbuf_tensor_at(f"tile_w{half}{part}", [P, 2 * DK, IH], F32R,
                                           offset=norm_at + 4 * (2 * half + part) * 2 * DK * IH)[:]
                   for part in range(2)] for half in range(2)]
        assert nc.sbuf_base - norm_at >= 4 * 8 * DK * IH
        prs_at = -(-nc.sbuf_base // 32) * 32
        prs = sb("prs", [P, PAIRS * 2 * XW])
        qkv_w1 = nc.alloc_sbuf_tensor_at("qkv_w1", [P, DK, 3 * D], F32, offset=prs_at)[:]
        out_w1 = nc.alloc_sbuf_tensor_at("out_w1", [P, DK, D], F32, offset=prs_at + 4 * DK * 3 * D)[:]
        Pr = [prs[:, b * HEADS * PITCH:(b + 1) * HEADS * PITCH].rearrange("p (h k) -> p h k", k=PITCH)
              for b in range(2)]
        mx = [sb(f"mx{b}", [P, HEADS]) for b in range(2)]
        sm = [sb(f"sm{b}", [P, HEADS]) for b in range(2)]
        rs = [sb(f"rs{b}", [P, HEADS]) for b in range(2)]

        shared_at = -(-nc.sbuf_base // 32) * 32
        shared = sb("shared", [P, EW])
        emb_w = nc.alloc_sbuf_tensor_at("emb_w", [P, PK, D], F32, offset=shared_at)[:]
        gu0_w = shared[:, 0:DK * 2 * I0].rearrange("p (c n) -> p c n", c=DK)
        dn0_w = shared[:, DK * 2 * I0:EW].rearrange("p (j n) -> p j n", j=6)
        xTs = [[nc.alloc_sbuf_tensor_at(f"xTs{b}{part}", [P, D], F32R, offset=shared_at + 4 * (EW - (2 * b + part + 1) * D))[:]
                for part in range(2)] for b in range(2)]
        Sgt = shared[:, 0:I0]
        Hdt = [shared[:, (1 + b) * I0:(2 + b) * I0] for b in range(2)]
        HTs = shared[:, 3 * I0:3 * I0 + 6 * P].rearrange("p (j m) -> p j m", j=6)
        assert 3 * I0 + 6 * P + 4 * D <= EW
        xt = [sb(f"xt{b}", [P, XW]) for b in range(2)]
        yt = [sb(f"yt{b}", [P, D]) for b in range(2)]

        Sg = [sb(f"Sg{b}", [P, N]) for b in range(2)]
        Hd = [sb(f"Hd{b}", [P, N]) for b in range(LAG + 1)]
        r_w = sb("r_w", [P, DK, EXPERTS])
        r_b = sb("r_b", [P, PAIRS * EXPERTS])
        rt = sb("rt", [P, 11, PAIRS * EXPERTS])
        place = sb("place", [P, EXPERTS])
        rows_x = [r[0:W2].rearrange("p (a k d) -> p a k d", a=PAIRS, k=2) for r in (prs, vts)]
        slot = [sb(f"slot{b}", [W2, 2, PAIRS], U32) for b in range(2)]
        slot_f = sb("slot_f", [W2, 2, PAIRS])
        slots_f = sb("slots_f", [W2, 2, GROUPS, PAIRS])
        slots = sb("slots", [W2, 2, GROUPS, PAIRS], U32)
        slot_g = [sb(f"slot_g{b}", [W2, 2, PAIRS], U32) for b in range(2)]
        ends = sb("ends", [1, EXPERTS], I32)
        zero_x = sb("zero_x", [P, XW])
        table = sb("table", [1, 2, TILES], I32)

        s_cst, s_embw, s_out = sem("s_cst"), sem("s_embw"), sem("s_out")
        s_embw2 = sem("s_embw2")
        first_hi, first_lo, patch_hi, patch_lo = sem("first_hi"), sem("first_lo"), sem("patch_hi"), sem("patch_lo")
        s_x = [sem("s_x0"), sem("s_x1")]
        s_attw, s_bias, s_rw, s_w1 = sem("s_attw"), sem("s_bias"), sem("s_rw"), sem("s_w1")
        s_shw, s_exw = sem("s_shw"), sem("s_exw")
        s_scat, s_junk, s_pad, s_table, s_t = sem("s_scat"), sem("s_junk"), sem("s_pad"), sem("s_table"), sem("s_t")
        s_ends = sem("s_ends")
        s_deq = sem("s_deq")
        s_upper, s_lower = sem("s_upper"), sem("s_lower")
        s_xt, s_yt = [sem("s_xt0"), sem("s_xt1")], sem("s_yt")
        s_turn = sem("s_turn")
        s_gat = [sem("s_gat0"), sem("s_gat1")]
        s_zero, s_tab = sem("s_zero"), sem("s_tab")
        emb_mm, emb_cp = sem("emb_mm"), sem("emb_cp")

        def group(g, w=N):
            return bass.ds(g * N, w)

        def counted(names, prefix):
            return namedtuple("Semaphores", names)(*[sem(prefix + n) for n in names.split()])

        A = [counted("mean_mm var_mm proj_mm S_mm PT_mm V_mm O_mm OT_mm out_mm "
                     "cen squ lnv rsd xn xh xl proj km sb mx sc ex sum rs PTs Vb On OTh OTs res", f"a{l}_") for l in range(2)]
        ffn_sems = "mean_mm var_mm gu_mm dn_mm cen squ lnv rsd xn xh xl sg hd hh hl y"
        routing_sems = " lg_mm cnt_mm rowA_mm rowB_mm sent lg rowA rowB r r_ex"
        F = [counted(ffn_sems + routing_sems, "f0_"), counted(ffn_sems, "f1_")]
        E = counted("xt_mm gu_mm ht_mm y_mm wh wl xh xt sg hd ht y stored", "e_")
        C = counted("mm0 mm1 slots slot h", "c_")

        block = ctx.enter_context(nc.Block())

        def weights_of(eng, t):
            return eng.value_load(table[0:1, 0, bass.ds(t, 1)], min_val=0, max_val=(EXPERTS - 1) * EW)

        def gate_up_of(w, half):
            return arena[:, bass.ds(w, 2 * DK * I0)].rearrange("p (q i) -> p q i", i=I0)[:, :, half * IH:(half + 1) * IH]

        def norms_idle(eng):
            eng.wait_ge(F[0].gu_mm, len(hidden_chunks(I0)) * GROUPS)
            eng.wait_ge(F[0].hd, FREE + len(hidden_chunks(I0)) * GROUPS)
            eng.wait_ge(F[0].sent, FREE + GROUPS)
            eng.wait_ge(s_table, 1)
            eng.wait_ge(s_exw, 16 * EXPERTS)

        def over_tiles(eng, step):
            with eng.Fori(0, (TILES - 3) // 2) as i:
                for k in (1, 2):
                    step(2 * i + k, k % 2, False)
            for t in range(TILES - 2, TILES):
                step(t, t % 2, t == TILES - 1)

        def over_groups(eng, step):
            step(0, 0, True, False)
            with eng.Fori(0, (GROUPS - 2) // 2) as i:
                for k in (1, 2):
                    step(2 * i + k, k % 2, False, False)
            step(GROUPS - 1, 1, False, True)

        def over_body(eng, l, step):
            first, body, last = ORDERS[l]
            step(0, 0, first, 0)
            with eng.Fori(0, (GROUPS - 2) // 2) as i:
                for k in (1, 2):
                    step(2 * i + k, k % 2, body, i + 1)
            step(GROUPS - 1, 1, last, None)

        def next_norm(l, g, X):
            return (F[l], 0) if X.last else (A[l], g + 1)

        @block.sync
        def _(sp):
            def patches(g, chunks=slice(0, PK)):
                return xT[bass.ds(g, 1), :, chunks].rearrange("a p k n -> (a p) k n")

            sp.dma_start(emb_a, embAdd).then_inc(s_embw, 16)
            sp.dma_start(one_s, onehot).then_inc(s_embw, 16)
            for chunks, done in zip(PK_HALVES, (s_embw, s_embw2)):
                sp.dma_start(emb_w[:, chunks], embW[:, chunks]).then_inc(done, 16)
                sp.dma_start(x_in[:, 0, chunks], patches(0, chunks)).then_inc(done, 16)
            sp.dma_start(x_in[:, 1], patches(1)).then_inc(s_x[1], 16)
            with sp.Fori(1, GROUPS // 2) as i:
                for b in range(2):
                    g = 2 * i + b
                    sp.wait_ge(patch_lo, g - 1)
                    sp.dma_start(x_in[:, b], patches(g)).then_inc(s_x[b], 16)
            sp.dma_start(gu0_w, gu0).then_inc(s_shw, 16)
            sp.dma_start(dn0_w, dn0).then_inc(s_shw, 16)
            sp.wait_ge(s_zero, 1)
            for k in range(SPARE):
                r = EXPERTS * REGION + k * P
                sp.dma_start(xs[r:r + P, :], zero_x[:]).then_inc(s_junk, 16)
            def load_experts(some):
                for e in some:
                    sp.dma_start(arena[:, e * EW:(e + 1) * EW], ew[e]).then_inc(s_exw, 16)

            beside = -(-embedding_at // EW)
            sp.wait_ge(emb_mm, FREE + GROUPS)
            load_experts(range(beside, EXPERTS))
            sp.wait_ge(A[0].res, FREE + 2 * GROUPS)
            load_experts(range(beside))

            sp.wait_ge(s_ends, 1)
            for e in range(EXPERTS):
                row = sp.value_load(ends[0:1, e:e + 1], min_val=0, max_val=ROWS - P)
                sp.dma_start(xs[bass.ds(row, P), :], zero_x[:]).then_inc(s_pad, 16)
            sp.wait_ge(s_scat, 128 * GROUPS)
            sp.wait_ge(s_pad, 16 * EXPERTS)
            sp.wait_ge(s_junk, 16 * SPARE)
            sp.wait_ge(s_table, 1)

            sp.dma_start(qkv_w1, qkv1).then_inc(s_attw, 16)
            sp.dma_start(out_w1, wo1).then_inc(s_attw, 16)

            def load(t, b):
                row = sp.value_load(table[0:1, 1, bass.ds(t, 1)], min_val=0, max_val=ROWS - P)
                sp.dma_start(xt[b][:], xs[bass.ds(row, P), :]).then_inc(s_xt[b], 16)

            load(0, 0)
            load(1, 1)
            with sp.Fori(0, (TILES - 3) // 2) as i:
                for b in range(2):
                    sp.wait_ge(E.hd, FREE + 4 * i + 2 * b + 2)
                    load(2 * i + b + 2, b)
            sp.wait_ge(E.hd, FREE + 2 * TILES - 4)
            load(TILES - 1, 0)

            sp.wait_ge(E.y_mm, TILES)
            sp.wait_ge(E.stored, FREE + TILES)
            sp.dma_start(gu1_i, gu1).then_inc(s_w1, 16)
            sp.dma_start(dn1_i, dn1).then_inc(s_w1, 16)
            with sp.Fori(0, GROUPS) as g:
                sp.wait_ge(F[1].y, FREE + 2 * g + 2)
                sp.dma_start(out[:, :, group(g)], h[:, :, group(g)]).then_inc(s_out, 16)
            sp.wait_ge(s_out, 16 * GROUPS)

        @block.gpsimd
        def _(pool):
            def km(a, l, n, p, b):
                pool.wait_ge(a.S_mm, n + 1)
                for c in range(DK):
                    src = KT[:, c, p * W2:(p + 1) * W2].unsqueeze(1).to_broadcast([P, HG, W2])
                    ins = pool.tensor_tensor(Km[p % 2][:, c], src, headmask.unsqueeze(2).to_broadcast([P, HG, W2]),
                                             ALU.mult)
                ins.then_inc(a.km, 1)

            def norm(s, g, b):
                pool.wait_ge(s.rsd, FREE + g + 1)
                pool.tensor_tensor(xn[b][:], cen[:], rsd[:].unsqueeze(1).to_broadcast([P, DK, N]),
                                   ALU.mult).then_inc(s.xn, 1)

            def lower_x(s, g, b, x):
                pool.wait_ge(s.xh, g + 1)
                pool.tensor_tensor(x[1], xn[b][:], x[0].bitcast(F32), ALU.subtract).then_inc(s.xl, 1)

            def attention(l):
                a = A[l]
                pool.wait_ge(s_upper, 2 * l + 2)
                pool.tensor_tensor(qkv_p[1], (qkv_w, qkv_w1)[l], qkv_p[0].bitcast(F32), ALU.subtract).then_inc(s_lower, 1)
                pool.tensor_tensor(out_p[1], (out_w, out_w1)[l], out_p[0].bitcast(F32), ALU.subtract).then_inc(s_lower, 1)
                if l == 1:
                    pool.memset(vts[:], 0.0)
                    for b in range(2):
                        pool.memset(Vb[b][:], 0.0)
                    pool.wait_ge(s_lower, 4)
                    pool.memset(prs[:], 0.0)
                for buf_free in (a.xn, a.km, F[l].xn) + ((F[l].sent,) if l == 0 else ()):
                    pool.sem_inc(buf_free, FREE)
                norm(a, 0, 0)
                lower_x(a, 0, 0, xa)
                pool.wait_ge(a.proj, FREE + 4)
                km(a, l, 0, 0, 0)
                km(a, l, 1, 1, 0)

                first, body, last = ORDERS[l]

                def step(g, b, X, more):
                    km(a, l, 4 * g + 2, 2, b)
                    km(a, l, 4 * g + 3, 3, b)
                    if more:
                        gather(g + 2, b, range(PAIRS // 2))
                    norm(*next_norm(l, g, X), 1 - b)
                    if X.last and l == 1:
                        lower_x(F[1], 0, 0, xf1[0])
                    if not X.last:
                        lower_x(a, g + 1, 1 - b, xa)
                        if more:
                            gather(g + 2, b, range(PAIRS // 2, PAIRS))
                        pool.wait_ge(a.proj, FREE + 6 * g + 10)
                        km(a, l, 4 * g + 4, 0, 1 - b)
                        km(a, l, 4 * g + 5, 1, 1 - b)
                more = l == 1
                step(0, 0, first, more)
                with pool.Fori(0, (GROUPS - 4) // 2) as i:
                    for k in (1, 2):
                        step(2 * i + k, k % 2, body, more)
                step(GROUPS - 3, 1, body, more)
                step(GROUPS - 2, 0, body, False)
                step(GROUPS - 1, 1, last, False)
                if l == 1:
                    pool.wait_ge(C.h, 2 * GROUPS)
                    for k, (w, (upper, lower)) in enumerate(((gu1_w, gu1_p), (dn1_w, dn1_p))):
                        pool.wait_ge(s_upper, 5 + k)
                        pool.tensor_tensor(lower, w, upper.bitcast(F32), ALU.subtract).then_inc(s_lower, 1)

            def scatter(s, g, b):
                pool.wait_ge(s.r, RCHAIN * (g + 1))
                pool.wait_ge(s.rowA, FREE + g + 1)
                pool.wait_ge(s.rowB, FREE + g + 1)
                pool.sem_inc(s_turn, 1)
                for p in range(PAIRS):
                    for k in range(2):
                        pool.indirect_dma_start(xs, bass.IndirectOffsetOnAxis(slot[b][:, k, p:p + 1], 0),
                                                rows_x[b][:, p, k, :], None).then_inc(s_scat, 16)

            def ffn(l):
                s = F[l]
                def step(g, b, first, last):
                    if l == 0:
                        scatter(s, g, b)
                    if not last:
                        norm(s, g + 1, 1 - b)
                        if l == 1:
                            lower_x(s, g + 1, 1 - b, xf1[1 - b])
                    if l == 0:
                        pool.wait_ge(s_scat, 128 * (g + 1))
                        pool.sem_inc(s.sent, 1)
                over_groups(pool, step)

            def stores():
                pool.sem_inc(E.stored, FREE)

                def store(t, b):
                    pool.wait_ge(E.y, FREE + t + 1)
                    pool.dma_start(ys[bass.ds(t * P, P), :], yt[b][:]).then_inc(s_yt, 16)
                    pool.wait_ge(s_yt, 16 * t + 16)
                    pool.sem_inc(E.stored, 1)
                with pool.Fori(0, TILES // 2) as i:
                    for b in range(2):
                        store(2 * i + b, b)
                store(TILES - 1, 0)

            def gather(g, b, pairs=range(PAIRS)):
                if 0 in pairs:
                    gather_slots(g, b)
                for p in pairs:
                    for k in range(2):
                        pool.indirect_dma_start(yg[b][:, p, k], None, ys,
                                                bass.IndirectOffsetOnAxis(slot_g[b][:, k, p:p + 1], 0))\
                            .then_inc(s_gat[b], 16)

            def gather_slots(g, b):
                pool.tensor_copy(slot_g[b][:], slots[:, :, bass.ds(g, 1), :].rearrange("p k g a -> p k (g a)"))\
                    .then_inc(C.slot, 1)
                pool.wait_ge(C.slot, FREE + g + 1)
                pool.wait_ge(C.mm1, g + 1)
                pool.sem_inc(s_turn, 1)

            pool.memset(zero_x[:], 0.0).then_inc(s_zero, 1)
            pool.memset(eps_t[:], EPS).then_inc(s_zero, 1)
            pool.memset(zero_t[:], 0.0).then_inc(s_zero, 1)
            pool.memset(QT[:, :, N:], 0.0).then_inc(s_zero, 1)
            pool.memset(vts[:], 0.0).then_inc(s_zero, 1)
            for b in range(2):
                pool.memset(Pr[b], 0.0).then_inc(s_zero, 1)
                pool.memset(Vb[b][:], 0.0).then_inc(s_zero, 1)
                pool.memset(On[b], 0.0).then_inc(s_zero, 1)
            pool.memset(bias[0][:], 0.0).then_inc(s_zero, 1)
            pool.memset(bias[1][:], 0.0).then_inc(s_zero, 1)
            pool.wait_ge(s_bias, 32)
            for l in range(2):
                for q in (0, PITCH):
                    tab = bias[l][q:q + T]
                    pool.affine_select(out=tab, in_=tab, compare_op=ALU.is_ge, fill=-BIG, base=0,
                                       pattern=[[0, HEADS], [-1, T]], channel_multiplier=1).then_inc(s_tab, 1)
            pool.wait_ge(s_cst, 16)
            pool.wait_ge(s_tab, 4)
            attention(0)
            ffn(0)
            stores()
            pool.memset(QT[:, :, N:], 0.0)
            for b in range(2):
                pool.memset(On[b], 0.0)
            pool.sem_inc(C.slot, FREE)
            pool.wait_ge(C.slots, 1)
            gather(0, 0)
            gather(1, 1)
            attention(1)
            ffn(1)

        @block.scalar
        def _(act):
            act.dma_start(cst[:], consts).then_inc(s_cst, 16)
            act.dma_start(qkv_w, qkv0).then_inc(s_attw, 16)
            act.dma_start(out_w, wo0).then_inc(s_attw, 16)
            for l, ob in enumerate((wob0, wob1)):
                act.dma_start(out_b[l][:], ob).then_inc(s_attw, 16)
            act.dma_start(qkv_b[:], qkvb0).then_inc(s_attw, 16)
            act.dma_start(r_w[:], rT).then_inc(s_rw, 16)
            act.dma_start(r_b[:], rb).then_inc(s_rw, 16)
            act.wait_ge(s_zero, 13)
            for q in (0, PITCH):
                act.dma_start(bias[0][q:q + T], bias0).then_inc(s_bias, 16)

            def embedding_out(g, b):
                act.wait_ge(emb_mm, FREE + g + 1)
                act.activation(h[:, :, group(g)], ps[:, 2 * b:2 * b + 2, 0:N], ACT.Copy).then_inc(emb_cp, 1)

            act.preload_act_table_set("natural_log_exp_and_others")
            def upper_patches(g, b, loaded):
                act.wait_ge(s_x[b], loaded)
                act.wait_ge(emb_mm, g + 1)
                act.activation(x_p[b][0], x_in[:, b], ACT.Copy).then_inc(patch_hi, 1)

            act.sem_inc(emb_cp, FREE)
            act.wait_ge(s_embw, 16 * 4)
            act.activation(add_p[0], emb_a, ACT.Copy).then_inc(first_hi, 1)
            act.activation(one_r, one_s, ACT.Copy).then_inc(first_hi, 1)
            for half, chunks in enumerate(PK_HALVES):
                if half == 1:
                    act.wait_ge(s_embw2, 32)
                act.activation(emb_p[0][:, chunks], emb_w[:, chunks], ACT.Copy).then_inc(first_hi, 1)
                act.activation(x_p[0][0][:, chunks], x_in[:, 0, chunks], ACT.Copy).then_inc(first_hi, 1)
            act.sem_inc(patch_hi, 1)
            upper_patches(1, 1, 16)
            with act.Fori(0, GROUPS // 2 - 1) as i:
                for b in range(2):
                    embedding_out(2 * i + b, b)
                    upper_patches(2 * i + b + 2, b, 16 * (i + 1) + 16 * b)

            def squares(s, g):
                act.wait_ge(s.cen, FREE + g + 1)
                act.activation(squ[:], cen[:], ACT.Square).then_inc(s.squ, 1)

            def deviation(s, g, bk):
                act.wait_ge(s.var_mm, g + 1)
                act.activation(lnv[:], ps[:, bk, 0:N], ACT.Ln, bias=eps_t[:]).then_inc(s.lnv, 1)
                act.wait_ge(s.lnv, FREE + g + 1)
                act.activation(rsd[:], lnv[:], ACT.Exp, bias=zero_t[:], scale=-0.5).then_inc(s.rsd, 1)

            def upper_x(s, g, b, x):
                act.wait_ge(s.xn, FREE + g + 1)
                act.activation(x[0], xn[b][:], ACT.Copy).then_inc(s.xh, 1)

            def attention(l):
                a = A[l]
                if l == 1:
                    act.preload_act_table_set("natural_log_exp_and_others")
                act.wait_ge(s_attw, 16 * (5, 7)[l])
                if l == 1:
                    act.wait_ge(E.y_mm, TILES)
                act.activation(qkv_p[0], (qkv_w, qkv_w1)[l], ACT.Copy).then_inc(s_upper, 1)
                act.activation(out_p[0], (out_w, out_w1)[l], ACT.Copy).then_inc(s_upper, 1)
                f = F[l]
                for buf_free in (a.squ, a.lnv, a.rsd, a.proj, a.ex, a.PTs, a.Vb, f.squ, f.lnv, f.rsd) + \
                        ((f.rowA, f.rowB) if l == 0 else ()):
                    act.sem_inc(buf_free, FREE)

                def project(g, b, k, bk):
                    act.wait_ge(a.proj_mm, 6 * g + k + 1)
                    if k < 2 * DK:
                        dst, src = (QT, KT)[k // DK][:, k % DK, 0:N], ps[:, bk, 0:N]
                    else:
                        dst = VT[:, k % DK, :, :, 0:T]
                        src = ps[:, bk, 0:N].rearrange("p (i t) -> p i t", t=T).unsqueeze(2).to_broadcast([P, GI, 2, T])
                    act.activation(dst, src, ACT.Identity,
                                   bias=qkv_b[:, k:k + 1] if l == 0 else zero_t[:]).then_inc(a.proj, 1)

                def exps(n, p):
                    act.wait_ge(a.sc, FREE + n + 1)
                    act.wait_ge(a.PT_mm, n + 1)
                    act.wait_ge(a.sum, n + 1)
                    act.activation(Pr[p % 2][:, :, 0:T], Sc[p % 2], ACT.Exp).then_inc(a.ex, 1)

                def probs_t(n, p):
                    act.wait_ge(a.PT_mm, FREE + n + 1)
                    act.wait_ge(a.O_mm, n + 1)
                    src = ps[:, 4:6, :].rearrange("p b (h i q) -> p (b h) i q", h=HP // 2, i=2)[:, :, :, 0:T]
                    act.activation(PTs[p % 2], src, ACT.Copy).then_inc(a.PTs, 1)

                def out_t(n, p, bk):
                    act.wait_ge(a.OT_mm, FREE + n + 1)
                    src = ps[:, bk, 0:DK * P].rearrange("p (c i q) -> p c i q", c=DK, i=2)[:, :, :, 0:T]
                    dst = OTs[0][:, :, p * W2:(p + 1) * W2].rearrange("p c (i q) -> p c i q", i=2)
                    act.activation(dst, src, ACT.Copy).then_inc(a.OTh, 1)

                def values(n, p, bk):
                    act.wait_ge(a.V_mm, n + 1)
                    act.wait_ge(a.O_mm, n + 1)
                    for half in range(2):
                        rows = slice(half * PITCH, half * PITCH + PITCH)
                        cols = slice(half * HD, half * HD + HD)
                        src = ps[rows, bk, :].rearrange("p (r w) -> p r w", w=2 * HD)[:, :, cols]
                        dst = Vb[p % 2][rows].rearrange("p i h w -> p (i h) w")[:, :, cols]
                        ins = act.activation(dst, src, ACT.Copy)
                    ins.then_inc(a.Vb, 1)

                def dequantise(w, as_integer, upper):
                    act.activation(w, as_integer, ACT.Copy, scale=SCALE1).then_inc(s_deq, 1)
                    act.wait_ge(s_deq, 1 if w is gu1_w else 2)
                    act.activation(upper, w, ACT.Copy).then_inc(s_upper, 1)

                if l == 1:
                    act.wait_ge(s_w1, 32)
                    dequantise(gu1_w, gu1_i, gu1_hi)
                    dequantise(dn1_w, dn1_i, dn1_hi)
                first, body, last = ORDERS[l]
                squares(a, 0)
                if l == 0:
                    embedding_out(GROUPS - 2, 0)
                deviation(a, 0, 7)
                upper_x(a, 0, 0, xa)
                if l == 0:
                    embedding_out(GROUPS - 1, 1)
                for k in range(6):
                    project(0, 0, k, 6 + k % 2)
                values(0, 0, 7)
                exps(0, 0)

                def step(g, b, X, turn):
                    n = 4 * g
                    values(n + 1, 1, X.bank("V1"))
                    probs_t(n, 0)
                    if not X.first:
                        out_t(n - 1, 3, X.bank("OT3p"))
                    exps(n + 1, 1)
                    squares(*next_norm(l, g, X))
                    values(n + 2, 2, X.bank("V2"))
                    probs_t(n + 1, 1)
                    deviation(*next_norm(l, g, X), X.bank("var"))
                    exps(n + 2, 2)
                    out_t(n, 0, X.bank("OT0"))
                    if X.last and l == 1:
                        upper_x(F[1], 0, 0, xf1[0])
                    if not X.last:
                        upper_x(a, g + 1, 1 - b, xa)
                    values(n + 3, 3, X.bank("V3"))
                    probs_t(n + 2, 2)
                    out_t(n + 1, 1, X.bank("OT1"))
                    if not X.last:
                        for k in range(2):
                            project(g + 1, 1 - b, k, X.bank(f"proj{k}"))
                    exps(n + 3, 3)
                    if not X.last:
                        for k in (2, 3):
                            project(g + 1, 1 - b, k, X.bank(f"proj{k}"))
                    probs_t(n + 3, 3)
                    if not X.last:
                        for k in (4, 5):
                            project(g + 1, 1 - b, k, X.bank(f"proj{k}"))
                    out_t(n + 2, 2, X.bank("OT2"))
                    if not X.last:
                        values(n + 4, 0, X.bank("V0n"))
                        exps(n + 4, 0)
                over_body(act, l, step)
                out_t(4 * GROUPS - 1, 3, last.bank("OT3"))

            def upper_hidden(s, n, j, r):
                act.wait_ge(s.hd, FREE + n + 1)
                act.wait_ge(s.dn_mm, n + 1)
                act.activation(Hf1[j % (LAG + 1)][0][0:r], Hd[j % (LAG + 1)][0:r], ACT.Copy).then_inc(s.hh, 1)

            def silus(s, g, rows, halved):
                for j, r in enumerate(rows):
                    act.wait_ge(s.gu_mm, len(rows) * g + j + 1)
                    act.wait_ge(s.hd, len(rows) * g + j + 1)
                    act.activation(Sg[j % 2][0:r], ps[0:r, 2 * (j % 2), 0:N], ACT.Silu).then_inc(s.sg, 1)
                    if halved:
                        upper_hidden(s, len(rows) * g + j, j, r)
                    yield j

            def ffn(l):
                s = F[l]
                def r_exp(g):
                    if l == 0:
                        act.wait_ge(s.r, RCHAIN * g + 10)
                        act.activation(rt[0:W2, 9, 0:PAIRS], rt[0:W2, 8, 0:PAIRS], ACT.Exp).then_inc(s.r_ex, 1)

                def rows(g, b, half):
                    if l == 0:
                        mm_done, done = (s.rowA_mm, s.rowB_mm)[half], (s.rowA, s.rowB)[half]
                        act.wait_ge(mm_done, g + 1)
                        src = ps[0:W2, 7, :].rearrange("p (a d) -> p a d", a=2).unsqueeze(2).to_broadcast([W2, 2, 2, D])
                        act.activation(rows_x[b][:, 2 * half:2 * half + 2, :, 0:D], src, ACT.Copy).then_inc(done, 1)

                def step(g, b, first, last):
                    for j in silus(s, g, hidden_chunks((I0, I1)[l]), l == 1):
                        if first and j == 0:
                            rows(0, 0, 0)
                            r_exp(0)
                        if j == 0:
                            rows(g, b, 1)
                        if j == MEAN_AT[l] + 1 and not last:
                            squares(s, g + 1)
                        if j == VARIANCE_AT[l] and not last:
                            act.preload_act_table_set("natural_log_exp_and_others")
                            deviation(s, g + 1, 7)
                        if l == 1 and j == VARIANCE_AT[l] + 1 and not last:
                            upper_x(s, g + 1, 1 - b, xf1[1 - b])
                    if not last:
                        if l == 0:
                            act.wait_ge(s.sent, g + 2)
                        rows(g + 1, 1 - b, 0)
                        r_exp(g + 1)
                over_groups(act, step)

            def routed():
                s = E
                for buf_free in (s.ht,):
                    act.sem_inc(buf_free, FREE)

                def gate(t, half):
                    act.wait_ge(s.gu_mm, 2 * t + half + 1)
                    act.activation(Sgt[:, half * IH:(half + 1) * IH], ps[:, half, 0:IH], ACT.Silu).then_inc(s.sg, 1)

                def hidden_t(t):
                    act.wait_ge(s.ht_mm, t + 1)
                    act.activation(HTs[:, 0:5], ps[:, 4:6, :].rearrange("p b (j m) -> p (b j) m", m=P)[:, 0:5],
                                   ACT.Copy)
                    act.activation(HTs[0:I0 - 5 * P, 5], ps[0:I0 - 5 * P, 5, P:2 * P], ACT.Copy).then_inc(s.ht, 1)

                def upper_weights(t, w, half):
                    act.activation(tile_w[half][0], gate_up_of(w, half), ACT.Copy).then_inc(s.wh, 1)

                def upper_in(t, b):
                    act.wait_ge(s.xt_mm, t + 1)
                    act.activation(xTs[b][0], ps[:, 6, 0:D], ACT.Copy).then_inc(s.xh, 1)

                def step(t, b, last):
                    if not last:
                        w = weights_of(act, t + 1)
                    gate(t, 0)
                    if not last:
                        upper_weights(t + 1, w, 0)
                    hidden_t(t - 1)
                    gate(t, 1)
                    if not last:
                        upper_in(t + 1, 1 - b)
                        upper_weights(t + 1, w, 1)

                norms_idle(act)
                w = weights_of(act, 0)
                upper_weights(0, w, 0)
                upper_weights(0, w, 1)
                upper_in(0, 0)
                w = weights_of(act, 1)
                gate(0, 0)
                upper_weights(1, w, 0)
                gate(0, 1)
                upper_in(1, 1)
                upper_weights(1, w, 1)
                over_tiles(act, step)
                hidden_t(TILES - 1)

            attention(0)
            ffn(0)
            routed()
            attention(1)
            ffn(1)

        @block.vector
        def _(dve):
            def centre(s, g, bk):
                dve.wait_ge(s.mean_mm, g + 1)
                dve.tensor_tensor(cen[:], h[:, :, group(g)], ps[:, bk, 0:N].unsqueeze(1).to_broadcast([P, DK, N]),
                                  ALU.subtract).then_inc(s.cen, 1)

            def attention(l):
                a = A[l]
                f = F[l]
                for buf_free in (f.cen, f.hd, f.hl, f.y) + ((f.lg,) if l == 0 else ()):
                    dve.sem_inc(buf_free, FREE)
                for buf_free in (a.cen, a.sb, a.mx, a.sc, a.sum, a.rs, a.On, a.OTs, a.res):
                    dve.sem_inc(buf_free, FREE)

                def softmax_in(n, p):
                    b = p % 2
                    dve.wait_ge(a.S_mm, FREE + n + 1)
                    dve.wait_ge(a.ex, n + 1)
                    src = ps[:, 2 * b:2 * b + 2, :].rearrange("p b (h k) -> p (b h) k", k=PITCH)[:, :, 0:T]
                    dve.scalar_tensor_tensor(out=Sb[b], in0=src, scalar=HD ** -0.5, in1=bias[l][:],
                                             op0=ALU.mult, op1=ALU.add).then_inc(a.sb, 1)
                    dve.wait_ge(a.sb, FREE + n + 1)
                    dve.tensor_reduce(mx[b][:], Sb[b], AX_X, ALU.max).then_inc(a.mx, 1)
                    dve.wait_ge(a.mx, FREE + n + 1)
                    dve.tensor_tensor(Sc[b], Sb[b], mx[b][:].unsqueeze(2).to_broadcast([P, HEADS, T]),
                                      ALU.subtract).then_inc(a.sc, 1)

                def sums(n, p):
                    b = p % 2
                    dve.wait_ge(a.ex, FREE + n + 1)
                    dve.tensor_reduce(sm[b][:], Pr[b][:, :, 0:T], AX_X, ALU.add).then_inc(a.sum, 1)
                    dve.wait_ge(a.sum, FREE + n + 1)
                    dve.reciprocal(rs[b][:], sm[b][:]).then_inc(a.rs, 1)

                def normalise(n, p, bk):
                    b = p % 2
                    dve.wait_ge(a.O_mm, FREE + n + 1)
                    dve.wait_ge(a.rs, FREE + n + 1)
                    dve.wait_ge(a.OT_mm, n + 1)
                    for i in range(2):
                        r = slice(i * PITCH, i * PITCH + T)
                        ins = dve.tensor_tensor(On[b][r].rearrange("p (h d) -> p h d", d=HD),
                                                ps[r, bk, 0:D].rearrange("p (h d) -> p h d", d=HD),
                                                rs[b][r].unsqueeze(2).to_broadcast([T, HEADS, HD]), ALU.mult)
                    ins.then_inc(a.On, 1)

                def lower_out(n, p, bk):
                    dve.wait_ge(a.OTh, n + 1)
                    cols = slice(p * W2, (p + 1) * W2)
                    src = ps[:, bk, 0:DK * P].rearrange("p (c i q) -> p c i q", c=DK, i=2)[:, :, :, 0:T]
                    upper, lower = [t[:, :, cols].rearrange("p c (i q) -> p c i q", i=2) for t in OTs]
                    dve.tensor_tensor(lower, src, upper.bitcast(F32), ALU.subtract).then_inc(a.OTs, 1)

                def residual(g, m, bk):
                    dve.wait_ge(a.out_mm, 2 * g + m + 1)
                    hm = h[:, m, group(g)]
                    dve.scalar_tensor_tensor(out=hm, in0=ps[:, bk, 0:N], scalar=out_b[l][:, m:m + 1], in1=hm,
                                             op0=ALU.add, op1=ALU.add).then_inc(a.res, 1)

                def add_routed(g, c, bk):
                    dve.wait_ge((C.mm0, C.mm1)[c], FREE + g + 1)
                    hc = h[:, c, group(g)]
                    dve.tensor_tensor(hc, hc, ps[:, bk, 0:N], ALU.add).then_inc(C.h, 1)

                first, body, last = ORDERS[l]
                if l == 1:
                    add_routed(0, 0, 6)
                    add_routed(0, 1, 7)
                centre(a, 0, 6)
                softmax_in(0, 0)

                def step(g, b, X, turn):
                    n = 4 * g
                    if l == 1 and not X.last:
                        add_routed(g + 1, 0, X.bank("comb0"))
                        add_routed(g + 1, 1, X.bank("comb1"))
                    if not X.first:
                        normalise(n - 1, 3, X.bank("O3p"))
                    softmax_in(n + 1, 1)
                    centre(*next_norm(l, g, X), X.bank("mean"))
                    if not X.first:
                        lower_out(n - 1, 3, X.bank("OT3p"))
                    sums(n, 0)
                    normalise(n, 0, X.bank("O0"))
                    softmax_in(n + 2, 2)
                    if not X.first:
                        residual(g - 1, 0, X.bank("out0p"))
                        residual(g - 1, 1, X.bank("out1p"))
                    sums(n + 1, 1)
                    lower_out(n, 0, X.bank("OT0"))
                    normalise(n + 1, 1, X.bank("O1"))
                    lower_out(n + 1, 1, X.bank("OT1"))
                    softmax_in(n + 3, 3)
                    sums(n + 2, 2)
                    normalise(n + 2, 2, X.bank("O2"))
                    sums(n + 3, 3)
                    lower_out(n + 2, 2, X.bank("OT2"))
                    if not X.last:
                        softmax_in(n + 4, 0)
                over_body(dve, l, step)
                normalise(4 * GROUPS - 1, 3, last.bank("O3"))
                lower_out(4 * GROUPS - 1, 3, last.bank("OT3"))
                residual(GROUPS - 1, 0, last.bank("out0"))
                residual(GROUPS - 1, 1, last.bank("out1"))

            def gates(s, g, rows, halved):
                for j, r in enumerate(rows):
                    n = len(rows) * g + j
                    dve.wait_ge(s.sg, n + 1)
                    dve.wait_ge(s.dn_mm, n + 1)
                    up = ps[0:P, 2 * (j % 2) + 1, 0:N] if r == P else ps[r:2 * r, 2 * (j % 2), 0:N]
                    if halved:
                        dve.wait_ge(s.hl, n + 1)
                    dve.tensor_tensor(Hd[j % (LAG + 1)][0:r], Sg[j % 2][0:r], up, ALU.mult).then_inc(s.hd, 1)
                    if halved:
                        dve.wait_ge(s.hh, n + 1)
                        upper, lower = [t[0:r] for t in Hf1[j % (LAG + 1)]]
                        dve.tensor_tensor(lower, Hd[j % (LAG + 1)][0:r], upper.bitcast(F32), ALU.subtract).then_inc(s.hl, 1)
                    yield j

            def ffn(l):
                s = F[l]
                R = slice(0, W2)
                done = [0]

                def t(i):
                    return rt[R, i].rearrange("p (a e) -> p a e", e=EXPERTS)

                def c(i):
                    return rt[R, i, 0:PAIRS]

                def wide(i):
                    return c(i).unsqueeze(2).to_broadcast([W2, PAIRS, EXPERTS])

                def linker(base):
                    done[0] = 0

                    def link(ins):
                        ins.then_inc(s.r, 1)
                        done[0] += 1
                        dve.wait_ge(s.r, base + done[0])
                    return link

                def route(g, b):
                    link = linker(RCHAIN * g)
                    pr = prio[R].rearrange("p (a e) -> p a e", e=EXPERTS)
                    dve.wait_ge(s.lg_mm, g + 1)
                    dve.tensor_tensor(rt[R, 0], ps[R, 6, 0:PAIRS * EXPERTS], r_b[R], ALU.add).then_inc(s.lg, 1)
                    dve.wait_ge(s.lg, FREE + g + 1)
                    link(dve.tensor_reduce(c(1), t(0), AX_X, ALU.max))
                    link(dve.tensor_tensor(t(2), t(0), wide(1), ALU.is_equal))
                    link(dve.tensor_tensor(t(2), t(2), pr, ALU.mult))
                    link(dve.tensor_reduce(c(3), t(2), AX_X, ALU.max))
                    link(dve.tensor_tensor(t(4), t(2), wide(3), ALU.is_equal))
                    link(dve.scalar_tensor_tensor(out=t(5), in0=t(4), scalar=-BIG, in1=t(0), op0=ALU.mult, op1=ALU.add))
                    link(dve.tensor_reduce(c(6), t(5), AX_X, ALU.max))
                    link(dve.tensor_tensor(t(7), t(5), wide(6), ALU.is_equal))
                    link(dve.tensor_tensor(t(7), t(7), pr, ALU.mult))
                    link(dve.tensor_tensor(c(8), c(6), c(1), ALU.subtract))
                    link(dve.tensor_reduce(c(3), t(7), AX_X, ALU.max))
                    link(dve.tensor_tensor(t(5), t(7), wide(3), ALU.is_equal))
                    link(dve.tensor_tensor(t(10), t(4), t(5), ALU.add))
                    dve.wait_ge(s.r_ex, g + 1)
                    link(dve.tensor_scalar(c(1), c(9), 1.0, None, ALU.add))
                    link(dve.reciprocal(c(6), c(1)))
                    link(dve.tensor_tensor(c(1), c(6), c(9), ALU.mult))
                    dve.wait_ge(s.sent, g + 1)
                    link(dve.tensor_copy(rows_x[b][:, :, 0, D], c(6)))
                    link(dve.tensor_copy(rows_x[b][:, :, 1, D], c(1)))
                    assert done[0] == ROUTE

                def slots_of(g, b):
                    link = linker(RCHAIN * g + ROUTE)
                    dve.wait_ge(s.cnt_mm, g + 1)
                    link(dve.tensor_tensor(t(7), ps[R, 6, 0:PAIRS * EXPERTS].rearrange("p (a e) -> p a e", e=EXPERTS),
                                           place[R].unsqueeze(1).to_broadcast([W2, PAIRS, EXPERTS]), ALU.add))
                    for k in range(2):
                        link(dve.tensor_tensor(t(2), t(7), t(4 + k), ALU.mult))
                        link(dve.tensor_reduce(slot_f[:, k], t(2), AX_X, ALU.add))
                    link(dve.tensor_copy(slot[b][:], slot_f[:]))
                    link(dve.tensor_copy(slots_f[:, :, bass.ds(g, 1), :].rearrange("p k g a -> p k (g a)"), slot_f[:]))
                    link(dve.tensor_tensor(place[:], place[:], ps[:, 6, 32:32 + EXPERTS], ALU.add))
                    assert done[0] == RCHAIN - ROUTE

                def table_of_tiles():
                    count = [0]

                    def link(ins):
                        ins.then_inc(s_t, 1)
                        count[0] += 1
                        dve.wait_ge(s_t, count[0])

                    dve.tensor_copy(ends[:], place[0:1]).then_inc(s_ends, 1)
                    at_a, at_b = cen[:].rearrange("p c n -> p (c n)"), squ[:].rearrange("p c n -> p (c n)")

                    def cut(src, at, *shape):
                        v = src[:, at:at + int(np.prod(shape))]
                        return v if len(shape) == 1 else v.rearrange("p (a b) -> p a b", b=shape[1])

                    def over(v, *shape):
                        return v.unsqueeze(1).to_broadcast([v.shape[0], *shape])

                    def under(v, *shape):
                        return v.unsqueeze(2).to_broadcast([v.shape[0], *shape])

                    count_e, tiles_e, last_e, move_e = [rt[:, i, 0:EXPERTS] for i in range(4)]
                    used, tri = cut(at_a, 0, EXPERTS, KT_MAX), cut(at_a, 136, EXPERTS, EXPERTS)
                    past, gone = cut(at_a, 192, TILES, EXPERTS), cut(at_b, 0, TILES, EXPERTS)
                    expert_t, first_t, row_t, w_t = [cut(at_b, 304 + 48 * i, TILES) for i in range(4)]
                    k128, tri_c = CONST.of(cst, "k128"), CONST.of(cst, "tri").rearrange("p (a b) -> p a b", b=EXPERTS)
                    tile_no, tile_row = CONST.of(cst, "tile_no"), CONST.of(cst, "tile_row")
                    link(dve.tensor_tensor(count_e, place[:], region0, ALU.subtract))
                    link(dve.tensor_tensor(used, over(k128, EXPERTS, KT_MAX), under(count_e, EXPERTS, KT_MAX), ALU.is_lt))
                    link(dve.tensor_reduce(tiles_e, used, AX_X, ALU.add))
                    yield
                    link(dve.tensor_tensor(tri, tri_c, over(tiles_e, EXPERTS, EXPERTS), ALU.mult))
                    link(dve.tensor_reduce(last_e, tri, AX_X, ALU.add))
                    link(dve.tensor_tensor(past, under(tile_no, TILES, EXPERTS), over(last_e, TILES, EXPERTS), ALU.is_ge))
                    link(dve.tensor_reduce(expert_t, past, AX_X, ALU.add))
                    yield
                    link(dve.tensor_tensor(gone, past, over(tiles_e, TILES, EXPERTS), ALU.mult))
                    link(dve.tensor_reduce(first_t, gone, AX_X, ALU.add))
                    link(dve.scalar_tensor_tensor(out=row_t, in0=expert_t, scalar=float(REGION), in1=tile_row,
                                                  op0=ALU.mult, op1=ALU.add))
                    link(dve.scalar_tensor_tensor(out=row_t, in0=first_t, scalar=-float(P), in1=row_t,
                                                  op0=ALU.mult, op1=ALU.add))
                    yield
                    link(dve.tensor_scalar(w_t, expert_t, float(EXPERTS - 1), float(EW), ALU.min, ALU.mult))
                    link(dve.tensor_copy(table[:, 0], w_t[0:1]))
                    dve.tensor_copy(table[:, 1], row_t[0:1]).then_inc(s_table, 1)
                    at = slots_f[:].rearrange("p k g a -> p (k g a)")
                    n = 2 * GROUPS * PAIRS
                    past, move = cut(at_a, 0, n, EXPERTS - 1), move_e[:, 0:EXPERTS - 1]
                    link(dve.tensor_scalar(move, tiles_e[:, 0:EXPERTS - 1], float(P), -float(REGION), ALU.mult, ALU.add))
                    link(dve.tensor_tensor(past[R], under(at, n, EXPERTS - 1), over(region0[R, 1:EXPERTS], n, EXPERTS - 1),
                                           ALU.is_ge))
                    link(dve.tensor_tensor(past[R], past[R], over(move[R], n, EXPERTS - 1), ALU.mult))
                    link(dve.tensor_reduce(at_b[R, 0:n], past[R], AX_X, ALU.add))
                    dve.tensor_tensor(slots[:].rearrange("p k g a -> p (k g a)"), at_b[R, 0:n], at, ALU.add)\
                        .then_inc(C.slots, 1)
                    yield

                def add_y(g):
                    dve.wait_ge(s.dn_mm, LAG + 1 + 6 * g + 6)
                    for m in range(DK):
                        hm = h[:, m, group(g)]
                        dve.tensor_tensor(hm, hm, ps[:, 4 + m, 0:N], ALU.add).then_inc(s.y, 1)

                def step(g, b, first, last):
                    for j in gates(s, g, hidden_chunks((I0, I1)[l]), l == 1):
                        if l == 0 and first and j == 0:
                            route(0, 0)
                        if l == 0 and j == 0:
                            slots_of(g, b)
                            pieces = table_of_tiles()
                        if l == 0 and last and j < TABLE_PIECES:
                            next(pieces)
                        if j == 1 and not first:
                            add_y(g - 1)
                        if j == MEAN_AT[l] and not last:
                            centre(s, g + 1, 6)
                    if l == 0 and not last:
                        route(g + 1, 1 - b)
                over_groups(dve, step)
                add_y(GROUPS - 1)

            def routed():
                s = E
                for buf_free in (s.xt, s.hd, s.y):
                    dve.sem_inc(buf_free, FREE)

                def lower_weights(t, w, half):
                    dve.wait_ge(s.wh, 2 * t + half + 1)
                    dve.tensor_tensor(tile_w[half][1], gate_up_of(w, half), tile_w[half][0].bitcast(F32),
                                      ALU.subtract).then_inc(s.wl, 1)

                def tile_in(t, b):
                    dve.wait_ge(s.xh, t + 1)
                    dve.tensor_tensor(xTs[b][1], ps[:, 6, 0:D], xTs[b][0].bitcast(F32), ALU.subtract).then_inc(s.xt, 1)

                def gate(t, b, half):
                    dve.wait_ge(s.sg, 2 * t + half + 1)
                    cols = slice(half * IH, (half + 1) * IH)
                    dve.scalar_tensor_tensor(out=Hdt[b][:, cols], in0=Sgt[:, cols], scalar=xt[b][:, D:XW],
                                             in1=ps[:, 2 + half, 0:IH], op0=ALU.mult, op1=ALU.mult).then_inc(s.hd, 1)

                def tile_out(t, b):
                    dve.wait_ge(s.y_mm, t + 1)
                    dve.wait_ge(s.stored, t + 1)
                    dve.tensor_copy(yt[b][:], ps[:, 7, 0:D]).then_inc(s.y, 1)

                norms_idle(dve)
                w = weights_of(dve, 0)
                lower_weights(0, w, 0)
                lower_weights(0, w, 1)
                tile_in(0, 0)
                w = weights_of(dve, 1)
                gate(0, 0, 0)
                lower_weights(1, w, 0)
                gate(0, 0, 1)
                tile_in(1, 1)
                lower_weights(1, w, 1)

                def step(t, b, last):
                    if not last:
                        w = weights_of(dve, t + 1)
                    gate(t, b, 0)
                    if not last:
                        lower_weights(t + 1, w, 0)
                    gate(t, b, 1)
                    if not last:
                        tile_in(t + 1, 1 - b)
                    tile_out(t - 1, 1 - b)
                    if not last:
                        lower_weights(t + 1, w, 1)
                over_tiles(dve, step)
                tile_out(TILES - 1, 0)

            def lower_patches(g, b):
                dve.wait_ge(patch_hi, g + 1)
                dve.tensor_tensor(x_p[b][1], x_in[:, b], x_p[b][0].bitcast(F32), ALU.subtract).then_inc(patch_lo, 1)

            dve.wait_ge(first_hi, 1)
            dve.tensor_tensor(add_p[1], emb_a, add_p[0].bitcast(F32), ALU.subtract).then_inc(first_lo, 1)
            for half, chunks in enumerate(PK_HALVES):
                dve.wait_ge(first_hi, 2 * half + 3)
                dve.tensor_tensor(emb_p[1][:, chunks], emb_w[:, chunks], emb_p[0][:, chunks].bitcast(F32),
                                  ALU.subtract).then_inc(first_lo, 1)
                dve.wait_ge(first_hi, 2 * half + 4)
                dve.tensor_tensor(x_p[0][1][:, chunks], x_in[:, 0, chunks], x_p[0][0][:, chunks].bitcast(F32),
                                  ALU.subtract).then_inc(first_lo, 1)
            dve.wait_ge(first_lo, 5)
            dve.sem_inc(patch_lo, 1)
            lower_patches(1, 1)
            with dve.Fori(0, GROUPS // 2 - 1) as i:
                for b in range(2):
                    lower_patches(2 * i + b + 2, b)
            dve.wait_ge(s_tab, 4)
            attention(0)
            dve.wait_ge(s_rw, 32)
            dve.tensor_copy(place[:], region0)
            dve.wait_ge(A[0].res, FREE + 2 * GROUPS)
            ffn(0)
            routed()
            dve.wait_ge(F[0].y, FREE + 2 * GROUPS)
            attention(1)
            dve.wait_ge(A[1].res, FREE + 2 * GROUPS)
            ffn(1)

        @block.tensor
        def _(pe):
            def mm(out_, lhsT, rhs, start=True, stop=True):
                return pe.matmul(out_, lhsT, rhs, start=start, stop=stop)

            def mm3(out_, w, x, start=True, stop=True):
                pe.matmul(out_, w[1], x[0], start=start, stop=False)
                pe.matmul(out_, w[0], x[1], start=False, stop=False)
                return pe.matmul(out_, w[0], x[0], start=False, stop=stop)

            def part(pair, *at):
                return [t[at] for t in pair]

            pe.sem_inc(emb_mm, FREE)
            def add_rows(m, bk):
                for k in (1, 0):
                    pe.matmul(ps[:, bk, 0:N], add_p[k][:, m * P:(m + 1) * P], one_r, start=k == 1, stop=False)

            def embed(g, b):
                pe.wait_ge(patch_lo, g + 1)
                pe.wait_ge(emb_cp, g + 1)
                for m in range(DK):
                    add_rows(m, 2 * b + m)
                    for k in range(PK):
                        ins = mm3(ps[:, 2 * b + m, 0:N], part(emb_p, ALL, k, slice(m * P, (m + 1) * P)),
                                  part(x_p[b], ALL, k), False, k == PK - 1)
                ins.then_inc(emb_mm, 1)

            pe.wait_ge(first_hi, 2)
            pe.wait_ge(first_lo, 1)
            for m in range(DK):
                add_rows(m, m)
            for half, chunks in enumerate(PK_HALVES):
                pe.wait_ge(first_lo, 2 * half + 3)
                for m in range(DK):
                    for k in range(chunks.start, chunks.stop):
                        ins = mm3(ps[:, m, 0:N], part(emb_p, ALL, k, slice(m * P, (m + 1) * P)), part(x_p[0], ALL, k),
                                  False, k == PK - 1)
            ins.then_inc(emb_mm, 1)
            embed(1, 1)
            with pe.Fori(1, GROUPS // 2 - 1) as i:
                for b in range(2):
                    embed(2 * i + b, b)

            def mean(s, g, bk):
                o = ps[:, bk, 0:N]
                for c in range(DK):
                    ins = mm(o, mean_w, h[:, c, group(g)], c == 0, c == DK - 1)
                ins.then_inc(s.mean_mm, 1)

            def variance(s, g, bk):
                pe.wait_ge(s.squ, FREE + g + 1)
                o = ps[:, bk, 0:N]
                for c in range(DK):
                    ins = mm(o, mean_w, squ[:, c], c == 0, c == DK - 1)
                ins.then_inc(s.var_mm, 1)

            def attention(l):
                a = A[l]
                for buf_free in (a.S_mm, a.PT_mm, a.O_mm, a.OT_mm):
                    pe.sem_inc(buf_free, FREE)

                def read_out(name, g, X):
                    kind, k, later = Turn.parts(name)
                    n = 4 * g + k + 4 * later
                    if kind == "V":
                        pe.wait_ge(a.Vb, FREE + n + 1)
                    elif kind == "O":
                        pe.wait_ge(a.On, FREE + n + 1)
                    elif kind == "OT":
                        pe.wait_ge(a.OTs, FREE + n + 1)
                    elif kind == "comb":
                        pe.wait_ge(C.h, 2 * (g + 1) + k + 1)
                    elif kind == "mean":
                        s, of = next_norm(l, g, X)
                        pe.wait_ge(s.cen, FREE + of + 1)
                    elif kind == "var":
                        s, of = next_norm(l, g, X)
                        pe.wait_ge(s.lnv, FREE + of + 1)
                    elif kind == "proj":
                        pe.wait_ge(a.proj, FREE + 6 * (g + 1) + k + 1)
                    elif kind == "out":
                        pe.wait_ge(a.res, FREE + 2 * (g + later) + k + 1)

                def project(g, b, k, bk):
                    pe.wait_ge(a.xl, g + 1)
                    for c in range(DK):
                        ins = mm3(ps[:, bk, 0:N], part(qkv_p, ALL, c, slice(k * P, (k + 1) * P)), part(xa, ALL, c),
                                  c == 0, c == DK - 1)
                    ins.then_inc(a.proj_mm, 1)

                def scores(n, p, b):
                    pe.wait_ge(a.km, FREE + n + 1)
                    pe.wait_ge(a.sb, n + 1)
                    for c in range(DK):
                        for i in range(2):
                            o = ps[i * PITCH:(i + 1) * PITCH, 2 * (p % 2) + c, :].rearrange("p (h k) -> p h k", k=PITCH)
                            q0 = (2 * p + i) * T
                            ins = mm(o[:, :, 0:T], QT[:, c, q0:q0 + PITCH], Km[p % 2][:, c, :, i * T:(i + 1) * T])
                    ins.then_inc(a.S_mm, 1)

                def values(n, p, b, bk):
                    for i in range(2):
                        for c in range(DK):
                            src = VT[:, c, 2 * p + i].rearrange("p a k -> p (a k)")
                            ins = pe.transpose(ps[:, bk, i * D + c * P:i * D + (c + 1) * P], src, ident)
                    ins.then_inc(a.V_mm, 1)

                def probs_t(n, p):
                    pe.wait_ge(a.ex, FREE + n + 1)
                    pe.wait_ge(a.PTs, FREE + n)
                    for hp in range(HP):
                        ins = pe.transpose(ps[:, 4 + hp // 4, (hp % 4) * P:(hp % 4 + 1) * P],
                                           Pr[p % 2][:, 2 * hp:2 * hp + 2, :].rearrange("p a k -> p (a k)"), ident)
                    ins.then_inc(a.PT_mm, 1)

                def outputs(n, p, bk):
                    pe.wait_ge(a.PTs, FREE + n + 1)
                    pe.wait_ge(a.Vb, FREE + n + 1)
                    for i in range(2):
                        for hp in range(HP):
                            ins = mm(ps[i * PITCH:i * PITCH + T, bk, hp * 2 * HD:(hp + 1) * 2 * HD],
                                     PTs[p % 2][:, hp, i], Vb[p % 2][:, i, hp])
                    ins.then_inc(a.O_mm, 1)

                def outputs_t(n, p, bk):
                    pe.wait_ge(a.On, FREE + n + 1)
                    for c in range(DK):
                        ins = pe.transpose(ps[:, bk, c * P:(c + 1) * P], On[p % 2][:, c * P:(c + 1) * P], ident)
                    ins.then_inc(a.OT_mm, 1)

                def out_proj(g, m, bk):
                    pe.wait_ge(a.OTs, FREE + 4 * g + 4)
                    for c in range(DK):
                        ins = mm3(ps[:, bk, 0:N], part(out_p, ALL, c, slice(m * P, (m + 1) * P)), part(OTs, ALL, c),
                                  c == 0, c == DK - 1)
                    ins.then_inc(a.out_mm, 1)

                def routed_out(g, b, turn, c, bk):
                    pe.wait_ge(s_gat[b], 128 * turn + 128)
                    for p in range(PAIRS):
                        for k in range(2):
                            ins = mm(ps[:, bk, p * W2:(p + 1) * W2], yg[b][:, p, k, c * P:(c + 1) * P],
                                     ident[0:W2, 0:W2], k == 0, k == 1)
                    ins.then_inc((C.mm0, C.mm1)[c], 1)

                if l == 1:
                    pe.sem_inc(C.mm0, FREE)
                    pe.sem_inc(C.mm1, FREE)
                    for c in range(DK):
                        routed_out(0, 0, 0, c, 6 + c)
                    pe.wait_ge(C.h, 2)
                mean(a, 0, 6)
                if l == 0:
                    embed(GROUPS - 2, 0)
                variance(a, 0, 7)
                if l == 0:
                    embed(GROUPS - 1, 1)
                pe.wait_ge(s_lower, 2 * l + 2)
                for k in range(6):
                    if k == 0:
                        pe.wait_ge(a.cen, FREE + 1)
                    elif k == 1:
                        pe.wait_ge(a.lnv, FREE + 1)
                    else:
                        pe.wait_ge(a.proj, FREE + k - 1)
                    project(0, 0, k, 6 + k % 2)
                if l == 0:
                    pe.wait_ge(emb_cp, FREE + GROUPS)
                scores(0, 0, 0)
                pe.wait_ge(a.proj, FREE + 6)
                values(0, 0, 0, 7)

                def step(g, b, X, turn):
                    n = 4 * g

                    def at(name, do, *args):
                        prev, back = X.before(name)
                        if prev is not None:
                            read_out(prev, g - back, X)
                        do(*args, X.bank(name))

                    def routed_out_next(c, bk):
                        routed_out(g + 1, 1 - b, turn, c, bk)

                    scores(n + 1, 1, b)
                    if l == 1 and not X.last:
                        for c in range(DK):
                            at(f"comb{c}", routed_out_next, c)
                    if not X.first:
                        at("O3p", outputs, n - 1, 3)
                    at("V1", values, n + 1, 1, b)
                    probs_t(n, 0)
                    if l == 1 and not X.last:
                        pe.wait_ge(C.h, 2 * g + 4)
                    at("mean", mean, *next_norm(l, g, X))
                    if not X.first:
                        at("OT3p", outputs_t, n - 1, 3)
                    scores(n + 2, 2, b)
                    at("O0", outputs, n, 0)
                    at("V2", values, n + 2, 2, b)
                    probs_t(n + 1, 1)
                    at("var", variance, *next_norm(l, g, X))
                    if not X.first:
                        at("out0p", out_proj, g - 1, 0)
                        at("out1p", out_proj, g - 1, 1)
                    at("OT0", outputs_t, n, 0)
                    scores(n + 3, 3, b)
                    at("O1", outputs, n + 1, 1)
                    at("V3", values, n + 3, 3, b)
                    probs_t(n + 2, 2)
                    at("OT1", outputs_t, n + 1, 1)
                    if not X.last:
                        for k in range(4):
                            at(f"proj{k}", project, g + 1, 1 - b, k)
                    at("O2", outputs, n + 2, 2)
                    probs_t(n + 3, 3)
                    if not X.last:
                        for k in (4, 5):
                            at(f"proj{k}", project, g + 1, 1 - b, k)
                    at("OT2", outputs_t, n + 2, 2)
                    if not X.last:
                        scores(n + 4, 0, 1 - b)
                        pe.wait_ge(a.proj, FREE + 6 * g + 12)
                        at("V0n", values, n + 4, 0, 1 - b)
                    else:
                        at("O3", outputs, n + 3, 3)
                        at("OT3", outputs_t, n + 3, 3)
                        at("out0", out_proj, g, 0)
                        at("out1", out_proj, g, 1)
                over_body(pe, l, step)

            def gate_up(s, g, j, rows, product, w, x):
                nj = len(rows)
                pe.wait_ge(s.hd, nj * g + j + 1)
                for half in range(2 if rows[j] == P else 1):
                    c0 = (2 * j + half) * P
                    for c in range(DK):
                        ins = product(ps[:, 2 * (j % 2) + half, 0:N], w(c, slice(c0, c0 + P)), x(c), c == 0, c == DK - 1)
                ins.then_inc(s.gu_mm, 1)

            def down(s, g, j, rows, product, w, hidden):
                nj, r = len(rows), rows[j]
                pe.wait_ge(s.hl if product is mm3 else s.hd, FREE + nj * g + j + 1)
                if j == 0:
                    pe.wait_ge(s.y, FREE + 2 * g)
                for m in range(DK):
                    ins = product(ps[:, 4 + m, 0:N], w(slice(0, r), j, slice(m * P, (m + 1) * P)), hidden(j % (LAG + 1), slice(0, r)),
                                  start=(j == 0), stop=(j == nj - 1))
                ins.then_inc(s.dn_mm, 1)

            def ffn(l):
                s = F[l]
                rows = hidden_chunks((I0, I1)[l])
                if l == 0:
                    product = mm
                    w_gu, w_dn = (lambda c, cols: gu0_w[:, c, cols]), (lambda r, j, cols: dn0_w[r, j, cols])
                    x_of, hidden = (lambda b, c: xn[b][:, c]), (lambda b, r: Hd[b][r])
                else:
                    product = mm3
                    w_gu, w_dn = (lambda c, cols: part(gu1_p, ALL, c, cols)), (lambda r, j, cols: part(dn1_p, r, j, cols))
                    x_of, hidden = (lambda b, c: part(xf1[b], ALL, c)), (lambda b, r: part(Hf1[b], r))
                pe.sem_inc(s.dn_mm, LAG + 1)

                def logits(g, b):
                    if l == 0:
                        pe.wait_ge(s.xn, FREE + g + 1)
                        pe.wait_ge(s.cen, FREE + g + 1)
                        for p in range(PAIRS):
                            for c in range(DK):
                                ins = mm(ps[0:W2, 6, p * EXPERTS:(p + 1) * EXPERTS], xn[b][:, c, p * W2:(p + 1) * W2],
                                         r_w[:, c], c == 0, c == DK - 1)
                        ins.then_inc(s.lg_mm, 1)

                def token_rows(g, b, half):
                    if l == 0:
                        for a in range(2):
                            for c in range(DK):
                                p = 2 * half + a
                                ins = pe.transpose(ps[0:W2, 7, a * D + c * P:a * D + (c + 1) * P],
                                                   xn[b][:, c, p * W2:(p + 1) * W2], ident)
                        ins.then_inc((s.rowA_mm, s.rowB_mm)[half], 1)

                def counts(g):
                    if l == 0:
                        pe.wait_ge(s.r, RCHAIN * g + 13)
                        n = PAIRS * EXPERTS
                        chosen = rt[0:W2, 10, 0:n]
                        mm(ps[0:W2, 6, 0:n], before, chosen, True, False)
                        for k in range(1, PAIRS):
                            mm(ps[0:W2, 6, k * EXPERTS:n], ones[0:W2, 0:W2], chosen[:, 0:n - k * EXPERTS],
                               False, k == PAIRS - 1)
                        for p in range(PAIRS):
                            ins = pe.matmul(ps[:, 6, 32:32 + EXPERTS], ones[0:W2], chosen[:, p * EXPERTS:(p + 1) * EXPERTS],
                                            start=False, stop=p == PAIRS - 1, skip_group_check=True)
                        ins.then_inc(s.cnt_mm, 1)

                def step(g, b, first, last):
                    x = lambda c: x_of(b, c)
                    if l == 0:
                        pe.wait_ge(s.xn, FREE + g + 1)
                    else:
                        pe.wait_ge(s.xl, g + 1)
                    nj = len(rows)
                    for j in range(nj):
                        gate_up(s, g, j, rows, product, w_gu, x)
                        if first and j == 0:
                            pe.wait_ge(A[l].res, FREE + 2 * GROUPS)
                            logits(0, 0)
                            token_rows(0, 0, 0)
                        if j == 1 and l == 0:
                            pe.wait_ge(s.lg, FREE + g + 1)
                            counts(g)
                            pe.wait_ge(s.rowA, FREE + g + 1)
                            token_rows(g, b, 1)
                        if j == MEAN_AT[l] and not last:
                            if l == 0:
                                pe.wait_ge(s.r, RCHAIN * (g + 1))
                            mean(s, g + 1, 6)
                        if j == VARIANCE_AT[l] and not last:
                            if l == 0:
                                pe.wait_ge(s.rowB, FREE + g + 1)
                            variance(s, g + 1, 7)
                        if j >= LAG:
                            down(s, g, j - LAG, rows, product, w_dn, hidden)
                        elif not first:
                            down(s, g - 1, nj + j - LAG, rows, product, w_dn, hidden)
                        if j == nj - 1 and not last:
                            logits(g + 1, 1 - b)
                            if l == 0:
                                pe.wait_ge(s.lnv, FREE + g + 2)
                            token_rows(g + 1, 1 - b, 0)
                over_groups(pe, step)
                for j in range(len(rows) - LAG, len(rows)):
                    down(s, GROUPS - 1, j, rows, product, w_dn, hidden)

            def routed():
                s = E

                def tile_in(t, b, turn):
                    pe.wait_ge(s_xt[b], 16 * turn + 16)
                    pe.wait_ge(s.xt, FREE + t)
                    for c in range(DK):
                        ins = pe.transpose(ps[:, 6, c * P:(c + 1) * P], xt[b][:, c * P:(c + 1) * P], ident)
                    ins.then_inc(s.xt_mm, 1)

                def gate_up_half(t, b, half):
                    pe.wait_ge(s.xt, FREE + t + 1)
                    pe.wait_ge(s.wl, 2 * t + half + 1)
                    pe.wait_ge(s.hd, FREE + 2 * t + half - 1)
                    for u in range(2):
                        for c in range(DK):
                            ins = mm3(ps[:, 2 * u + half, 0:IH], part(xTs[b], ALL, slice(c * P, (c + 1) * P)),
                                      part(tile_w[half], ALL, 2 * c + u), c == 0, c == DK - 1)
                    ins.then_inc(s.gu_mm, 1)

                def hidden_t(t, b):
                    pe.wait_ge(s.hd, FREE + 2 * t + 2)
                    pe.wait_ge(s.ht, FREE + t)
                    for j, r in enumerate(hidden_chunks(I0)):
                        ins = pe.transpose(ps[0:r, 4 + j // 4, (j % 4) * P:(j % 4 + 1) * P],
                                           Hdt[b][:, j * P:j * P + r], ident)
                    ins.then_inc(s.ht_mm, 1)

                def tile_out(t, w):
                    pe.wait_ge(s.ht, FREE + t + 1)
                    pe.wait_ge(s.y, FREE + t)
                    for j, r in enumerate(hidden_chunks(I0)):
                        ins = mm(ps[:, 7, 0:D], HTs[0:r, j], arena[0:r, bass.ds(w + DK * 2 * I0 + j * D, D)],
                                 j == 0, j == 5)
                    ins.then_inc(s.y_mm, 1)

                def step(t, b, turn_next, last):
                    w_before = weights_of(pe, t - 1)
                    gate_up_half(t, b, 0)
                    hidden_t(t - 1, 1 - b)
                    gate_up_half(t, b, 1)
                    if not last:
                        tile_in(t + 1, 1 - b, turn_next)
                    tile_out(t - 1, w_before)

                tile_in(0, 0, 0)
                gate_up_half(0, 0, 0)
                gate_up_half(0, 0, 1)
                tile_in(1, 1, 0)
                with pe.Fori(0, (TILES - 3) // 2) as i:
                    step(2 * i + 1, 1, i + 1, False)
                    step(2 * i + 2, 0, i + 1, False)
                step(TILES - 2, 1, (TILES - 1) // 2, False)
                step(TILES - 1, 0, None, True)
                hidden_t(TILES - 1, 0)
                tile_out(TILES - 1, weights_of(pe, TILES - 1))

            pe.wait_ge(s_cst, 16)
            pe.wait_ge(s_attw, 16 * 5)
            pe.wait_ge(s_zero, 13)
            attention(0)
            pe.wait_ge(s_shw, 32)
            pe.wait_ge(s_rw, 32)
            ffn(0)
            pe.wait_ge(F[0].y, FREE + 2 * GROUPS)
            pe.wait_ge(F[0].rowB, FREE + GROUPS)
            pe.wait_ge(s_table, 1)
            pe.wait_ge(s_exw, 16 * EXPERTS)
            routed()
            pe.wait_ge(E.y, FREE + TILES)
            attention(1)
            pe.wait_ge(s_lower, 6)
            ffn(1)


ROUTE = 18
RCHAIN = ROUTE + 8
TABLE_PIECES = 4


class Packed:

    def __init__(self, **widths):
        self.at, self.width = {}, 0
        for name, w in widths.items():
            self.at[name] = (self.width, w)
            self.width += w

    def of(self, tensor, name):
        a, w = self.at[name]
        return tensor[:, a:a + w]


CONST = Packed(ident=P, mean=P, ones=P, before=W2, headmask=HG, prio=PAIRS * EXPERTS, region0=EXPERTS,
               k128=KT_MAX, tri=EXPERTS * EXPERTS, tile_no=TILES, tile_row=TILES)


class Turn:

    def __init__(self, order, last_two):
        self.order = order.split()
        self.last_two = last_two
        self.first, self.last = last_two[0] is None, "out0" in self.order

    @staticmethod
    def parts(name):
        later = {"p": -1, "n": 1}.get(name[-1], 0) if name[-2].isdigit() else 0
        stem = name[:-1] if later else name
        kind = stem.rstrip("0123456789")
        return kind, int(stem[len(kind):] or 0), later

    def bank(self, name):
        return 6 + self.order.index(name) % 2

    def before(self, name):
        i = self.order.index(name)
        return (self.order[i - 2], 0) if i >= 2 else (self.last_two[i], 1)


_FIRST = "V1 mean O0 V2 var OT0 O1 V3 OT1 proj0 proj1 proj2 proj3 O2 proj4 proj5 OT2 V0n"
_BODY = "O3p V1 mean OT3p O0 V2 var out0p out1p OT0 O1 V3 OT1 proj0 proj1 proj2 proj3 O2 proj4 proj5 OT2 V0n"
_LAST = "O3p V1 mean OT3p O0 V2 var out0p out1p OT0 O1 V3 OT1 O2 OT2 O3 OT3 out0 out1"
ORDERS = [(Turn(merge + _FIRST, (None, "V0n")), Turn(merge + _BODY, ("OT2", "V0n")), Turn(_LAST, ("OT2", "V0n")))
          for merge in ("", "comb0 comb1 ")]

_INS = "xT onehot embW embAdd consts qkv0 qkvb0 wo0 wob0 bias0 qkv1 wo1 wob1 gu0 dn0 ew rT rb gu1 dn1".split()


def kernel(**inputs):
    import numpy as np
    import concourse.bacc as bacc
    from concourse.bass_utils import run_bass_kernel_spmd

    v = {k: np.asarray(a) for k, a in inputs.items()}

    def rows(w):
        return w.reshape(-1, P, w.shape[1]).transpose(1, 0, 2)

    def cols(b):
        return b.reshape(-1, P).T

    side = SIDE // PATCH
    px = v["x"].reshape(IMAGES, CHANNELS, side, PATCH, side, PATCH).transpose(0, 2, 4, 1, 3, 5)
    px = px.reshape(IMAGES, T - 1, PK * P)
    px = np.concatenate([np.zeros((IMAGES, 1, PK * P), px.dtype), px], axis=1)
    onehot = np.zeros((ADDED, N), np.float32)
    at = np.arange(N)
    onehot[at % T, at] = 1.0
    onehot[T, at[at % T == 0]] = 1.0
    onehot[T + 1, at[at % T != 0]] = 1.0

    consts = np.zeros((P, CONST.width), np.float32)
    CONST.of(consts, "ident")[:] = np.eye(P)
    CONST.of(consts, "mean")[:] = 1.0 / D
    CONST.of(consts, "ones")[:] = 1.0
    CONST.of(consts, "before")[0:W2] = np.triu(np.ones((W2, W2)), 1)
    CONST.of(consts, "headmask")[np.arange(P), np.arange(P) // HD] = 1.0
    CONST.of(consts, "prio")[:] = np.tile(EXPERTS - np.arange(EXPERTS), PAIRS)
    CONST.of(consts, "region0")[:] = REGION * np.arange(EXPERTS)
    CONST.of(consts, "k128")[:] = P * np.arange(KT_MAX)
    CONST.of(consts, "tri")[:] = np.tril(np.ones((EXPERTS, EXPERTS))).reshape(-1)
    CONST.of(consts, "tile_no")[:] = np.arange(TILES)
    CONST.of(consts, "tile_row")[:] = P * np.arange(TILES)

    def gate_up(g, u):
        parts = [w[a:a + P] for a in range(0, g.shape[0], P) for w in (g, u)]
        return rows(np.concatenate(parts, axis=0).T)

    def down(d):
        w = d.T
        pad = -w.shape[0] % P
        return rows(np.concatenate([w, np.zeros((pad, D), w.dtype)], axis=0))

    relT = v["L0_attn_rel_emb"].T
    mid = (v["L0_attn_rel_emb"].shape[0] - 1) // 2

    def expert(g, u, d):
        gu = rows(np.concatenate([g.T, u.T], axis=1)).reshape(P, -1)
        return np.concatenate([gu, down(d).reshape(P, -1)], axis=1)

    arrays = {
        "xT": px.reshape(GROUPS, N, PK, P).transpose(0, 3, 2, 1),
        "onehot": onehot,
        "embW": rows(v["L0_tok_W"].T),
        "embAdd": np.concatenate([v["L0_tok_pos_enc"][0], v["L0_tok_cls_token"][0], v["L0_tok_b"][None]], axis=0),
        "consts": consts,
        "qkv0": rows(v["L0_attn_Wqkv"]),
        "qkvb0": cols(v["L0_attn_bqkv"]),
        "wo0": rows(v["L0_attn_Wout"]),
        "wob0": cols(v["L0_attn_bout"]),
        "bias0": np.stack([relT[:, mid - q:mid - q + T] for q in range(T)]),
        "qkv1": rows(np.concatenate([v["L1_attn_Wq"].T, v["L1_attn_Wk"].T, v["L1_attn_Wv"].T], axis=1)),
        "wo1": rows(v["L1_attn_Wo"].T),
        "wob1": cols(v["L1_attn_bo"]),
        "gu0": gate_up(v["L0_ffn_sg"], v["L0_ffn_su"]),
        "dn0": down(v["L0_ffn_sd"]),
        "ew": np.stack([expert(v["L0_ffn_rg"][e], v["L0_ffn_ru"][e], v["L0_ffn_rd"][e]) for e in range(EXPERTS)]),
        "rT": rows(v["L0_ffn_wr"].T),
        "rb": np.broadcast_to(v["L0_ffn_rb"], (P, PAIRS, EXPERTS)).reshape(P, PAIRS * EXPERTS),
        "gu1": gate_up(v["L1_ffn_w_gate"], v["L1_ffn_w_up"]),
        "dn1": down(v["L1_ffn_w_down"]),
    }
    nc = bacc.Bacc("TRN2", target_bir_lowering=False, num_devices=1)
    arrays = {f"in_{k}_dram": np.ascontiguousarray(arrays[k]) for k in _INS}
    args = [nc.dram_tensor(k, a.shape, mybir.dt.from_np(a.dtype), kind="ExternalInput").ap() for k, a in arrays.items()]
    out = nc.dram_tensor("out_0_dram", (P, DK, TOKENS), F32, kind="ExternalOutput").ap()
    xs = nc.dram_tensor("routed_in", (ROWS, XW), F32, kind="Internal").ap()
    ys = nc.dram_tensor("routed_out", (TILES * P, D), F32, kind="Internal").ap()
    vit_kernel(nc, *args, xs, ys, out)
    r = run_bass_kernel_spmd(nc, [arrays], core_ids=[0])
    got = r.results[0]["out_0_dram"]
    return got.transpose(2, 1, 0).reshape(IMAGES, T, D)
```
